# Optimizing a Trainium2 kernel written in Bass

```python
import numpy as np
import jax
import jax.numpy as jnp

def _softmax(x, axis=-1):
    return jax.nn.softmax(x, axis=axis)

def _gelu(x):
    return jax.nn.gelu(x, approximate=True)

def _silu(x):
    return jax.nn.silu(x)

def _sigmoid(x):
    return jax.nn.sigmoid(x)

def _layernorm(x, axis=-1, eps=1e-05):
    m = jnp.mean(x, axis=axis, keepdims=True)
    v = jnp.var(x, axis=axis, keepdims=True)
    return (x - m) / jnp.sqrt(v + eps)

def _scatter_add(tgt, idx, src, axis=0):
    return tgt.at[idx].add(src)

def _segment_sum(src, seg, n):
    return jax.ops.segment_sum(src, seg, n)
kernel_name = 'mk_adj_ffn_d2_adj_r2_2e8bff'

def setup_inputs(seed: int=0):
    np.random.seed(seed)
    _w = jnp.asarray

    def _rec_inputs():
        import jax
        import jax.numpy as jnp
        _gk = jax.random.key(seed)
        x = 7.22e-05 + 1 * jax.random.normal(jax.random.fold_in(_gk, 1), (2048, 512), jnp.float32)
        _a = jax.random.bernoulli(jax.random.fold_in(_gk, 2), 0.00390625, (2048, 2048))
        _a = jnp.logical_or(_a, jnp.swapaxes(_a, -1, -2))
        _a = jnp.logical_or(_a, jnp.eye(2048, dtype=bool))
        _af = _a.astype(jnp.float32)
        _d = jnp.maximum(_af.sum(-1), 1.0) ** (-0.5)
        _af = _af * _d[..., :, None] * _d[..., None, :]
        adj = _af
        return (x, adj)
    x, adj = _rec_inputs()

    def _L0_gnn_setup():
        import jax, jax.numpy as jnp
        import numpy as np
        N = 4096
        D = 512

        def adjacent_mat(adj):
            adj = adj + jnp.eye(adj.shape[0], dtype=adj.dtype)
            deg = jnp.sum(adj, axis=1)
            dinv = jnp.where(deg > 0, deg ** (-0.5), 0.0).astype(adj.dtype)
            return dinv[:, None] * adj * dinv[None, :]
        key = jax.random.key(seed)
        k1, k2 = jax.random.split(key)
        x = jax.random.normal(k1, (N, D), dtype=jnp.float32)
        Coefficient2 = 1e-08 * jnp.ones((N, N), dtype=jnp.float32)
        A = jax.random.uniform(k2, (N, N), dtype=jnp.float32)
        return {'x': x, 'Coefficient2': Coefficient2, 'A': A}
    _L0_gnn_all = _L0_gnn_setup()
    _L0_gnn_in = {k: v for k, v in _L0_gnn_all.items() if k in ()}
    del _L0_gnn_all

    def _L0_ffn_setup():
        import jax, jax.numpy as jnp
        import numpy as np
        D_MODEL = 512
        D_FF = 2048
        N_EXPERTS = 8
        TOP_K = 2
        D_FF_PER = D_FF // N_EXPERTS
        B, T = (4, 1024)
        key = jax.random.key(seed)
        ks = jax.random.split(key, 7)
        b1_bound = 1.0 / np.sqrt(D_MODEL)
        b2_bound = 1.0 / np.sqrt(D_FF_PER)
        return {'x': jax.random.normal(ks[0], (B, T, D_MODEL), dtype=jnp.float32), 'router_w': jax.random.uniform(ks[1], (D_MODEL, N_EXPERTS), minval=-b1_bound, maxval=b1_bound, dtype=jnp.float32), 'router_b': jax.random.uniform(ks[2], (N_EXPERTS,), minval=-b1_bound, maxval=b1_bound, dtype=jnp.float32), 'W1': jax.random.uniform(ks[3], (N_EXPERTS, D_MODEL, D_FF_PER), minval=-b1_bound, maxval=b1_bound, dtype=jnp.float32), 'b1': jax.random.uniform(ks[4], (N_EXPERTS, D_FF_PER), minval=-b1_bound, maxval=b1_bound, dtype=jnp.float32), 'W2': jax.random.uniform(ks[5], (N_EXPERTS, D_FF_PER, D_MODEL), minval=-b2_bound, maxval=b2_bound, dtype=jnp.float32), 'b2': jax.random.uniform(ks[6], (N_EXPERTS, D_MODEL), minval=-b2_bound, maxval=b2_bound, dtype=jnp.float32)}
    _L0_ffn_all = _L0_ffn_setup()
    _L0_ffn_in = {k: v for k, v in _L0_ffn_all.items() if k in ('router_w', 'router_b', 'W1', 'b1', 'W2', 'b2')}
    del _L0_ffn_all

    def _L1_gnn_setup():
        import jax, jax.numpy as jnp
        import numpy as np
        ALPHA = 0.2
        NEG = -9000000000000000.0
        N, NFEAT, NHID, NHEADS = (2048, 512, 64, 8)
        EMB = NHID * NHEADS
        key = jax.random.key(seed)
        ks = jax.random.split(key, 16)
        x = jax.random.normal(ks[0], (N, NFEAT), dtype=jnp.float32)
        adj = (jax.random.uniform(ks[1], (N, N)) < 0.01).astype(jnp.float32)
        adj = jnp.maximum(adj, jnp.eye(N, dtype=jnp.float32))
        s = 0.05
        W = jax.random.normal(ks[2], (NHEADS, NFEAT, NHID), dtype=jnp.float32) * s
        a1 = jax.random.normal(ks[3], (NHEADS, NHID), dtype=jnp.float32) * s
        a2 = jax.random.normal(ks[4], (NHEADS, NHID), dtype=jnp.float32) * s
        W1 = jax.random.normal(ks[5], (EMB // 2, EMB), dtype=jnp.float32) * s
        b1 = jnp.zeros((EMB // 2,), dtype=jnp.float32)
        W2 = jax.random.normal(ks[6], (NFEAT // 4, EMB // 2), dtype=jnp.float32) * s
        b2 = jnp.zeros((NFEAT // 4,), dtype=jnp.float32)
        W3 = jax.random.normal(ks[7], (NFEAT // 2, NFEAT // 4), dtype=jnp.float32) * s
        b3 = jnp.zeros((NFEAT // 2,), dtype=jnp.float32)
        W4 = jax.random.normal(ks[8], (NFEAT, NFEAT // 2), dtype=jnp.float32) * s
        b4 = jnp.zeros((NFEAT,), dtype=jnp.float32)
        return {'x': x, 'adj': adj, 'W': W, 'a1': a1, 'a2': a2, 'W1': W1, 'b1': b1, 'W2': W2, 'b2': b2, 'W3': W3, 'b3': b3, 'W4': W4, 'b4': b4}
    _L1_gnn_all = _L1_gnn_setup()
    _L1_gnn_in = {k: v for k, v in _L1_gnn_all.items() if k in ('W', 'a1', 'a2', 'W1', 'b1', 'W2', 'b2', 'W3', 'b3', 'W4', 'b4')}
    del _L1_gnn_all

    def _L1_ffn_setup():
        import jax, jax.numpy as jnp
        import numpy as np
        DIM = 512
        INTER = 512
        E = 32
        K = 4
        G = 8
        LG = 4
        ROUTE_SCALE = 1.0
        CAP_FACTOR = 1.25
        B, S = (4, 1024)

        def _gate(xf, wg):
            logits = xf @ wg.T
            scores = jax.nn.softmax(logits, axis=-1)
            sg = scores.reshape(-1, G, E // G)
            group_scores = sg.max(axis=-1)
            _, gtop = jax.lax.top_k(group_scores, LG)
            keep_g = jnp.sum(jax.nn.one_hot(gtop, G, dtype=jnp.float32), axis=1) > 0
            masked = jnp.where(keep_g[:, :, None], sg, -jnp.inf).reshape(-1, E)
            _, idx = jax.lax.top_k(masked, K)
            w = jnp.take_along_axis(scores, idx, axis=1)
            w = w / (w.sum(-1, keepdims=True) + 1e-09) * ROUTE_SCALE
            return (w.astype(xf.dtype), idx)

        def _forward(x, wg, w1, w2, w3, sw1, sw2, sw3):
            shape = x.shape
            xf = x.reshape(-1, DIM)
            N = xf.shape[0]
            cap = max(1, int(CAP_FACTOR * N * K / E))
            w, idx = _gate(xf, wg)
            fe = idx.reshape(-1)
            oh = jax.nn.one_hot(fe, E, dtype=jnp.int32)
            pos = (jnp.cumsum(oh, axis=0) * oh).sum(-1) - 1
            keep = pos < cap
            dest = jnp.where(keep, fe * cap + pos, E * cap)
            tok = jnp.arange(N * K, dtype=jnp.int32) // K
            buf_tok = jnp.full((E * cap + 1,), N, jnp.int32).at[dest].set(tok)[:-1]
            buf_w = jnp.zeros((E * cap + 1,), x.dtype).at[dest].set(w.reshape(-1))[:-1]
            xp = jnp.concatenate([xf, jnp.zeros((1, DIM), x.dtype)], axis=0)
            xe = xp[buf_tok].reshape(E, cap, DIM)
            h = jax.nn.silu(jnp.einsum('ecd,edh->ech', xe, w1)) * jnp.einsum('ecd,edh->ech', xe, w3)
            out = jnp.einsum('ech,ehd->ecd', h, w2) * buf_w.reshape(E, cap, 1)
            y = jnp.zeros((N + 1, DIM), x.dtype).at[buf_tok].add(out.reshape(E * cap, DIM))[:N]
            z = jax.nn.silu(xf @ sw1) * (xf @ sw3) @ sw2
            return (y + z).reshape(shape)
        key = jax.random.key(seed)
        ks = jax.random.split(key, 9)
        sd = DIM ** (-0.5)
        si = INTER ** (-0.5)
        x = jax.random.normal(ks[0], (B, S, DIM), jnp.float32)
        wg = jax.random.normal(ks[1], (E, DIM), jnp.float32) * sd
        w1 = jax.random.normal(ks[2], (E, DIM, INTER), jnp.float32) * sd
        w3 = jax.random.normal(ks[3], (E, DIM, INTER), jnp.float32) * sd
        w2 = jax.random.normal(ks[4], (E, INTER, DIM), jnp.float32) * si
        sw1 = jax.random.normal(ks[5], (DIM, INTER), jnp.float32) * sd
        sw3 = jax.random.normal(ks[6], (DIM, INTER), jnp.float32) * sd
        sw2 = jax.random.normal(ks[7], (INTER, DIM), jnp.float32) * si
        return dict(x=x, wg=wg, w1=w1, w2=w2, w3=w3, sw1=sw1, sw2=sw2, sw3=sw3)
    _L1_ffn_all = _L1_ffn_setup()
    _L1_ffn_in = {k: v for k, v in _L1_ffn_all.items() if k in ('wg', 'w1', 'w2', 'w3', 'sw1', 'sw2', 'sw3')}
    del _L1_ffn_all
    return {'x': x, 'adj': adj, 'L0_ffn_router_w': _L0_ffn_in['router_w'], 'L0_ffn_router_b': _L0_ffn_in['router_b'], 'L0_ffn_W1': _L0_ffn_in['W1'], 'L0_ffn_b1': _L0_ffn_in['b1'], 'L0_ffn_W2': _L0_ffn_in['W2'], 'L0_ffn_b2': _L0_ffn_in['b2'], 'L1_gnn_W': _L1_gnn_in['W'], 'L1_gnn_a1': _L1_gnn_in['a1'], 'L1_gnn_a2': _L1_gnn_in['a2'], 'L1_gnn_W1': _L1_gnn_in['W1'], 'L1_gnn_b1': _L1_gnn_in['b1'], 'L1_gnn_W2': _L1_gnn_in['W2'], 'L1_gnn_b2': _L1_gnn_in['b2'], 'L1_gnn_W3': _L1_gnn_in['W3'], 'L1_gnn_b3': _L1_gnn_in['b3'], 'L1_gnn_W4': _L1_gnn_in['W4'], 'L1_gnn_b4': _L1_gnn_in['b4'], 'L1_ffn_wg': _L1_ffn_in['wg'], 'L1_ffn_w1': _L1_ffn_in['w1'], 'L1_ffn_w2': _L1_ffn_in['w2'], 'L1_ffn_w3': _L1_ffn_in['w3'], 'L1_ffn_sw1': _L1_ffn_in['sw1'], 'L1_ffn_sw2': _L1_ffn_in['sw2'], 'L1_ffn_sw3': _L1_ffn_in['sw3']}

def reference(x, adj, L0_ffn_router_w, L0_ffn_router_b, L0_ffn_W1, L0_ffn_b1, L0_ffn_W2, L0_ffn_b2, L1_gnn_W, L1_gnn_a1, L1_gnn_a2, L1_gnn_W1, L1_gnn_b1, L1_gnn_W2, L1_gnn_b2, L1_gnn_W3, L1_gnn_b3, L1_gnn_W4, L1_gnn_b4, L1_ffn_wg, L1_ffn_w1, L1_ffn_w2, L1_ffn_w3, L1_ffn_sw1, L1_ffn_sw2, L1_ffn_sw3):
    import jax
    import jax.numpy as jnp

    def _L0_gnn_ref(x, Coefficient2, A):
        import jax, jax.numpy as jnp
        import numpy as np
        N = 4096
        D = 512

        def adjacent_mat(adj):
            adj = adj + jnp.eye(adj.shape[0], dtype=adj.dtype)
            deg = jnp.sum(adj, axis=1)
            dinv = jnp.where(deg > 0, deg ** (-0.5), 0.0).astype(adj.dtype)
            return dinv[:, None] * adj * dinv[None, :]
        A_c = jax.lax.stop_gradient(A)
        adj = adjacent_mat((A_c + A_c.T) * 0.5)
        y = Coefficient2 @ adj
        y = y @ x
        return y

    def _L0_ffn_ref(x, router_w, router_b, W1, b1, W2, b2):
        import jax, jax.numpy as jnp
        import numpy as np
        D_MODEL = 512
        D_FF = 2048
        N_EXPERTS = 8
        TOP_K = 2
        D_FF_PER = D_FF // N_EXPERTS
        B, T = (4, 1024)
        router_logits = x @ router_w + router_b
        routing_weights = jax.nn.softmax(router_logits, axis=-1)
        top_k_weights, top_k_indices = jax.lax.top_k(routing_weights, TOP_K)
        top_k_weights = top_k_weights / jnp.sum(top_k_weights, axis=-1, keepdims=True)
        routing_mask = jnp.zeros_like(routing_weights)
        routing_mask = jnp.take_along_axis(routing_mask, top_k_indices, axis=-1)
        b_idx = jnp.arange(x.shape[0])[:, None, None]
        t_idx = jnp.arange(x.shape[1])[None, :, None]
        routing_mask = jnp.zeros_like(routing_weights).at[b_idx, t_idx, top_k_indices].set(top_k_weights)
        h1 = jnp.einsum('btd,nde->btne', x, W1) + b1
        h1 = jax.nn.gelu(h1, approximate=False)
        out_per_expert = jnp.einsum('btne,nef->btnf', h1, W2) + b2
        output = jnp.sum(out_per_expert * routing_mask[..., None], axis=-2)
        return output

    def _L1_gnn_ref(x, adj, W, a1, a2, W1, b1, W2, b2, W3, b3, W4, b4):
        import jax, jax.numpy as jnp
        import numpy as np
        ALPHA = 0.2
        NEG = -9000000000000000.0
        N, NFEAT, NHID, NHEADS = (2048, 512, 64, 8)
        EMB = NHID * NHEADS
        Wh = jnp.einsum('nf,hfd->hnd', x, W)
        e_src = jnp.einsum('hnd,hd->hn', Wh, a1)
        e_dst = jnp.einsum('hnd,hd->hn', Wh, a2)
        e = jax.nn.leaky_relu(e_src[:, :, None] + e_dst[:, None, :], ALPHA)
        e = jnp.where(adj[None] > 0, e, NEG)
        att = jax.nn.softmax(e, axis=-1)
        h = jnp.einsum('hnm,hmd->hnd', att, Wh)
        h = jax.nn.elu(h)
        enc = jnp.transpose(h, (1, 0, 2)).reshape(x.shape[0], -1)
        out = jax.nn.relu(enc @ W1.T + b1)
        out = jax.nn.relu(out @ W2.T + b2)
        out = jax.nn.relu(out @ W3.T + b3)
        out = out @ W4.T + b4
        return out

    def _L1_ffn_ref(x, wg, w1, w2, w3, sw1, sw2, sw3):
        import jax, jax.numpy as jnp
        import numpy as np
        DIM = 512
        INTER = 512
        E = 32
        K = 4
        G = 8
        LG = 4
        ROUTE_SCALE = 1.0
        CAP_FACTOR = 1.25
        B, S = (4, 1024)

        def _gate(xf, wg):
            logits = xf @ wg.T
            scores = jax.nn.softmax(logits, axis=-1)
            sg = scores.reshape(-1, G, E // G)
            group_scores = sg.max(axis=-1)
            _, gtop = jax.lax.top_k(group_scores, LG)
            keep_g = jnp.sum(jax.nn.one_hot(gtop, G, dtype=jnp.float32), axis=1) > 0
            masked = jnp.where(keep_g[:, :, None], sg, -jnp.inf).reshape(-1, E)
            _, idx = jax.lax.top_k(masked, K)
            w = jnp.take_along_axis(scores, idx, axis=1)
            w = w / (w.sum(-1, keepdims=True) + 1e-09) * ROUTE_SCALE
            return (w.astype(xf.dtype), idx)

        def _forward(x, wg, w1, w2, w3, sw1, sw2, sw3):
            shape = x.shape
            xf = x.reshape(-1, DIM)
            N = xf.shape[0]
            cap = max(1, int(CAP_FACTOR * N * K / E))
            w, idx = _gate(xf, wg)
            fe = idx.reshape(-1)
            oh = jax.nn.one_hot(fe, E, dtype=jnp.int32)
            pos = (jnp.cumsum(oh, axis=0) * oh).sum(-1) - 1
            keep = pos < cap
            dest = jnp.where(keep, fe * cap + pos, E * cap)
            tok = jnp.arange(N * K, dtype=jnp.int32) // K
            buf_tok = jnp.full((E * cap + 1,), N, jnp.int32).at[dest].set(tok)[:-1]
            buf_w = jnp.zeros((E * cap + 1,), x.dtype).at[dest].set(w.reshape(-1))[:-1]
            xp = jnp.concatenate([xf, jnp.zeros((1, DIM), x.dtype)], axis=0)
            xe = xp[buf_tok].reshape(E, cap, DIM)
            h = jax.nn.silu(jnp.einsum('ecd,edh->ech', xe, w1)) * jnp.einsum('ecd,edh->ech', xe, w3)
            out = jnp.einsum('ech,ehd->ecd', h, w2) * buf_w.reshape(E, cap, 1)
            y = jnp.zeros((N + 1, DIM), x.dtype).at[buf_tok].add(out.reshape(E * cap, DIM))[:N]
            z = jax.nn.silu(xf @ sw1) * (xf @ sw3) @ sw2
            return (y + z).reshape(shape)
        return _forward(x, wg, w1, w2, w3, sw1, sw2, sw3)
    x = x + _L0_gnn_ref(_layernorm(x, axis=-1), adj, adj)
    x = x + _L0_ffn_ref(_layernorm(x, axis=-1)[None], L0_ffn_router_w, L0_ffn_router_b, L0_ffn_W1, L0_ffn_b1, L0_ffn_W2, L0_ffn_b2)[0]
    x = x + _L1_gnn_ref(_layernorm(x, axis=-1), adj, L1_gnn_W, L1_gnn_a1, L1_gnn_a2, L1_gnn_W1, L1_gnn_b1, L1_gnn_W2, L1_gnn_b2, L1_gnn_W3, L1_gnn_b3, L1_gnn_W4, L1_gnn_b4)
    x = x + _L1_ffn_ref(_layernorm(x, axis=-1)[None], L1_ffn_wg, L1_ffn_w1, L1_ffn_w2, L1_ffn_w3, L1_ffn_sw1, L1_ffn_sw2, L1_ffn_sw3)[0]
    return x

_drawn_inputs = setup_inputs


def setup_inputs(seed=0):
    import zlib

    import numpy as np

    out = dict(_drawn_inputs(seed))
    spreads = {'L1_gnn_b1': (0.0, 0.304),
     'L1_gnn_b2': (0.0, 0.1),
     'L1_gnn_b3': (0.0, 0.1),
     'L1_gnn_b4': (0.0, 0.1)}
    factors = {'L0_ffn_b1': 3.444, 'L1_gnn_a1': 17.9, 'L1_gnn_a2': 2.688}
    for name, (base, spread) in spreads.items():
        noise = np.random.default_rng([zlib.crc32(name.encode()), seed]).standard_normal(out[name].shape)
        drawn = base * np.exp(spread * noise) if base else spread * noise
        out[name] = jnp.asarray(drawn.astype(out[name].dtype))
    for name, factor in factors.items():
        out[name] = (out[name] * factor).astype(out[name].dtype)
    return out
```

```python
from contextlib import ExitStack

import numpy as np

import concourse.bass as bass
from concourse import mybir

ALU = mybir.AluOpType
ACT = mybir.ActivationFunctionType
AX = mybir.AxisListType.X
F32 = mybir.dt.float32
BF16 = mybir.dt.bfloat16
U32 = mybir.dt.uint32
I32 = mybir.dt.int32

P = 128
N, D = 2048, 512
NT = N // P
DC = D // P
NB = 512
EPS = 1e-5

E0, F0 = 8, 256
HC0 = F0 // P
HEADS, HID = 8, 64
HP = HEADS // 2
ALPHA = 0.2
BIG = float(2**53)
NW = 1024
M1, M2, M3 = 256, 128, 256
E1, K1, G1, KG = 32, 4, 8, 4
EG = E1 // G1
CAP = int(1.25 * N * K1 / E1)
SLOTS = E1 * CAP
CT = [min(P, CAP - j) for j in range(0, CAP, P)]
NCT = len(CT)


def layernorm_block(nc, c, tag, transposed, rows=None):
    with ExitStack() as ctx:
        stats = ctx.enter_context(nc.sbuf_tensor(f"ln_stats{tag}", [P, NT, 6], F32))
        mv = ctx.enter_context(nc.sbuf_tensor(f"ln_mv{tag}", [P, NT, 2], F32))
        std = ctx.enter_context(nc.sbuf_tensor(f"ln_std{tag}", [P, NT], F32))
        rstd = ctx.enter_context(nc.sbuf_tensor(f"ln_rstd{tag}", [P, NT], F32))
        if rows is None:
            rows = ctx.enter_context(nc.sbuf_tensor(f"ln_rows{tag}", [P, NT, D], F32))
        banks = [ctx.enter_context(nc.psum_tensor(f"ln_ps{tag}{i}", [P, DC, P], F32)) for i in range(4)]
        stats_ready = nc.alloc_semaphore(f"ln_stats_ready{tag}")
        var_ready = nc.alloc_semaphore(f"ln_var_ready{tag}")
        std_ready = nc.alloc_semaphore(f"ln_std_ready{tag}")
        rstd_ready = nc.alloc_semaphore(f"ln_rstd_ready{tag}")
        rows_ready = nc.alloc_semaphore(f"ln_rows_ready{tag}")
        turned = nc.alloc_semaphore(f"ln_turned{tag}")
        bank_free = nc.alloc_semaphore(f"ln_bank_free{tag}")
        X = c.X
        with nc.Block() as block:

            @block.vector
            def _(dve):
                for t in range(NT):
                    dve.bn_stats(stats[:, t, :], X[:, t, :]).then_inc(stats_ready, 1)
                for t in range(NT):
                    dve.wait_ge(stats_ready, t + 1)
                    dve.bn_aggr(mv[:, t, :], stats[:, t, :]).then_inc(var_ready, 1)
                dve.wait_ge(var_ready, NT)
                dve.tensor_scalar(std[:, :], mv[:, :, 1], EPS, None, ALU.add).then_inc(var_ready, 1)
                dve.wait_ge(std_ready, 1)
                dve.reciprocal(rstd[:, :], std[:, :]).then_inc(rstd_ready, 1)
                dve.wait_ge(rstd_ready, 1)
                for t in range(NT):
                    dve.tensor_scalar(rows[:, t, :], X[:, t, :], mv[:, t, 0:1], rstd[:, t:t + 1],
                                      ALU.subtract, ALU.mult).then_inc(rows_ready, 1)

            @block.scalar
            def _(act):
                act.wait_ge(var_ready, NT + 1)
                act.activation(std[:, :], std[:, :], ACT.Sqrt).then_inc(std_ready, 1)
                if transposed is None:
                    return
                for t in range(NT):
                    act.wait_ge(turned, t + 1)
                    act.activation(transposed[:, :, t * P:(t + 1) * P], banks[t % 4][:, :, :],
                                   ACT.Copy).then_inc(bank_free, 1)

            @block.tensor
            def _(pe):
                if transposed is None:
                    return
                for t in range(NT):
                    pe.wait_ge(rows_ready, t + 1)
                    if t >= 4:
                        pe.wait_ge(bank_free, t - 3)
                    for k in range(DC):
                        mm = pe.transpose(banks[t % 4][:, k, :], rows[:, t, k * P:(k + 1) * P], c.ident[:, :])
                    mm.then_inc(turned, 1)


def load_block(nc, c, x, consts):
    arrived = nc.alloc_semaphore("start_arrived")
    with nc.Block() as block:

        @block.sync
        def _(sp):
            sp.dma_start(c.X[:, :, :], x.rearrange("(t p) d -> p t d", p=P)).then_inc(arrived, 16)
            for sb, dram in consts:
                sp.dma_start(sb[:, :], dram).then_inc(arrived, 16)
            sp.wait_ge(arrived, 16 * (1 + len(consts)))


def degree_block(nc, c, adj, adj_t, xn, dinv):
    with ExitStack() as ctx:
        a = [ctx.enter_context(nc.sbuf_tensor(f"deg_a{i}", [P, N], F32)) for i in range(2)]
        b = [ctx.enter_context(nc.sbuf_tensor(f"deg_b{i}", [P, N], F32)) for i in range(2)]
        sums = ctx.enter_context(nc.sbuf_tensor("deg_sums", [P, 2, NT], F32))
        small = ctx.enter_context(nc.sbuf_tensor("deg_small", [P, 5, NT], F32))
        arrived = [nc.alloc_semaphore(f"deg_arrived{i}") for i in range(2)]
        a_free = nc.alloc_semaphore("deg_a_free")
        b_free = nc.alloc_semaphore("deg_b_free")
        b_sum = nc.alloc_semaphore("deg_b_sum")
        chain = nc.alloc_semaphore("deg_chain")
        root = nc.alloc_semaphore("deg_root")
        with nc.Block() as block:

            @block.sync
            def _(sp):
                with sp.Fori(0, NT // 2) as i:
                    for s in range(2):
                        sp.wait_ge(a_free, 2 * i + s + 1)
                        sp.wait_ge(b_free, 2 * i + s + 1)
                        at = (2 * i + s) * P
                        sp.dma_start(a[s][:, :], adj[bass.ds(at, P), :]).then_inc(arrived[s], 16)
                        sp.dma_start(b[s][:, :], adj_t[bass.ds(at, P), :]).then_inc(arrived[s], 16)

            @block.scalar
            def _(act):
                act.sem_inc(b_free, 2)
                for t in range(NT):
                    act.wait_ge(arrived[t % 2], 32 * (t // 2 + 1))
                    act.activation(b[t % 2][:, :], b[t % 2][:, :], ACT.Copy,
                                   accum_out=sums[:, 1, t:t + 1]).then_inc(b_free, 1)
                act.wait_ge(chain, 3)
                act.activation(small[:, 2, :], small[:, 1, :], ACT.Sqrt).then_inc(root, 1)

            @block.vector
            def _(dve):
                dve.sem_inc(a_free, 2)
                for t in range(NT):
                    dve.wait_ge(arrived[t % 2], 32 * (t // 2 + 1))
                    dve.tensor_reduce(sums[:, 0, t:t + 1], a[t % 2][:, :], AX, ALU.add).then_inc(a_free, 1)
                dve.wait_ge(a_free, NT + 2)
                dve.wait_ge(b_free, NT + 2)
                deg, safe, rt, inv, above = (small[:, k, :] for k in range(5))
                dve.tensor_tensor(deg, sums[:, 0, :], sums[:, 1, :], ALU.add).then_inc(chain, 1)
                dve.wait_ge(chain, 1)
                dve.tensor_scalar(deg, deg, 0.5, 1.0, ALU.mult, ALU.add).then_inc(chain, 1)
                dve.wait_ge(chain, 2)
                dve.tensor_scalar(safe, deg, 1e-30, None, ALU.max).then_inc(chain, 1)
                dve.tensor_scalar(above, deg, 0.0, None, ALU.is_gt).then_inc(chain, 1)
                dve.wait_ge(root, 1)
                dve.reciprocal(inv, rt).then_inc(chain, 1)
                dve.wait_ge(chain, 5)
                dve.tensor_tensor(dinv[:, :], inv, above, ALU.mult).then_inc(chain, 1)
                dve.wait_ge(chain, 6)
                for t in range(NT):
                    dve.tensor_scalar(xn[:, t, :], xn[:, t, :], dinv[:, t:t + 1], None,
                                      ALU.mult).then_inc(chain, 1)


def mix_block(nc, c, adj, adj_t, z, y, dinv):
    first = z is not None
    tag = "s" if first else "a"
    src = z if first else y
    with ExitStack() as ctx:
        pa = [ctx.enter_context(nc.sbuf_tensor(f"mix_{tag}_pa{i}", [P, NT, P], F32)) for i in range(2)]
        pb = [ctx.enter_context(nc.sbuf_tensor(f"mix_{tag}_pb{i}", [P, NT, P], F32)) for i in range(2)] if first else None
        half = [ctx.enter_context(nc.sbuf_tensor(f"mix_{tag}_half{i}", [P, D], F32)) for i in range(2)] if first else None
        ps = [ctx.enter_context(nc.psum_tensor(f"mix_{tag}_ps{i}", [P, D], F32)) for i in range(2)]
        arrived = [nc.alloc_semaphore(f"mix_{tag}_arrived{i}") for i in range(2)]
        panel_ready = nc.alloc_semaphore(f"mix_{tag}_panel_ready")
        product = nc.alloc_semaphore(f"mix_{tag}_product")
        bank_free = nc.alloc_semaphore(f"mix_{tag}_bank_free")
        halved = nc.alloc_semaphore(f"mix_{tag}_halved")
        half_free = nc.alloc_semaphore(f"mix_{tag}_half_free")
        a_v = adj.rearrange("(k p) m -> p k m", p=P)
        at_v = adj_t.rearrange("(k p) m -> p k m", p=P)
        with nc.Block() as block:

            @block.sync
            def _(sp):
                def load(i, s):
                    cols = bass.ds((2 * i + s) * P, P)
                    sp.dma_start(pa[s][:, :, :], at_v[:, :, cols]).then_inc(arrived[s], 16)
                    if first:
                        sp.dma_start(pb[s][:, :, :], a_v[:, :, cols]).then_inc(arrived[s], 16)

                load(0, 0)
                load(0, 1)
                with sp.Fori(0, NT // 2 - 1) as i:
                    for s in range(2):
                        sp.wait_ge(product, 2 * i + s + 1)
                        load(i + 1, s)

            @block.vector
            def _(dve):
                dve.sem_inc(bank_free, 2)

                def panel(i, s):
                    dve.wait_ge(arrived[s], 32 * i + 32)
                    dve.tensor_tensor(pa[s][:, :, :], pa[s][:, :, :], pb[s][:, :, :],
                                      ALU.add).then_inc(panel_ready, 1)

                def finish(i, s):
                    dve.wait_ge(product, 2 * i + s + 1)
                    t = 2 * i + s
                    if first:
                        dve.wait_ge(half_free, 2 * i + s + 1)
                        dve.scalar_tensor_tensor(out=half[s][:, :], in0=ps[s][:, :], scalar=0.5, in1=z[:, t, :],
                                                 op0=ALU.mult, op1=ALU.add).then_inc(halved, 1)
                    else:
                        dve.tensor_tensor(c.X[:, t, :], ps[s][:, :], c.X[:, t, :], ALU.add).then_inc(bank_free, 1)

                if first:
                    panel(0, 0)
                    panel(0, 1)
                    with dve.Fori(0, NT // 2 - 1) as i:
                        for s in range(2):
                            finish(i, s)
                            panel(i + 1, s)
                    for s in range(2):
                        finish(NT // 2 - 1, s)
                else:
                    with dve.Fori(0, NT // 2) as i:
                        for s in range(2):
                            finish(i, s)

            @block.scalar
            def _(act):
                if not first:
                    return
                act.sem_inc(half_free, 2)
                with act.Fori(0, NT // 2) as i:
                    for s in range(2):
                        act.wait_ge(arrived[s], 32)
                        act.wait_ge(halved, 2 * i + s + 1)
                        act.sem_inc(c.passed, 1)
                        act.activation(y[:, 2 * i + s, :], half[s][:, :], ACT.Copy,
                                       scale=dinv[:, bass.ds(2 * i + s, 1)]).then_inc(half_free, 1)

            @block.tensor
            def _(pe):
                with pe.Fori(0, NT // 2) as i:
                    for s in range(2):
                        if first:
                            pe.wait_ge(panel_ready, 2 * i + s + 1)
                            pe.wait_ge(half_free, 2 * i + s + 1)
                        else:
                            pe.wait_ge(arrived[s], 16 * i + 16)
                            pe.wait_ge(bank_free, 2 * i + s + 1)
                        for k in range(NT):
                            mm = pe.matmul(ps[s][:, :], pa[s][:, k, :], src[:, k, :],
                                           start=(k == 0), stop=(k == NT - 1))
                        mm.then_inc(product, 1)


def moe0_block(nc, c, xt, router_w, router_b, w1, b1, w2, b2):
    with ExitStack() as ctx:
        def sb(name, shape, dt=F32):
            return ctx.enter_context(nc.sbuf_tensor(f"m0_{name}", shape, dt))
        rw = sb("rw", [P, DC, E0])
        rb = sb("rb", [P, E0])
        b1s = sb("b1", [P, E0 * HC0])
        b2s = sb("b2", [E0, D])
        w1s = [sb(f"w1_{i}", [P, DC, F0]) for i in range(2)]
        w2s = [sb(f"w2_{i}", [P, HC0, D]) for i in range(2)]
        ht = [sb(f"ht{i}", [P, HC0, NB]) for i in range(2)]
        lg = sb("lg", [P, NT, E0])
        ex = sb("ex", [P, NT, E0])
        top = sb("top", [P, NT, 8])
        idx = sb("idx", [P, NT, 8], U32)
        idf = sb("idf", [P, NT, 8])
        sel = sb("sel", [P, NT, E0])
        sel2 = sb("sel2", [P, NT, E0])
        col = sb("col", [P, NT])
        R = sb("R", [P, E0 * NT])
        RT = sb("RT", [E0, N])
        psh = [ctx.enter_context(nc.psum_tensor(f"m0_h{i}", [P, NB], F32)) for i in range(4)]
        pso = [ctx.enter_context(nc.psum_tensor(f"m0_o{i}", [P, NB], F32)) for i in range(4)]
        s = lambda name: nc.alloc_semaphore(f"m0_{name}")
        small_in, logits, chain, expd = s("small_in"), s("logits"), s("chain"), s("expd")
        turned, rt_ready = s("turned"), s("rt_ready")
        w_in = [s("w_in0"), s("w_in1")]
        w_free, h_ready, h_done, o_ready, o_free = s("w_free"), s("h_ready"), s("h_done"), s("o_ready"), s("o_free")
        NBS = N // NB
        TPB = NB // P
        STEPS = 2 * NBS
        with nc.Block() as block:

            @block.sync
            def _(sp):
                sp.dma_start(rw[:, :, :], router_w.rearrange("(k p) e -> p k e", p=P)).then_inc(small_in, 16)
                sp.dma_start(rb[:, :], router_b.rearrange("(a e) -> a e", a=1).broadcast_to([P, E0])).then_inc(small_in, 16)
                sp.dma_start(b1s[:, :], b1).then_inc(small_in, 16)
                sp.dma_start(b2s[:, :], b2).then_inc(small_in, 16)
                with sp.Fori(0, E0 // 2) as i:
                    for u in range(2):
                        sp.wait_ge(w_free, 2 * i + u + 1)
                        sp.dma_start(w1s[u][:, :, :], w1[bass.ds((2 * i + u) * D, D), :].rearrange("(k p) f -> p k f", p=P)).then_inc(w_in[u], 16)
                        sp.dma_start(w2s[u][:, :, :], w2[bass.ds((2 * i + u) * F0, F0), :].rearrange("(k p) f -> p k f", p=P)).then_inc(w_in[u], 16)

            @block.tensor
            def _(pe):
                pe.sem_inc(w_free, 2)
                pe.wait_ge(small_in, 64)
                lgp = psh[0][:, 0:NT * E0].rearrange("p (t e) -> p t e", e=E0)
                for t in range(NT):
                    for k in range(DC):
                        mm = pe.matmul(lgp[:, t, :], xt[:, k, t * P:(t + 1) * P], rw[:, k, :],
                                       start=(k == 0), stop=(k == DC - 1))
                mm.then_inc(logits, 1)
                pe.wait_ge(chain, 13)
                for t in range(NT):
                    mm = pe.transpose(psh[t // TPB][0:E0, (t % TPB) * P:(t % TPB + 1) * P],
                                      R[:, :].rearrange("p (e t) -> p t e", t=NT)[:, t, :], c.ident[:, :])
                mm.then_inc(turned, 1)
                pe.wait_ge(rt_ready, 1)
                for t in range(NT):
                    pe.wait_ge(o_free, t + 1)
                    pe.matmul(pso[t % 4][:, :], RT[:, t * P:(t + 1) * P], b2s[:, :],
                              start=True, stop=True).then_inc(o_ready, 1)

                def hidden(i, v):
                    u, nb = v // NBS, v % NBS
                    if nb == 0:
                        pe.wait_ge(w_in[u], 32 * i + 32)
                    for h in range(HC0):
                        if v >= 2:
                            pe.wait_ge(h_done, (STEPS * i + v - 2) * HC0 + h + 1)
                        for k in range(DC):
                            mm = pe.matmul(psh[(v % 2) * HC0 + h][:, :], w1s[u][:, k, h * P:(h + 1) * P],
                                           xt[:, k, nb * NB:(nb + 1) * NB], start=(k == 0), stop=(k == DC - 1))
                        mm.then_inc(h_ready, 1)

                def outs(i, v):
                    u, nb = v // NBS, v % NBS
                    pe.wait_ge(h_done, (STEPS * i + v + 1) * HC0)
                    for j in range(TPB):
                        pe.wait_ge(o_free, NT + (STEPS * i + v) * TPB + j + 1)
                        for h in range(HC0):
                            mm = pe.matmul(pso[j][:, :], ht[v % 2][:, h, j * P:(j + 1) * P], w2s[u][:, h, :],
                                           start=(h == 0), stop=(h == HC0 - 1))
                        mm.then_inc(o_ready, 1)

                with pe.Fori(0, E0 // 2) as i:
                    for v in range(STEPS):
                        hidden(i, v)
                        if v:
                            outs(i, v - 1)
                        if v == NBS:
                            pe.wait_ge(o_ready, NT + (STEPS * i + NBS) * TPB)
                            pe.sem_inc(w_free, 1)
                    outs(i, STEPS - 1)
                    pe.wait_ge(o_ready, NT + (STEPS * i + STEPS) * TPB)
                    pe.sem_inc(w_free, 1)

            @block.scalar
            def _(act):
                act.wait_ge(chain, 3)
                act.activation(ex[:, :, :], lg[:, :, :], ACT.Exp).then_inc(expd, 1)
                act.wait_ge(turned, 1)
                for q in range(4):
                    ins = act.activation(RT[:, q * NB:(q + 1) * NB], psh[q][0:E0, :], ACT.Copy)
                ins.then_inc(rt_ready, 1)
                with act.Fori(0, E0 // 2) as i:
                    for v in range(STEPS):
                        for h in range(HC0):
                            act.wait_ge(small_in, 64)
                            act.wait_ge(h_ready, (STEPS * i + v) * HC0 + h + 1)
                            act.sem_inc(c.passed, 1)
                            bias = b1s[:, bass.ds((2 * i + v // NBS) * HC0 + h, 1)]
                            act.activation(ht[v % 2][:, h, :], psh[(v % 2) * HC0 + h][:, :], ACT.Gelu,
                                           bias=bias).then_inc(h_done, 1)

            @block.vector
            def _(dve):
                dve.sem_inc(o_free, 4)
                n = [0]

                def link(ins):
                    n[0] += 1
                    ins.then_inc(chain, 1)
                    dve.wait_ge(chain, n[0])

                dve.wait_ge(small_in, 64)
                dve.wait_ge(logits, 1)
                link(dve.tensor_tensor(lg[:, :, :], psh[0][:, 0:NT * E0].rearrange("p (t e) -> p t e", e=E0),
                                       rb[:, :].unsqueeze(1).broadcast_to([P, NT, E0]), ALU.add))
                link(dve.tensor_reduce(col[:, :], lg[:, :, :], AX, ALU.max))
                link(dve.tensor_tensor(lg[:, :, :], lg[:, :, :], col[:, :].unsqueeze(2).broadcast_to([P, NT, E0]), ALU.subtract))
                dve.wait_ge(expd, 1)
                for t in range(NT):
                    ins = dve.max(top[:, t, :], ex[:, t, :])
                link(ins)
                for t in range(NT):
                    ins = dve.max_index(idx[:, t, :], top[:, t, :], ex[:, t, :])
                link(ins)
                link(dve.tensor_copy(idf[:, :, :], idx[:, :, :]))
                iota = c.iota[:, 0:E0].unsqueeze(1).broadcast_to([P, NT, E0])
                link(dve.tensor_tensor(sel[:, :, :], iota, idf[:, :, 0:1].broadcast_to([P, NT, E0]), ALU.is_equal))
                link(dve.tensor_tensor(sel2[:, :, :], iota, idf[:, :, 1:2].broadcast_to([P, NT, E0]), ALU.is_equal))
                link(dve.tensor_tensor(sel[:, :, :], sel[:, :, :], sel2[:, :, :], ALU.add))
                link(dve.tensor_tensor(sel[:, :, :], sel[:, :, :], ex[:, :, :], ALU.mult))
                link(dve.tensor_tensor(col[:, :], top[:, :, 0], top[:, :, 1], ALU.add))
                link(dve.reciprocal(col[:, :], col[:, :]))
                link(dve.tensor_tensor(R[:, :].rearrange("p (e t) -> p t e", t=NT), sel[:, :, :],
                                       col[:, :].unsqueeze(2).broadcast_to([P, NT, E0]), ALU.mult))
                assert n[0] == 13
                for t in range(NT):
                    dve.wait_ge(o_ready, t + 1)
                    dve.tensor_tensor(c.X[:, t, :], pso[t % 4][:, :], c.X[:, t, :], ALU.add).then_inc(o_free, 1)
                with dve.Fori(0, E0 // 2) as i:
                    for v in range(STEPS):
                        for j in range(TPB):
                            t = (v % NBS) * TPB + j
                            at = NT + (STEPS * i + v) * TPB + j
                            dve.wait_ge(o_ready, at + 1)
                            dve.wait_ge(o_free, at + 4 - NT + 1)
                            dve.scalar_tensor_tensor(out=c.X[:, t, :], in0=pso[j][:, :],
                                                     scalar=R[:, bass.ds((2 * i + v // NBS) * NT + t, 1)],
                                                     in1=c.X[:, t, :], op0=ALU.mult, op1=ALU.add).then_inc(o_free, 1)


def project_block(nc, c, xt, w, a_rows, wh, src, dst):
    with ExitStack() as ctx:
        ws = ctx.enter_context(nc.sbuf_tensor("pr_w", [P, DC, D], F32))
        ar = ctx.enter_context(nc.sbuf_tensor("pr_a", [P, 2, D], F32))
        prod = [ctx.enter_context(nc.sbuf_tensor(f"pr_prod{i}", [P, D], F32)) for i in range(2)]
        ps = [ctx.enter_context(nc.psum_tensor(f"pr_ps{i}", [P, D], F32)) for i in range(4)]
        arrived, done, copied = (nc.alloc_semaphore(f"pr_{n}") for n in ("arrived", "done", "copied"))
        multiplied, reduced = (nc.alloc_semaphore(f"pr_{n}") for n in ("multiplied", "reduced"))
        with nc.Block() as block:

            @block.sync
            def _(sp):
                sp.dma_start(ws[:, :, :], w.rearrange("(k p) f -> p k f", p=P)).then_inc(arrived, 16)
                for j in range(2):
                    sp.dma_start(ar[:, j, :], a_rows[j:j + 1, :].broadcast_to([P, D])).then_inc(arrived, 16)

            @block.tensor
            def _(pe):
                pe.wait_ge(arrived, 48)
                for t in range(NT):
                    if t >= 4:
                        pe.wait_ge(copied, t - 3)
                    for k in range(DC):
                        mm = pe.matmul(ps[t % 4][:, :], xt[:, k, t * P:(t + 1) * P], ws[:, k, :],
                                       start=(k == 0), stop=(k == DC - 1))
                    mm.then_inc(done, 1)

            @block.scalar
            def _(act):
                for t in range(NT):
                    act.wait_ge(done, t + 1)
                    act.activation(wh[:, t, 0:D], ps[t % 4][:, :], ACT.Copy)
                    act.activation(wh[:, t, D:D + HID], ps[t % 4][:, 0:HID], ACT.Copy).then_inc(copied, 1)

            @block.vector
            def _(dve):
                dve.wait_ge(arrived, 48)
                for t in range(NT):
                    dve.wait_ge(copied, t + 1)
                    for j, to in enumerate((src, dst)):
                        m = 2 * t + j
                        if m >= 2:
                            dve.wait_ge(reduced, m - 1)
                        dve.tensor_tensor(prod[j][:, :], wh[:, t, 0:D], ar[:, j, :], ALU.mult).then_inc(multiplied, 1)
                    for j, to in enumerate((src, dst)):
                        dve.wait_ge(multiplied, 2 * t + j + 1)
                        dve.tensor_reduce(to[:, :, t], prod[j][:, :].rearrange("p (h d) -> p h d", d=HID), AX,
                                          ALU.add).then_inc(reduced, 1)


def rows_out(nc, c, ctx, tag, parts):
    sbs = [ctx.enter_context(nc.sbuf_tensor(f"rows{tag}{j}", [f.shape[1], N], dt)) for j, (f, dt, _) in enumerate(parts)]
    banks = [ctx.enter_context(nc.psum_tensor(f"rows{tag}_ps{i}", [32, NB], F32)) for i in range(4)]
    turned, copied, stored = (nc.alloc_semaphore(f"rows{tag}_{n}") for n in ("turned", "copied", "stored"))
    with nc.Block() as block:

        @block.tensor
        def _(pe):
            for j, (f, _, _) in enumerate(parts):
                r = f.shape[1]
                for q in range(N // NB):
                    if j:
                        pe.wait_ge(copied, (j - 1) * (N // NB) + q + 1)
                    for m in range(NB // P):
                        mm = pe.transpose(banks[q][0:r, m * P:(m + 1) * P], f[:, :, q * (NB // P) + m], c.ident[:, :])
                    mm.then_inc(turned, 1)

        @block.vector
        def _(dve):
            for j, (f, _, _) in enumerate(parts):
                r = f.shape[1]
                for q in range(N // NB):
                    dve.wait_ge(turned, j * (N // NB) + q + 1)
                    dve.tensor_copy(sbs[j][:, q * NB:(q + 1) * NB], banks[q][0:r, :]).then_inc(copied, 1)

        @block.sync
        def _(sp):
            for j, (_, _, to) in enumerate(parts):
                sp.wait_ge(copied, (j + 1) * (N // NB))
                sp.dma_start(to, sbs[j][:, :]).then_inc(stored, 16)
            sp.wait_ge(stored, 16 * len(parts))


def neighbour_max_block(nc, c, adj, dst_rows, maxd):
    with ExitStack() as ctx:
        dst_bc = ctx.enter_context(nc.sbuf_tensor("nm_dst", [P, HEADS, N], F32))
        a = [ctx.enter_context(nc.sbuf_tensor(f"nm_a{i}", [P, N], F32)) for i in range(2)]
        masks = [ctx.enter_context(nc.sbuf_tensor(f"nm_mask{i}", [P, N], F32)) for i in range(2)]
        sums = ctx.enter_context(nc.sbuf_tensor("nm_sums", [P, N], F32))
        acc = [ctx.enter_context(nc.sbuf_tensor(f"nm_acc{i}", [P, HEADS], F32)) for i in range(2)]
        dst_in = nc.alloc_semaphore("nm_dst_in")
        a_in = [nc.alloc_semaphore(f"nm_a_in{i}") for i in range(2)]
        masked, maxed, kept = (nc.alloc_semaphore(f"nm_{n}") for n in ("masked", "maxed", "kept"))
        with nc.Block() as block:

            @block.sync
            def _(sp):
                def load(t, s):
                    sp.dma_start(a[s][:, :], adj[bass.ds(t * P, P), :]).then_inc(a_in[s], 16)

                load(0, 0)
                load(1, 1)
                for h in range(HEADS):
                    sp.dma_start(dst_bc[:, h, :], dst_rows[h:h + 1, :].broadcast_to([P, N])).then_inc(dst_in, 16)
                with sp.Fori(0, NT // 2 - 1) as i:
                    for s in range(2):
                        sp.wait_ge(masked, 2 * i + s + 1)
                        load(2 * i + 2 + s, s)

            @block.vector
            def _(dve):
                dve.wait_ge(dst_in, 16 * HEADS)
                with dve.Fori(0, NT // 2) as i:
                    for s in range(2):
                        dve.wait_ge(a_in[s], 16 * i + 16)
                        dve.tensor_scalar(masks[s][:, :], a[s][:, :], 0.0, -BIG / ALPHA, ALU.is_le, ALU.mult).then_inc(masked, 1)
                        for h in range(HEADS):
                            dve.wait_ge(dst_in, 16 * HEADS)
                            if h:
                                dve.wait_ge(maxed, (2 * i + s) * HEADS + h)
                            else:
                                dve.wait_ge(masked, 2 * i + s + 1)
                            dve.sem_inc(c.passed, 1)
                            dve.tensor_tensor_reduce(out=sums[:, :], in0=dst_bc[:, h, :], in1=masks[s][:, :], scale=1.0,
                                                     scalar=-3.0e38, op0=ALU.add, op1=ALU.max,
                                                     accum_out=acc[s][:, h:h + 1]).then_inc(maxed, 1)
                        dve.wait_ge(maxed, (2 * i + s + 1) * HEADS)
                        dve.tensor_copy(maxd[:, :, bass.ds(2 * i + s, 1)], acc[s][:, :].unsqueeze(2)).then_inc(kept, 1)


def row_terms_block(nc, c, src, dst, maxd, s8, d8, v):
    with ExitStack() as ctx:
        s = ctx.enter_context(nc.sbuf_tensor("rt_s", [P, HEADS, NT], F32))
        m = ctx.enter_context(nc.sbuf_tensor("rt_m", [P, HEADS, NT], F32))
        chain = nc.alloc_semaphore("rt_chain")
        with nc.Block() as block:

            @block.vector
            def _(dve):
                n = [0]

                def link(ins):
                    n[0] += 1
                    ins.then_inc(chain, 1)
                    dve.wait_ge(chain, n[0])

                al = lambda t: t[:, :, :]
                link(dve.tensor_tensor(al(s), al(src), al(maxd), ALU.add))
                link(dve.scalar_tensor_tensor(out=al(m), in0=al(s), scalar=ALPHA, in1=al(s), op0=ALU.mult, op1=ALU.max))
                link(dve.scalar_tensor_tensor(out=al(v), in0=al(src), scalar=ALPHA, in1=al(m), op0=ALU.mult, op1=ALU.subtract))
                link(dve.tensor_scalar(al(s8), al(src), 1.0 - ALPHA, None, ALU.mult))
                link(dve.tensor_scalar(al(d8), al(dst), ALPHA - 1.0, None, ALU.mult))


def attention_block(nc, c, adj_t, wh, dst, d8, s8_rows, v_rows, sums, weights):
    MASK_STEPS = 4
    POOLED = MASK_STEPS - 1
    TAIL_AT, NEXT_AT = 6, 8
    with ExitStack() as ctx:
        def sb(name, shape, dt=F32):
            return ctx.enter_context(nc.sbuf_tensor(f"at_{name}", shape, dt))
        mask = sb("mask", [P, NT, N], BF16)
        work = sb("work", [P, 8, NW])
        arg = [work[:, i, :] for i in range(4)]
        pr = [work[:, 4 + i, :] for i in range(4)]
        at = [work[:, 2 * i:2 * i + 2, :].rearrange("p a n -> p (a n)") for i in range(2)]
        whc = [sb(f"whc{i}", [P, NT, P]) for i in range(2)]
        s8 = [sb(f"s8_{i}", [P, NW]) for i in range(2)]
        vb = [sb(f"v{i}", [P, NW]) for i in range(2)]
        stage = [sb(f"stage{i}", [P, NW]) for i in range(2)]
        pso = [ctx.enter_context(nc.psum_tensor(f"at_pso{i}", [P, NW], F32)) for i in range(2)]
        s = lambda name: nc.alloc_semaphore(f"at_{name}")
        at_in = [s("at_in0"), s("at_in1")]
        rows_in = [s("rows_in0"), s("rows_in1")]
        mask_ready, ones_ready, whc_ready = s("mask_ready"), s("ones_ready"), s("whc_ready")
        arg_ready, pooled, self_masked, pr_ready, pr_used = s("arg_ready"), s("pooled"), s("self_masked"), s("pr_ready"), s("pr_used")
        pso_free, staged, stage_free, stored = s("pso_free"), s("staged"), s("stage_free"), s("stored")
        NBW = N // NW
        W2 = NW // NB
        PAIR = 2 * NT
        order = [(b, h) for b in range(NBW) for h in range(HEADS)]
        flat = lambda a: a[:, :, :].rearrange("p h t -> p (h t)")
        with nc.Block() as block:

            @block.sync
            def _(sp):
                sp.sem_inc(stage_free, 3)
                for t in range(NT):
                    if t >= 2:
                        sp.wait_ge(mask_ready, t - 1)
                    sp.dma_start(at[t % 2], adj_t[t * P:(t + 1) * P, :]).then_inc(at_in[t % 2], 16)

                def store(n):
                    b, h = order[n]
                    mine, other = (n % 2) * HID, (1 - n % 2) * HID
                    sp.wait_ge(staged, n + 2)
                    sp.dma_start(sums[n * HID:(n + 1) * HID, :], stage[n % 2][mine:mine + HID, :]).then_inc(stored, 16)
                    sp.dma_start(weights[n:n + 1, :], stage[n % 2][other:other + 1, :]).then_inc(stored, 16)
                    sp.wait_ge(stored, 32 * (n + 1))
                    sp.sem_inc(stage_free, 1)

                for n, (b, h) in enumerate(order):
                    if n >= 2:
                        sp.wait_ge(arg_ready, NT * (n - 1))
                    cols = slice(b * NW, (b + 1) * NW)
                    sp.dma_start(s8[n % 2][:, :], s8_rows[h:h + 1, cols].broadcast_to([P, NW])).then_inc(rows_in[n % 2], 16)
                    sp.dma_start(vb[n % 2][:, :], v_rows[h:h + 1, cols].broadcast_to([P, NW])).then_inc(rows_in[n % 2], 16)
                    if n >= 2:
                        store(n - 2)
                for n in range(len(order) - 2, len(order)):
                    store(n)

            @block.gpsimd
            def _(pool):
                pool.memset(whc[0][:, :, HID:P], 1.0).then_inc(ones_ready, 1)
                pool.memset(whc[1][:, :, 0:HID], 1.0).then_inc(ones_ready, 1)
                pool.wait_ge(mask_ready, NT)
                with pool.Fori(0, NBW) as b:
                    with pool.Fori(0, HP) as i:
                        for k in range(PAIR):
                            if k % MASK_STEPS == POOLED:
                                continue
                            pool.wait_ge(arg_ready, PAIR * (HP * b + i) + k + 1)
                            pool.sem_inc(c.passed, 1)
                            pool.tensor_tensor(arg[k % 4], arg[k % 4], mask[:, k % NT, bass.ds(b * NW, NW)], ALU.add).then_inc(pooled, 1)

            @block.tensor
            def _(pe):
                pe.wait_ge(ones_ready, 2)
                with pe.Fori(0, NBW) as b:
                    with pe.Fori(0, HP) as i:
                        for k in range(PAIR):
                            u, t = k // NT, k % NT
                            if t == 0:
                                pe.wait_ge(whc_ready, 2 * (HP * b + i) + u + 1)
                                pe.wait_ge(pso_free, 2 * (HP * b + i) + u + 1)
                            pe.wait_ge(pr_ready, PAIR * (HP * b + i) + k + 5)
                            for q in range(W2):
                                at_q = slice(q * NB, (q + 1) * NB)
                                mm = pe.matmul(pso[u][:, at_q], whc[u][:, t, :], pr[k % 4][:, at_q],
                                               start=(t == 0), stop=(t == NT - 1))
                            mm.then_inc(pr_used, 1)

            @block.scalar
            def _(act):
                act.sem_inc(pr_ready, 4)

                def take(u, head):
                    act.activation(whc[u][:, :, u * HID:(u + 1) * HID], wh[:, :, bass.ds(head * HID, HID)],
                                   ACT.Copy).then_inc(whc_ready, 1)

                def tail(u, count):
                    act.wait_ge(pr_used, NT * count + 4)
                    act.wait_ge(stage_free, count + 1)
                    act.activation(stage[u][:, :], pso[u][:, :], ACT.Copy).then_inc(pso_free, 1)

                act.activation(whc[0][:, :, 0:HID], wh[:, :, 0:HID], ACT.Copy).then_inc(whc_ready, 1)
                act.wait_ge(mask_ready, NT + 1)
                with act.Fori(0, NBW) as b:
                    with act.Fori(0, HP) as i:
                        for k in range(PAIR):
                            u, t = k // NT, k % NT
                            pair = HP * b + i
                            if k % MASK_STEPS == POOLED:
                                act.wait_ge(self_masked, (PAIR // MASK_STEPS) * pair + k // MASK_STEPS + 1)
                            else:
                                act.wait_ge(pooled, (PAIR - PAIR // MASK_STEPS) * pair + k - k // MASK_STEPS + 1)
                            act.wait_ge(pr_used, PAIR * pair + k + 1)
                            act.sem_inc(c.passed, 1)
                            act.activation(pr[k % 4], arg[k % 4], ACT.Exp,
                                           bias=flat(dst)[:, bass.ds((2 * i + u) * NT + t, 1)]).then_inc(pr_ready, 1)
                            if t == TAIL_AT:
                                tail(1 - u, 2 * pair + u)
                                act.wait_ge(pso_free, 2 * pair + u + 2)
                                act.sem_inc(staged, 1)
                            if t == NEXT_AT:
                                act.wait_ge(pso_free, 2 * pair + u + 2)
                                act.sem_inc(c.passed, 1)
                                take(1 - u, 2 * i + u + 1)
                tail(1, HEADS * NBW)
                act.wait_ge(pso_free, HEADS * NBW + 2)
                act.sem_inc(staged, 1)

            @block.vector
            def _(dve):
                dve.sem_inc(pr_used, 4)
                dve.sem_inc(pso_free, 1)
                for t in range(NT):
                    dve.wait_ge(at_in[t % 2], 16 * (t // 2 + 1))
                    dve.tensor_scalar(mask[:, t, :], at[t % 2], 0.0, -BIG, ALU.is_le, ALU.mult).then_inc(mask_ready, 1)
                dve.memset(pso[1][:, :], 0.0).then_inc(mask_ready, 1)
                dve.wait_ge(mask_ready, NT + 1)
                with dve.Fori(0, NBW) as b:
                    with dve.Fori(0, HP) as i:
                        for k in range(PAIR):
                            g = PAIR * (HP * b + i) + k
                            u = k // NT
                            dve.wait_ge(pr_ready, g + 1)
                            if k % NT == 0:
                                dve.wait_ge(rows_in[u], 32 * (HP * b + i) + 32)
                            dve.scalar_tensor_tensor(
                                out=arg[k % 4], in0=s8[u][:, :], scalar=flat(d8)[:, bass.ds((2 * i + u) * NT + k % NT, 1)],
                                in1=vb[u][:, :], op0=ALU.max, op1=ALU.add).then_inc(arg_ready, 1)
                            if k % MASK_STEPS == POOLED:
                                dve.wait_ge(arg_ready, g + 1)
                                dve.tensor_tensor(arg[k % 4], arg[k % 4], mask[:, k % NT, bass.ds(b * NW, NW)], ALU.add).then_inc(self_masked, 1)


def encoder_block(nc, c, sums, weights, reciprocals, ws, bs):
    TILES = N // NW * HP
    dims = (D, M1, M2, M3)
    with ExitStack() as ctx:
        encs = ctx.enter_context(nc.sbuf_tensor("en_enc", [P, TILES, NW], F32))
        rec = ctx.enter_context(nc.sbuf_tensor("en_rec", [P, TILES, NW], F32))
        low = [ctx.enter_context(nc.sbuf_tensor(f"en_low{i}", [P, NW], F32)) for i in range(2)]
        den = ctx.enter_context(nc.sbuf_tensor("en_den", [P, N // NW * HEADS * NW // P], F32))
        w = [ctx.enter_context(nc.sbuf_tensor(f"en_w{j}", [P, dims[j] // P, dims[j + 1] if j < 3 else D], F32)) for j in range(4)]
        bias = [ctx.enter_context(nc.sbuf_tensor(f"en_b{j}", [P, dims[j + 1] // P], F32)) for j in range(3)]
        b4 = ctx.enter_context(nc.sbuf_tensor("en_b4", [P, D], F32))
        hid = [ctx.enter_context(nc.sbuf_tensor(f"en_h{j}", [P, dims[j + 1] // P, NB], F32)) for j in range(3)]
        psh = [ctx.enter_context(nc.psum_tensor(f"en_ph{i}", [P, NB], F32)) for i in range(2)]
        pso = [ctx.enter_context(nc.psum_tensor(f"en_po{i}", [P, NB], F32)) for i in range(4)]
        s = lambda name: nc.alloc_semaphore(f"en_{name}")
        arrived, h_ready, h_done, o_ready, o_free, biased = (s(n) for n in ("arrived", "h_ready", "h_done", "o_ready", "o_free", "biased"))
        den_in, inverted, rec_out, mean, halves, exped = (s(n) for n in ("den_in", "inverted", "rec_out", "mean", "halves", "exped"))
        rec_in = [s("rec_in0"), s("rec_in1")]
        enc_ready = s("enc_ready")
        hidden = [(j, o) for j in range(3) for o in range(dims[j + 1] // P)]
        TPB = NB // P
        with nc.Block() as block:

            @block.sync
            def _(sp):
                sp.dma_start(den[:, :], weights.rearrange("r (a n) -> (r a) n", n=den.shape[1])).then_inc(den_in, 16)
                sp.dma_start(encs[:, :, :], sums.rearrange("(a p) n -> p a n", p=P)).then_inc(arrived, 16)
                sp.wait_ge(inverted, 1)
                sp.dma_start(reciprocals.rearrange("r (a n) -> (r a) n", n=den.shape[1]), den[:, :]).then_inc(rec_out, 16)
                sp.wait_ge(rec_out, 16)
                for j in range(TILES):
                    if j >= 2:
                        sp.wait_ge(mean, j - 1)
                    for u in range(2):
                        r = 2 * j + u
                        sp.dma_start(rec[u * HID:(u + 1) * HID, j, :], reciprocals[r:r + 1, :].broadcast_to([HID, NW])).then_inc(rec_in[j % 2], 16)
                for j in range(4):
                    sp.dma_start(w[j][:, :, :], ws[j].rearrange("(k p) o -> p k o", p=P)).then_inc(arrived, 16)
                for j in range(3):
                    sp.dma_start(bias[j][:, :], bs[j]).then_inc(arrived, 16)
                sp.dma_start(b4[:, :], bs[3].rearrange("(a n) -> a n", a=1).broadcast_to([P, D])).then_inc(arrived, 16)

            @block.tensor
            def _(pe):
                pe.wait_ge(arrived, 144)
                for q in range(N // NB):
                    if q % (NW // NB) == 0:
                        pe.wait_ge(enc_ready, (q // (NW // NB) + 1) * HP)
                    b, at_q = q // (NW // NB), slice((q % (NW // NB)) * NB, (q % (NW // NB) + 1) * NB)
                    for x, (j, o) in enumerate(hidden):
                        m = q * len(hidden) + x
                        need = max(m - 1, q * len(hidden) + (0 if j == 0 else [h[0] for h in hidden].index(j)))
                        if need:
                            pe.wait_ge(h_done, need)
                        for k in range(dims[j] // P):
                            rhs = encs[:, b * HP + k, at_q] if j == 0 else hid[j - 1][:, k, :]
                            mm = pe.matmul(psh[m % 2][:, :], w[j][:, k, o * P:(o + 1) * P], rhs,
                                           start=(k == 0), stop=(k == dims[j] // P - 1))
                        mm.then_inc(h_ready, 1)
                    pe.wait_ge(h_done, (q + 1) * len(hidden))
                    for t in range(TPB):
                        pe.wait_ge(o_free, q * TPB + t + 1)
                        for k in range(M3 // P):
                            mm = pe.matmul(pso[t][:, :], hid[2][:, k, t * P:(t + 1) * P], w[3][:, k, :],
                                           start=(k == 0), stop=(k == M3 // P - 1))
                        mm.then_inc(o_ready, 1)

            @block.scalar
            def _(act):
                for j in range(TILES):
                    act.wait_ge(halves, j + 1)
                    act.activation(low[j % 2][:, :], low[j % 2][:, :], ACT.Exp).then_inc(exped, 1)
                act.wait_ge(arrived, 144)
                for q in range(N // NB):
                    for x, (j, o) in enumerate(hidden):
                        m = q * len(hidden) + x
                        act.wait_ge(h_ready, m + 1)
                        act.activation(hid[j][:, o, :], psh[m % 2][:, :], ACT.Relu, bias=bias[j][:, o:o + 1]).then_inc(h_done, 1)

            @block.vector
            def _(dve):
                dve.sem_inc(o_free, 4)
                dve.wait_ge(den_in, 16)
                dve.reciprocal(den[:, :], den[:, :]).then_inc(inverted, 1)
                dve.wait_ge(arrived, 16)

                def elu_end(j):
                    dve.wait_ge(exped, j + 1)
                    dve.scalar_tensor_tensor(out=encs[:, j, :], in0=low[j % 2][:, :], scalar=-1.0, in1=encs[:, j, :],
                                             op0=ALU.add, op1=ALU.max).then_inc(enc_ready, 1)

                for j in range(TILES):
                    dve.wait_ge(rec_in[j % 2], 32 * (j // 2 + 1))
                    dve.tensor_tensor(encs[:, j, :], encs[:, j, :], rec[:, j, :], ALU.mult).then_inc(mean, 1)
                    if j:
                        elu_end(j - 1)
                    dve.wait_ge(mean, j + 1)
                    if j >= 2:
                        dve.wait_ge(enc_ready, j - 1)
                    dve.tensor_scalar(low[j % 2][:, :], encs[:, j, :], 0.0, None, ALU.min).then_inc(halves, 1)
                elu_end(TILES - 1)
                dve.wait_ge(arrived, 144)
                for t in range(NT):
                    dve.tensor_tensor(c.X[:, t, :], c.X[:, t, :], b4[:, :], ALU.add).then_inc(biased, 1)
                for t in range(NT):
                    dve.wait_ge(biased, t + 1)
                    dve.wait_ge(o_ready, t + 1)
                    dve.tensor_tensor(c.X[:, t, :], pso[t % 4][:, :], c.X[:, t, :], ALU.add).then_inc(o_free, 1)


def attention_stage(nc, c, dram):
    with ExitStack() as st:
        def sb(name, shape):
            return st.enter_context(nc.sbuf_tensor(f"ga_{name}", shape, F32))
        dst_rows = nc.dram_tensor("ga_dst_rows", [HEADS, N], F32).ap()
        s8_rows = nc.dram_tensor("ga_s8_rows", [HEADS, N], F32).ap()
        v_rows = nc.dram_tensor("ga_v_rows", [HEADS, N], F32).ap()
        sums = nc.dram_tensor("ga_sums", [N // NW * D, NW], F32).ap()
        weights, reciprocals = (nc.dram_tensor(f"ga_{n}", [N // NW * HEADS, NW], F32).ap() for n in ("weights", "reciprocals"))
        src, dst, maxd = (sb(n, [P, HEADS, NT]) for n in ("src", "dst", "maxd"))
        s8, d8 = (sb(n, [P, HEADS, NT]) for n in ("s8", "d8"))
        v = sb("v", [P, HEADS, NT])
        with ExitStack() as whs:
            wh = whs.enter_context(nc.sbuf_tensor("ga_wh", [P, NT, D + HID], F32))
            with ExitStack() as pre:
                xt = pre.enter_context(nc.sbuf_tensor("ga_xt", [P, DC, N], F32))
                layernorm_block(nc, c, "2", xt)
                project_block(nc, c, xt, dram["w_heads"], dram["a_rows"], wh, src, dst)
            with ExitStack() as pre:
                rows_out(nc, c, pre, "d", [(dst, F32, dst_rows)])
            neighbour_max_block(nc, c, dram["adj"], dst_rows, maxd)
            row_terms_block(nc, c, src, dst, maxd, s8, d8, v)
            with ExitStack() as pre:
                rows_out(nc, c, pre, "s", [(s8, F32, s8_rows), (v, F32, v_rows)])
            attention_block(nc, c, dram["adj_t"], wh, dst, d8, s8_rows, v_rows, sums, weights)
        encoder_block(nc, c, sums, weights, reciprocals, [dram[f"enc_w{j}"] for j in range(4)], [dram[f"enc_b{j}"] for j in range(4)])


def route_block(nc, c, rows, xt, dram, xp, oe, slot_tokens, dest, weight):
    with ExitStack() as ctx:
        def sb(name, shape, dt=F32):
            return ctx.enter_context(nc.sbuf_tensor(f"r_{name}", shape, dt))
        wg = sb("wg", [P, DC, E1])
        before, ones, first_slot = sb("before", [P, P]), sb("ones", [P, P]), sb("first_slot", [P, E1])
        tokens = sb("tokens", [P, NT])
        zero = sb("zero", [1, D])
        sc, hot, mask, places = sb("sc", [P, NT, E1]), sb("hot", [P, K1, NT, E1]), sb("mask", [P, NT, E1]), sb("places", [P, NT, E1])
        tmp = sb("tmp", [P, NT, E1])
        col, gm, keep, kept = sb("col", [P, NT]), sb("gm", [P, NT, G1]), sb("keep", [P, NT, G1]), sb("kept", [P, KG, NT, G1])
        top, idx, idf = sb("top", [P, NT, 8]), sb("idx", [P, NT, 8], U32), sb("idf", [P, NT, 8])
        carry = sb("carry", [P, NT, E1])
        destf = sb("destf", [P, K1, NT])
        sw = [sb(f"sw{j}", [P, DC, D]) for j in range(3)]
        gate = [sb(f"gate{i}", [P, NB]) for i in range(2)]
        hid = sb("hid", [P, DC, NB])
        psl = ctx.enter_context(nc.psum_tensor("r_psl", [P, NT, E1], F32))
        pst = ctx.enter_context(nc.psum_tensor("r_pst", [P, NT, E1], F32))
        ps1 = [ctx.enter_context(nc.psum_tensor(f"r_ps1_{i}", [P, NB], F32)) for i in range(2)]
        ps3 = [ctx.enter_context(nc.psum_tensor(f"r_ps3_{i}", [P, NB], F32)) for i in range(2)]
        pso = [ctx.enter_context(nc.psum_tensor(f"r_pso{i}", [P, NB], F32)) for i in range(2)]
        s = lambda name: nc.alloc_semaphore(f"r_{name}")
        small_in, sw_in, stored, filled, scattered = s("small_in"), s("sw_in"), s("stored"), s("filled"), s("scattered")
        logits, expd, chain, counted, zeroed = s("logits"), s("expd"), s("chain"), s("counted"), s("zeroed")
        h_ready, gated, h_done, o_ready, o_free = s("h_ready"), s("gated"), s("h_done"), s("o_ready"), s("o_free")
        TPB = NB // P
        BLOCKS = N // NB
        with nc.Block() as block:

            @block.sync
            def _(sp):
                sp.dma_start(wg[:, :, :], dram["wg_t"].rearrange("(k p) e -> p k e", p=P)).then_inc(small_in, 16)
                for t, n in ((before, "c_before"), (ones, "c_ones"), (first_slot, "c_first_slot"), (tokens, "c_tokens")):
                    sp.dma_start(t[:, :], dram[n]).then_inc(small_in, 16)
                for j, n in enumerate(("sw1", "sw3", "sw2")):
                    sp.dma_start(sw[j][:, :, :], dram[n].rearrange("(k p) f -> p k f", p=P)).then_inc(sw_in, 16)
                sp.dma_start(slot_tokens, dram["c_no_token"]).then_inc(filled, 16)
                sp.dma_start(xp[0:N, :].rearrange("(t p) d -> p t d", p=P), rows[:, :, :]).then_inc(stored, 16)
                sp.wait_ge(zeroed, 1)
                sp.dma_start(xp[N:N + 1, :], zero[:, :]).then_inc(stored, 16)
                sp.dma_start(oe[SLOTS:SLOTS + 1, :], zero[:, :]).then_inc(stored, 16)
                sp.wait_ge(stored, 48)

            @block.gpsimd
            def _(pool):
                pool.memset(zero[:, :], 0.0).then_inc(zeroed, 1)
                pool.wait_ge(filled, 16)
                pool.wait_ge(small_in, 80)
                pool.wait_ge(chain, DEST_AT)
                for k in range(K1):
                    for t in range(NT):
                        pool.indirect_dma_start(out=slot_tokens, out_offset=bass.IndirectOffsetOnAxis(ap=dest[:, k, t:t + 1], axis=0),
                                                in_=tokens[:, t:t + 1], in_offset=None, bounds_check=SLOTS - 1,
                                                oob_is_err=False).then_inc(scattered, 16)
                pool.wait_ge(scattered, 16 * K1 * NT)

            @block.tensor
            def _(pe):
                pe.wait_ge(small_in, 80)
                for t in range(NT):
                    for k in range(DC):
                        mm = pe.matmul(psl[:, t, :], xt[:, k, t * P:(t + 1) * P], wg[:, k, :], start=(k == 0), stop=(k == DC - 1))
                mm.then_inc(logits, 1)

                def hidden(q):
                    for f in range(DC):
                        m = q * DC + f
                        if m >= 2:
                            pe.wait_ge(h_done, m - 1)
                        for j, ps in enumerate((ps1, ps3)):
                            for k in range(DC):
                                mm = pe.matmul(ps[m % 2][:, :], sw[j][:, k, f * P:(f + 1) * P], xt[:, k, q * NB:(q + 1) * NB],
                                               start=(k == 0), stop=(k == DC - 1))
                        mm.then_inc(h_ready, 1)

                def outs(q):
                    pe.wait_ge(h_done, (q + 1) * DC)
                    for t in range(TPB):
                        pe.wait_ge(o_free, q * TPB + t + 1)
                        for f in range(DC):
                            mm = pe.matmul(pso[t % 2][:, :], hid[:, f, t * P:(t + 1) * P], sw[2][:, f, :], start=(f == 0), stop=(f == DC - 1))
                        mm.then_inc(o_ready, 1)

                pe.wait_ge(chain, MASK_AT)
                flat = mask[:, :, :].rearrange("p t e -> p (t e)")
                pe.matmul(psl[:, :, :].rearrange("p t e -> p (t e)"), before[:, :], flat, start=True, stop=True)
                pe.matmul(pst[:, :, :].rearrange("p t e -> p (t e)"), ones[:, :], flat, start=True, stop=True).then_inc(counted, 1)
                pe.wait_ge(sw_in, 48)
                for q in range(BLOCKS):
                    hidden(q)
                    outs(q)

            @block.scalar
            def _(act):
                act.wait_ge(chain, 2)
                act.activation(sc[:, :, :], sc[:, :, :], ACT.Exp).then_inc(expd, 1)
                for m in range(BLOCKS * DC):
                    act.wait_ge(h_ready, m + 1)
                    if m >= 2:
                        act.wait_ge(h_done, m - 1)
                    act.activation(gate[m % 2][:, :], ps1[m % 2][:, :], ACT.Silu).then_inc(gated, 1)

            @block.vector
            def _(dve):
                dve.sem_inc(o_free, 2)
                n = [0]

                def link(ins):
                    n[0] += 1
                    ins.then_inc(chain, 1)
                    dve.wait_ge(chain, n[0])

                def over(ap, e):
                    return ap.unsqueeze(2).broadcast_to([P, NT, e])

                def one_hot(out, e, column):
                    link(dve.tensor_tensor(out, c.iota[:, 0:e].unsqueeze(1).broadcast_to([P, NT, e]), over(column, e), ALU.is_equal))

                def top8(values):
                    for t in range(NT):
                        ins = dve.max(top[:, t, :], values[:, t, :])
                    link(ins)
                    for t in range(NT):
                        ins = dve.max_index(idx[:, t, :], top[:, t, :], values[:, t, :])
                    link(ins)
                    link(dve.tensor_copy(idf[:, :, :], idx[:, :, :]))

                dve.wait_ge(small_in, 80)
                dve.wait_ge(logits, 1)
                link(dve.tensor_reduce(col[:, :], psl[:, :, :], AX, ALU.max))
                link(dve.tensor_tensor(sc[:, :, :], psl[:, :, :], over(col[:, :], E1), ALU.subtract))
                dve.wait_ge(expd, 1)
                link(dve.tensor_reduce(col[:, :], sc[:, :, :], AX, ALU.add))
                link(dve.reciprocal(col[:, :], col[:, :]))
                link(dve.tensor_tensor(sc[:, :, :], sc[:, :, :], over(col[:, :], E1), ALU.mult))
                link(dve.tensor_reduce(gm[:, :, :], sc[:, :, :].rearrange("p t (g e) -> p t g e", e=EG), AX, ALU.max))
                top8(gm)
                for k in range(KG):
                    one_hot(kept[:, k, :, :], G1, idf[:, :, k])
                link(dve.tensor_tensor(keep[:, :, :], kept[:, 0, :, :], kept[:, 1, :, :], ALU.add))
                for k in range(2, KG):
                    link(dve.tensor_tensor(keep[:, :, :], keep[:, :, :], kept[:, k, :, :], ALU.add))
                spread = lambda a: a[:, :, :].rearrange("p t g -> p (t g)").unsqueeze(2).broadcast_to([P, NT * G1, EG])
                grouped = lambda a: a[:, :, :].rearrange("p t (g e) -> p (t g) e", e=EG)
                link(dve.tensor_tensor(grouped(tmp), grouped(sc), spread(keep), ALU.mult))
                link(dve.tensor_scalar(keep[:, :, :], keep[:, :, :], -1.0, None, ALU.add))
                link(dve.tensor_tensor(grouped(tmp), grouped(tmp), spread(keep), ALU.add))
                top8(tmp)
                for k in range(K1):
                    one_hot(hot[:, k, :, :], E1, idf[:, :, k])
                link(dve.tensor_tensor(mask[:, :, :], hot[:, 0, :, :], hot[:, 1, :, :], ALU.add))
                for k in range(2, K1):
                    link(dve.tensor_tensor(mask[:, :, :], mask[:, :, :], hot[:, k, :, :], ALU.add))
                assert n[0] == MASK_AT
                link(dve.tensor_reduce(col[:, :], top[:, :, 0:K1], AX, ALU.add))
                link(dve.tensor_scalar(col[:, :], col[:, :], 1e-9, None, ALU.add))
                link(dve.reciprocal(col[:, :], col[:, :]))
                link(dve.tensor_tensor(weight[:, :, :].rearrange("p k t -> p t k"), top[:, :, 0:K1], over(col[:, :], K1), ALU.mult))
                dve.wait_ge(counted, 1)
                link(dve.memset(carry[:, 0, :], 0.0))
                for t in range(1, NT):
                    link(dve.tensor_tensor(carry[:, t, :], pst[:, t - 1, :], carry[:, t - 1, :], ALU.add))
                link(dve.tensor_tensor(places[:, :, :], psl[:, :, :], carry[:, :, :], ALU.add))
                link(dve.tensor_scalar(tmp[:, :, :], places[:, :, :], float(CAP), None, ALU.is_lt))
                slots = first_slot[:, :].unsqueeze(1).broadcast_to([P, NT, E1])
                link(dve.tensor_tensor(places[:, :, :], places[:, :, :], slots, ALU.add))
                link(dve.scalar_tensor_tensor(out=places[:, :, :], in0=places[:, :, :], scalar=-float(SLOTS), in1=tmp[:, :, :], op0=ALU.add, op1=ALU.mult))
                link(dve.tensor_scalar(places[:, :, :], places[:, :, :], float(SLOTS), None, ALU.add))
                for k in range(K1):
                    link(dve.tensor_tensor(hot[:, k, :, :], hot[:, k, :, :], places[:, :, :], ALU.mult))
                    link(dve.tensor_reduce(destf[:, k, :], hot[:, k, :, :], AX, ALU.add))
                link(dve.tensor_copy(dest[:, :, :], destf[:, :, :]))
                assert n[0] == DEST_AT

                for q in range(BLOCKS):
                    for f in range(DC):
                        m = q * DC + f
                        dve.wait_ge(gated, m + 1)
                        if f == 0 and q:
                            dve.wait_ge(o_ready, q * TPB)
                        dve.tensor_tensor(hid[:, f, :], ps3[m % 2][:, :], gate[m % 2][:, :], ALU.mult).then_inc(h_done, 1)
                    for t in range(TPB):
                        dve.wait_ge(o_ready, q * TPB + t + 1)
                        dve.tensor_tensor(c.X[:, q * TPB + t, :], pso[t % 2][:, :], c.X[:, q * TPB + t, :], ALU.add).then_inc(o_free, 1)


MASK_AT = 6 + 3 + KG + (KG - 1) + 3 + 3 + K1 + (K1 - 1)
DEST_AT = MASK_AT + 4 + NT + 5 + 2 * K1 + 1


def experts_block(nc, c, dram, xp, oe, slot_tokens):
    with ExitStack() as ctx:
        def sb(name, shape, dt=F32):
            return ctx.enter_context(nc.sbuf_tensor(f"e_{name}", shape, dt))
        idx = sb("idx", [P, NCT, E1], U32)
        tok = sb("tok", [E1, CAP])
        idn = [sb(f"idn{u}", [P, NCT], U32) for u in range(2)]
        xe = [sb(f"xe{u}", [P, NCT, D]) for u in range(2)]
        xet = [sb(f"xet{u}", [P, DC, CAP]) for u in range(2)]
        w = [[sb(f"w{j}_{u}", [P, DC, D]) for j in range(3)] for u in range(2)]
        gate = [sb(f"gate{i}", [P, CAP]) for i in range(2)]
        hid = [sb(f"hid{u}", [P, DC, CAP]) for u in range(2)]
        res = [sb(f"res{u}", [P, NCT, D]) for u in range(2)]
        pst = [ctx.enter_context(nc.psum_tensor(f"e_pst{i}", [P, DC, P], F32)) for i in range(2)]
        ps1 = [ctx.enter_context(nc.psum_tensor(f"e_ps1_{i}", [P, NB], F32)) for i in range(2)]
        ps3 = [ctx.enter_context(nc.psum_tensor(f"e_ps3_{i}", [P, NB], F32)) for i in range(2)]
        pso = [ctx.enter_context(nc.psum_tensor(f"e_pso{i}", [P, D], F32)) for i in range(2)]
        s = lambda name: nc.alloc_semaphore(f"e_{name}")
        tok_in, tok_turned, idx_ready, idn_ready = s("tok_in"), s("tok_turned"), s("idx_ready"), s("idn_ready")
        w_in = [s("w_in0"), s("w_in1")]
        x_in = [s("x_in0"), s("x_in1")]
        res_out, res_free = [s("res_out0"), s("res_out1")], s("res_free")
        turned, copied = s("turned"), s("copied")
        h_ready, gated, h_done, o_ready, o_done = s("h_ready"), s("gated"), s("h_done"), s("o_ready"), s("o_done")
        HALF = E1 // 2
        with nc.Block() as block:

            @block.sync
            def _(sp):
                sp.dma_start(tok[:, :], slot_tokens.rearrange("(e s) a -> e (s a)", s=CAP)).then_inc(tok_in, 16)

                def load(i, u):
                    for j, name in enumerate(("w1_1", "w3_1", "w2_1")):
                        src = dram[name][bass.ds((2 * i + u) * D, D), :].rearrange("(k p) f -> p k f", p=P)
                        sp.dma_start(w[u][j][:, :, :], src).then_inc(w_in[u], 16)

                def store(i, u):
                    sp.wait_ge(o_done, 2 + (2 * i + u + 1) * NCT)
                    at = (2 * i + u) * CAP
                    whole = CAP // P
                    sp.dma_start(oe[bass.ds(at, whole * P), :].rearrange("(j p) d -> p j d", p=P), res[u][:, 0:whole, :]).then_inc(res_out[u], 16)
                    sp.dma_start(oe[bass.ds(at + whole * P, CAP - whole * P), :], res[u][0:CT[-1], whole, :]).then_inc(res_out[u], 16)
                    sp.wait_ge(res_out[u], 32 * i + 32)
                    sp.sem_inc(res_free, 1)

                sp.sem_inc(res_free, 2)
                load(0, 0)
                load(0, 1)
                with sp.Fori(0, HALF - 1) as i:
                    for u in range(2):
                        sp.wait_ge(o_ready, (2 * i + u + 1) * NCT)
                        load(i + 1, u)
                        store(i, u)
                for u in range(2):
                    store(HALF - 1, u)

            @block.gpsimd
            def _(pool):
                pool.wait_ge(idx_ready, NCT)

                def gather(i, u):
                    e = 2 * i + u
                    for j, r in enumerate(CT):
                        pool.tensor_copy(idn[u][0:r, j:j + 1], idx[0:r, j, bass.ds(e, 1)]).then_inc(idn_ready, 1)
                    for j, r in enumerate(CT):
                        pool.wait_ge(idx_ready, NCT)
                        pool.wait_ge(idn_ready, e * NCT + j + 1)
                        pool.sem_inc(c.passed, 1)
                        pool.indirect_dma_start(out=xe[u][0:r, j, :], out_offset=None, in_=xp,
                                                in_offset=bass.IndirectOffsetOnAxis(ap=idn[u][0:r, j:j + 1], axis=0)).then_inc(x_in[u], 16)

                gather(0, 0)
                gather(0, 1)
                with pool.Fori(0, HALF - 1) as i:
                    for u in range(2):
                        pool.wait_ge(turned, (2 * i + u + 1) * NCT)
                        gather(i + 1, u)

            @block.tensor
            def _(pe):
                pe.wait_ge(tok_in, 16)
                for j, r in enumerate(CT):
                    mm = pe.transpose(ps1[0][0:r, j * P:j * P + E1], tok[:, j * P:j * P + r], c.ident[0:E1, 0:E1])
                mm.then_inc(tok_turned, 1)
                with pe.Fori(0, HALF) as i:
                    for u in range(2):
                        for j, r in enumerate(CT):
                            pe.wait_ge(tok_in, 16)
                            if j == 0:
                                pe.wait_ge(x_in[u], 16 * NCT * i + 16 * NCT)
                            pe.wait_ge(copied, (2 * i + u) * NCT + j + 1)
                            pe.sem_inc(c.passed, 1)
                            for k in range(DC):
                                mm = pe.transpose(pst[(u * NCT + j) % 2][:, k, 0:r], xe[u][0:r, j, k * P:(k + 1) * P], c.ident[0:r, 0:r])
                            mm.then_inc(turned, 1)
                    for u in range(2):
                        pe.wait_ge(w_in[u], 48 * i + 48)
                        pe.wait_ge(copied, 2 + (2 * i + u + 1) * NCT)
                        for f in range(DC):
                            pe.wait_ge(h_done, (2 * i + u) * DC + f + 1)
                            for j, ps in enumerate((ps1, ps3)):
                                for k in range(DC):
                                    mm = pe.matmul(ps[f % 2][:, 0:CAP], w[u][j][:, k, f * P:(f + 1) * P], xet[u][:, k, :],
                                                   start=(k == 0), stop=(k == DC - 1))
                            mm.then_inc(h_ready, 1)
                    for u in range(2):
                        pe.wait_ge(h_done, 2 + (2 * i + u + 1) * DC)
                        for j, r in enumerate(CT):
                            pe.wait_ge(o_done, (2 * i + u) * NCT + j + 1)
                            for f in range(DC):
                                mm = pe.matmul(pso[(u * NCT + j) % 2][0:r, :], hid[u][:, f, j * P:j * P + r], w[u][2][:, f, :],
                                               start=(f == 0), stop=(f == DC - 1))
                            mm.then_inc(o_ready, 1)

            @block.scalar
            def _(act):
                act.sem_inc(copied, 2)
                with act.Fori(0, HALF) as i:
                    for u in range(2):
                        for j, r in enumerate(CT):
                            act.wait_ge(turned, (2 * i + u) * NCT + j + 1)
                            act.activation(xet[u][:, :, j * P:j * P + r], pst[(u * NCT + j) % 2][:, :, 0:r], ACT.Copy).then_inc(copied, 1)
                    for u in range(2):
                        for f in range(DC):
                            act.wait_ge(h_ready, (2 * i + u) * DC + f + 1)
                            act.activation(gate[f % 2][:, :], ps1[f % 2][:, 0:CAP], ACT.Silu).then_inc(gated, 1)

            @block.vector
            def _(dve):
                dve.wait_ge(tok_turned, 1)
                for j, r in enumerate(CT):
                    dve.tensor_copy(idx[0:r, j, :], ps1[0][0:r, j * P:j * P + E1]).then_inc(idx_ready, 1)
                dve.wait_ge(idx_ready, NCT)
                dve.sem_inc(h_done, 2)
                dve.sem_inc(o_done, 2)
                with dve.Fori(0, HALF) as i:
                    for u in range(2):
                        for f in range(DC):
                            dve.wait_ge(gated, (2 * i + u) * DC + f + 1)
                            dve.tensor_tensor(hid[u][:, f, :], ps3[f % 2][:, 0:CAP], gate[f % 2][:, :], ALU.mult).then_inc(h_done, 1)
                    for u in range(2):
                        dve.wait_ge(res_free, 2 * i + u + 1)
                        for j, r in enumerate(CT):
                            dve.wait_ge(o_ready, (2 * i + u) * NCT + j + 1)
                            dve.tensor_copy(res[u][0:r, j, :], pso[(u * NCT + j) % 2][0:r, :]).then_inc(o_done, 1)


def combine_block(nc, c, oe, dest, weight, out):
    RING = 8
    with ExitStack() as ctx:
        got = [ctx.enter_context(nc.sbuf_tensor(f"c_got{i}", [P, D], F32)) for i in range(RING)]
        got_in = [nc.alloc_semaphore(f"c_got_in{i}") for i in range(RING)]
        added, stored = nc.alloc_semaphore("c_added"), nc.alloc_semaphore("c_stored")
        with nc.Block() as block:

            @block.gpsimd
            def _(pool):
                for m in range(NT * K1):
                    t, k = m // K1, m % K1
                    if m >= RING:
                        pool.wait_ge(added, m - RING + 1)
                    pool.indirect_dma_start(out=got[m % RING][:, :], out_offset=None, in_=oe,
                                            in_offset=bass.IndirectOffsetOnAxis(ap=dest[:, k, t:t + 1], axis=0)).then_inc(got_in[m % RING], 16)

            @block.vector
            def _(dve):
                for m in range(NT * K1):
                    t, k = m // K1, m % K1
                    dve.wait_ge(got_in[m % RING], 16 * (m // RING + 1))
                    if k:
                        dve.wait_ge(added, m)
                    dve.scalar_tensor_tensor(out=c.X[:, t, :], in0=got[m % RING][:, :], scalar=weight[:, k, t:t + 1],
                                             in1=c.X[:, t, :], op0=ALU.mult, op1=ALU.add).then_inc(added, 1)

            @block.sync
            def _(sp):
                for t in range(NT):
                    sp.wait_ge(added, K1 * (t + 1))
                    sp.dma_start(out[t * P:(t + 1) * P, :], c.X[:, t, :]).then_inc(stored, 16)
                sp.wait_ge(stored, 16 * NT)


def moe1_stage(nc, c, dram, out):
    xp = nc.dram_tensor("m1_xp", [N + 1, D], F32).ap()
    oe = nc.dram_tensor("m1_oe", [SLOTS + 1, D], F32).ap()
    slot_tokens = nc.dram_tensor("m1_slot_tokens", [SLOTS, 1], F32).ap()
    with ExitStack() as st:
        dest = st.enter_context(nc.sbuf_tensor("m1_dest", [P, K1, NT], U32))
        weight = st.enter_context(nc.sbuf_tensor("m1_weight", [P, K1, NT], F32))
        with ExitStack() as pre:
            rows = pre.enter_context(nc.sbuf_tensor("m1_rows", [P, NT, D], F32))
            xt = pre.enter_context(nc.sbuf_tensor("m1_xt", [P, DC, N], F32))
            layernorm_block(nc, c, "3", xt, rows)
            route_block(nc, c, rows, xt, dram, xp, oe, slot_tokens, dest, weight)
        experts_block(nc, c, dram, xp, oe, slot_tokens)
        combine_block(nc, c, oe, dest, weight, out)


class Shared:
    pass


def build(nc, dram, out):
    c = Shared()
    with ExitStack() as ctx:
        def sb(name, shape, dt=F32):
            return ctx.enter_context(nc.sbuf_tensor(name, shape, dt))
        c.X = sb("X", [P, NT, D])
        c.ident = sb("ident", [P, P])
        c.iota = sb("iota", [P, E1])
        c.passed = nc.alloc_semaphore("passed")
        load_block(nc, c, dram["x"], [(c.ident, dram["c_ident"]), (c.iota, dram["c_iota"])])
        with ExitStack() as st:
            xn = st.enter_context(nc.sbuf_tensor("g0_xn", [P, NT, D], F32))
            y = st.enter_context(nc.sbuf_tensor("g0_y", [P, NT, D], F32))
            dinv = st.enter_context(nc.sbuf_tensor("g0_dinv", [P, NT], F32))
            layernorm_block(nc, c, "0", None, xn)
            degree_block(nc, c, dram["adj"], dram["adj_t"], xn, dinv)
            mix_block(nc, c, dram["adj"], dram["adj_t"], xn, y, dinv)
            mix_block(nc, c, dram["adj"], dram["adj_t"], None, y, dinv)
        with ExitStack() as st:
            xt = st.enter_context(nc.sbuf_tensor("m0_xt", [P, DC, N], F32))
            layernorm_block(nc, c, "1", xt)
            moe0_block(nc, c, xt, dram["L0_ffn_router_w"], dram["L0_ffn_router_b"], dram["w1_0"],
                       dram["b1_0"], dram["w2_0"], dram["L0_ffn_b2"])
        attention_stage(nc, c, dram)
        moe1_stage(nc, c, dram, out)


def layouts(np, inp):
    a = {k: np.ascontiguousarray(inp[k]) for k in ("x", "adj", "L0_ffn_router_w", "L0_ffn_router_b", "L0_ffn_b2")}
    a["adj_t"] = np.ascontiguousarray(inp["adj"].T)
    a["w1_0"] = np.ascontiguousarray(inp["L0_ffn_W1"]).reshape(E0 * D, F0)
    a["w2_0"] = np.ascontiguousarray(inp["L0_ffn_W2"]).reshape(E0 * F0, D)
    a["b1_0"] = np.ascontiguousarray(inp["L0_ffn_b1"].reshape(E0 * HC0, P).T)
    a["c_ident"] = np.eye(P, dtype=np.float32)
    a["c_iota"] = np.tile(np.arange(E1, dtype=np.float32), (P, 1))
    a["w_heads"] = np.ascontiguousarray(inp["L1_gnn_W"].transpose(1, 0, 2)).reshape(D, HEADS * HID)
    a["a_rows"] = np.stack([inp["L1_gnn_a1"].reshape(-1), inp["L1_gnn_a2"].reshape(-1)])
    for j in range(4):
        a[f"enc_w{j}"] = np.ascontiguousarray(inp[f"L1_gnn_W{j + 1}"].T)
        b = inp[f"L1_gnn_b{j + 1}"]
        a[f"enc_b{j}"] = np.ascontiguousarray(b.reshape(-1, P).T) if j < 3 else np.ascontiguousarray(b)
    a["wg_t"] = np.ascontiguousarray(inp["L1_ffn_wg"].T)
    for j in (1, 2, 3):
        a[f"w{j}_1"] = np.ascontiguousarray(inp[f"L1_ffn_w{j}"]).reshape(E1 * D, D)
        a[f"sw{j}"] = np.ascontiguousarray(inp[f"L1_ffn_sw{j}"])
    a["c_before"] = np.triu(np.ones((P, P), np.float32), 1)
    a["c_ones"] = np.ones((P, P), np.float32)
    a["c_first_slot"] = np.tile(np.arange(E1, dtype=np.float32) * CAP, (P, 1))
    a["c_tokens"] = (np.arange(NT) * P + np.arange(P)[:, None]).astype(np.float32)
    a["c_no_token"] = np.full((SLOTS, 1), N, np.float32)
    return a


def kernel(**inputs):
    import numpy as _np
    import concourse.bacc as _bacc
    from concourse import mybir as _mybir
    from concourse.bass_utils import run_bass_kernel_spmd as _run

    nc = _bacc.Bacc("TRN2", target_bir_lowering=False, num_devices=1)
    arrays = {f"in_{k}": v for k, v in layouts(_np, {k: _np.asarray(v) for k, v in inputs.items()}).items()}
    dram = {k[3:]: nc.dram_tensor(k, v.shape, _mybir.dt.from_np(v.dtype), kind="ExternalInput").ap() for k, v in arrays.items()}
    out = nc.dram_tensor("out_dram", (N, D), _mybir.dt.float32, kind="ExternalOutput").ap()
    build(nc, dram, out)
    return _run(nc, [arrays], core_ids=[0]).results[0]["out_dram"]
```

```python
from contextlib import ExitStack

import numpy as np

import concourse.bass as bass
from concourse import mybir

ALU = mybir.AluOpType
ACT = mybir.ActivationFunctionType
AX = mybir.AxisListType.X
F32 = mybir.dt.float32
F32R = mybir.dt.float32r
BF16 = mybir.dt.bfloat16
U32 = mybir.dt.uint32
I32 = mybir.dt.int32

P = 128
N, D = 2048, 512
NT = N // P
DC = D // P
NB = 512
EPS = 1e-5

E0, F0 = 8, 256
HC0 = F0 // P
HEADS, HID = 8, 64
HP = HEADS // 2
ALPHA = 0.2
BIG = float(2**53)
NW = 1024
M1, M2, M3 = 256, 128, 256
E1, K1, G1, KG = 32, 4, 8, 4
EG = E1 // G1
CAP = int(1.25 * N * K1 / E1)
SLOTS = E1 * CAP
CT = [min(P, CAP - j) for j in range(0, CAP, P)]
NCT = len(CT)


PASSES = ((0, 0), (0, 1), (1, 0))


def product(pe, out, left, right, first, last):
    for n, (a, b) in enumerate(PASSES):
        mm = pe.matmul(out, left(a), right(b), start=first and n == 0, stop=last and n == len(PASSES) - 1)
    return mm


def split_tile(ctx, nc, name, shape):
    return [ctx.enter_context(nc.sbuf_tensor(f"{name}_{part}", shape, F32R)) for part in ("high", "low")]


def layernorm_block(nc, c, tag, turned_to, rows=None, store=None):
    with ExitStack() as ctx:
        stats = ctx.enter_context(nc.sbuf_tensor(f"ln_stats{tag}", [P, NT, 6], F32))
        mv = ctx.enter_context(nc.sbuf_tensor(f"ln_mv{tag}", [P, NT, 2], F32))
        std = ctx.enter_context(nc.sbuf_tensor(f"ln_std{tag}", [P, NT], F32))
        rstd = ctx.enter_context(nc.sbuf_tensor(f"ln_rstd{tag}", [P, NT], F32))
        if rows is None:
            rows = ctx.enter_context(nc.sbuf_tensor(f"ln_rows{tag}", [P, NT, D], F32))
        banks = [ctx.enter_context(nc.psum_tensor(f"ln_ps{tag}{i}", [P, DC, P], F32)) for i in range(4)]
        stats_ready = c.semaphore(f"ln_stats_ready{tag}")
        var_ready = c.semaphore(f"ln_var_ready{tag}")
        std_ready = c.semaphore(f"ln_std_ready{tag}")
        rstd_ready = c.semaphore(f"ln_rstd_ready{tag}")
        rows_ready = c.semaphore(f"ln_rows_ready{tag}")
        if turned_to is not None:
            turned = c.semaphore(f"ln_turned{tag}")
            high_ready = c.semaphore(f"ln_high_ready{tag}")
            bank_free = c.semaphore(f"ln_bank_free{tag}")
        if store is not None:
            zero = ctx.enter_context(nc.sbuf_tensor(f"ln_zero{tag}", [1, D], F32))
            stored = c.semaphore(f"ln_stored{tag}")
            zeroed = c.semaphore(f"ln_zeroed{tag}")
        X = c.X
        with nc.Block() as block:

            @block.vector
            def _(dve):
                for t in range(NT):
                    dve.bn_stats(stats[:, t, :], X[:, t, :]).then_inc(stats_ready, 1)
                for t in range(NT):
                    dve.wait_ge(stats_ready, t + 1)
                    dve.bn_aggr(mv[:, t, :], stats[:, t, :]).then_inc(var_ready, 1)
                dve.wait_ge(var_ready, NT)
                dve.tensor_scalar(std[:, :], mv[:, :, 1], EPS, None, ALU.add).then_inc(var_ready, 1)
                dve.wait_ge(std_ready, 1)
                dve.reciprocal(rstd[:, :], std[:, :]).then_inc(rstd_ready, 1)
                dve.wait_ge(rstd_ready, 1)

                def low(t):
                    dve.wait_ge(high_ready, t + 1)
                    at = slice(t * P, (t + 1) * P)
                    dve.tensor_tensor(turned_to[1][:, :, at], banks[t % 4][:, :, :], turned_to[0][:, :, at].bitcast(F32),
                                      ALU.subtract).then_inc(bank_free, 1)

                for t in range(NT):
                    dve.tensor_scalar(rows[:, t, :], X[:, t, :], mv[:, t, 0:1], rstd[:, t:t + 1],
                                      ALU.subtract, ALU.mult).then_inc(rows_ready, 1)
                    if turned_to is not None and t >= 3:
                        low(t - 3)
                if turned_to is not None:
                    for t in range(NT - 3, NT):
                        low(t)

            @block.scalar
            def _(act):
                act.wait_ge(var_ready, NT + 1)
                act.activation(std[:, :], std[:, :], ACT.Sqrt).then_inc(std_ready, 1)
                if turned_to is None:
                    return
                for t in range(NT):
                    act.wait_ge(turned, t + 1)
                    act.activation(turned_to[0][:, :, t * P:(t + 1) * P], banks[t % 4][:, :, :],
                                   ACT.Copy).then_inc(high_ready, 1)

            @block.tensor
            def _(pe):
                if turned_to is None:
                    return
                for t in range(NT):
                    pe.wait_ge(rows_ready, t + 1)
                    if t >= 4:
                        pe.wait_ge(bank_free, t - 3)
                    for k in range(DC):
                        mm = pe.transpose(banks[t % 4][:, k, :], rows[:, t, k * P:(k + 1) * P], c.ident[:, :])
                    mm.then_inc(turned, 1)

            @block.sync
            def _(sp):
                if store is None:
                    return
                for q in range(4):
                    a, b = q * NT // 4, (q + 1) * NT // 4
                    sp.wait_ge(rows_ready, b)
                    sp.dma_start(store[a * P:b * P, :].rearrange("(t p) d -> p t d", p=P), rows[:, a:b, :]).then_inc(stored, 16)
                sp.wait_ge(zeroed, 1)
                sp.dma_start(store[N:N + 1, :], zero[:, :]).then_inc(stored, 16)
                sp.wait_ge(stored, 80)

            @block.gpsimd
            def _(pool):
                if store is not None:
                    pool.memset(zero[:, :], 0.0).then_inc(zeroed, 1)


def load_block(nc, c, x, consts):
    arrived = c.semaphore("start_arrived")
    with nc.Block() as block:

        @block.sync
        def _(sp):
            sp.dma_start(c.X[:, :, :], x.rearrange("(t p) d -> p t d", p=P)).then_inc(arrived, 16)
            for sb, dram in consts:
                sp.dma_start(sb[:, :], dram).then_inc(arrived, 16)
            sp.wait_ge(arrived, 16 * (1 + len(consts)))


def degree_block(nc, c, adj, xn, dinv):
    RING = 3
    with ExitStack() as ctx:
        a = [ctx.enter_context(nc.sbuf_tensor(f"deg_a{i}", [P, N], F32)) for i in range(RING)]
        ones = ctx.enter_context(nc.sbuf_tensor("deg_ones", [P, 1], F32))
        rows = ctx.enter_context(nc.sbuf_tensor("deg_rows", [P, NT], F32))
        column_row = ctx.enter_context(nc.sbuf_tensor("deg_column_row", [1, N], F32))
        small = ctx.enter_context(nc.sbuf_tensor("deg_small", [P, 5, NT], F32))
        ps = [ctx.enter_context(nc.psum_tensor(f"deg_ps{i}", [1, NB], F32)) for i in range(N // NB)]
        columns = ctx.enter_context(nc.psum_tensor("deg_columns", [P, NT], F32))
        arrived = [c.semaphore(f"deg_arrived{i}") for i in range(RING)]
        summed, columned, row_ready, turned = (c.semaphore(f"deg_{n}") for n in ("summed", "columned", "row_ready", "turned"))
        ready, chain, root = (c.semaphore(f"deg_{n}") for n in ("ready", "chain", "root"))
        with nc.Block() as block:

            @block.sync
            def _(sp):
                for t in range(NT):
                    if t >= RING:
                        sp.wait_ge(summed, t - RING + 1)
                        sp.wait_ge(columned, t - RING + 1)
                    sp.dma_start(a[t % RING][:, :], adj[t * P:(t + 1) * P, :]).then_inc(arrived[t % RING], 16)

            @block.tensor
            def _(pe):
                pe.wait_ge(ready, 1)
                for t in range(NT):
                    pe.wait_ge(arrived[t % RING], 16 * (t // RING + 1))
                    for j in range(N // NB):
                        mm = pe.matmul(ps[j][:, :], ones[:, :], a[t % RING][:, j * NB:(j + 1) * NB], start=(t == 0), stop=(t == NT - 1))
                    mm.then_inc(columned, 1)
                pe.wait_ge(row_ready, 1)
                for j in range(NT):
                    mm = pe.matmul(columns[:, j:j + 1], column_row[:, j * P:(j + 1) * P], ones[0:1, :], start=True, stop=True)
                mm.then_inc(turned, 1)

            @block.scalar
            def _(act):
                act.wait_ge(columned, NT)
                for j in range(N // NB):
                    ins = act.activation(column_row[:, j * NB:(j + 1) * NB], ps[j][:, :], ACT.Copy)
                ins.then_inc(row_ready, 1)
                act.wait_ge(chain, 3)
                act.activation(small[:, 2, :], small[:, 1, :], ACT.Sqrt).then_inc(root, 1)

            @block.vector
            def _(dve):
                dve.memset(ones[:, :], 1.0).then_inc(ready, 1)
                for t in range(NT):
                    dve.wait_ge(arrived[t % RING], 16 * (t // RING + 1))
                    dve.tensor_reduce(rows[:, t:t + 1], a[t % RING][:, :], AX, ALU.add).then_inc(summed, 1)
                dve.wait_ge(summed, NT)
                dve.wait_ge(turned, 1)
                deg, safe, rt, inv, above = (small[:, k, :] for k in range(5))
                dve.tensor_tensor(deg, columns[:, :], rows[:, :], ALU.add).then_inc(chain, 1)
                dve.wait_ge(chain, 1)
                dve.tensor_scalar(deg, deg, 0.5, 1.0, ALU.mult, ALU.add).then_inc(chain, 1)
                dve.wait_ge(chain, 2)
                dve.tensor_scalar(safe, deg, 1e-30, None, ALU.max).then_inc(chain, 1)
                dve.tensor_scalar(above, deg, 0.0, None, ALU.is_gt).then_inc(chain, 1)
                dve.wait_ge(root, 1)
                dve.reciprocal(inv, rt).then_inc(chain, 1)
                dve.wait_ge(chain, 5)
                dve.tensor_tensor(dinv[:, :], inv, above, ALU.mult).then_inc(chain, 1)
                dve.wait_ge(chain, 6)
                for t in range(NT):
                    dve.tensor_scalar(xn[:, t, :], xn[:, t, :], dinv[:, t:t + 1], None,
                                      ALU.mult).then_inc(chain, 1)


def mix_block(nc, c, adj, adj_t, z, y, dinv):
    first = z is not None
    tag = "s" if first else "a"
    src = z if first else y
    with ExitStack() as ctx:
        pa = [ctx.enter_context(nc.sbuf_tensor(f"mix_{tag}_pa{i}", [P, NT, P], F32)) for i in range(2)]
        pb = [ctx.enter_context(nc.sbuf_tensor(f"mix_{tag}_pb{i}", [P, NT, P], F32)) for i in range(2)] if first else None
        half = [ctx.enter_context(nc.sbuf_tensor(f"mix_{tag}_half{i}", [P, D], F32)) for i in range(2)] if first else None
        ps = [ctx.enter_context(nc.psum_tensor(f"mix_{tag}_ps{i}", [P, D], F32)) for i in range(2)]
        arrived = [c.semaphore(f"mix_{tag}_arrived{i}") for i in range(2)]
        panel_ready = c.semaphore(f"mix_{tag}_panel_ready")
        product = c.semaphore(f"mix_{tag}_product")
        bank_free = c.semaphore(f"mix_{tag}_bank_free")
        halved = c.semaphore(f"mix_{tag}_halved")
        half_free = c.semaphore(f"mix_{tag}_half_free")
        a_v = adj.rearrange("(k p) m -> p k m", p=P)
        at_v = adj_t.rearrange("(k p) m -> p k m", p=P)
        with nc.Block() as block:

            @block.sync
            def _(sp):
                def load(i, s):
                    cols = bass.ds((2 * i + s) * P, P)
                    sp.dma_start(pa[s][:, :, :], at_v[:, :, cols]).then_inc(arrived[s], 16)
                    if first:
                        sp.dma_start(pb[s][:, :, :], a_v[:, :, cols]).then_inc(arrived[s], 16)

                load(0, 0)
                load(0, 1)
                with sp.Fori(0, NT // 2 - 1) as i:
                    for s in range(2):
                        sp.wait_ge(product, 2 * i + s + 1)
                        load(i + 1, s)

            @block.vector
            def _(dve):
                dve.sem_inc(bank_free, 2)

                def panel(i, s):
                    dve.wait_ge(arrived[s], 32 * i + 32)
                    dve.tensor_tensor(pa[s][:, :, :], pa[s][:, :, :], pb[s][:, :, :],
                                      ALU.add).then_inc(panel_ready, 1)

                def finish(i, s):
                    dve.wait_ge(product, 2 * i + s + 1)
                    t = 2 * i + s
                    if first:
                        dve.wait_ge(half_free, 2 * i + s + 1)
                        dve.scalar_tensor_tensor(out=half[s][:, :], in0=ps[s][:, :], scalar=0.5, in1=z[:, t, :],
                                                 op0=ALU.mult, op1=ALU.add).then_inc(halved, 1)
                    else:
                        dve.tensor_tensor(c.X[:, t, :], ps[s][:, :], c.X[:, t, :], ALU.add).then_inc(bank_free, 1)

                if first:
                    panel(0, 0)
                    panel(0, 1)
                    with dve.Fori(0, NT // 2 - 1) as i:
                        for s in range(2):
                            finish(i, s)
                            panel(i + 1, s)
                    for s in range(2):
                        finish(NT // 2 - 1, s)
                else:
                    with dve.Fori(0, NT // 2) as i:
                        for s in range(2):
                            finish(i, s)

            @block.scalar
            def _(act):
                if not first:
                    return
                act.sem_inc(half_free, 2)
                with act.Fori(0, NT // 2) as i:
                    for s in range(2):
                        act.wait_ge(arrived[s], 32)
                        act.wait_ge(halved, 2 * i + s + 1)
                        act.sem_inc(c.passed, 1)
                        act.activation(y[:, 2 * i + s, :], half[s][:, :], ACT.Copy,
                                       scale=dinv[:, bass.ds(2 * i + s, 1)]).then_inc(half_free, 1)

            @block.tensor
            def _(pe):
                with pe.Fori(0, NT // 2) as i:
                    for s in range(2):
                        if first:
                            pe.wait_ge(panel_ready, 2 * i + s + 1)
                            pe.wait_ge(half_free, 2 * i + s + 1)
                        else:
                            pe.wait_ge(arrived[s], 16 * i + 16)
                            pe.wait_ge(bank_free, 2 * i + s + 1)
                        for k in range(NT):
                            mm = pe.matmul(ps[s][:, :], pa[s][:, k, :], src[:, k, :],
                                           start=(k == 0), stop=(k == NT - 1))
                        mm.then_inc(product, 1)


def moe0_block(nc, c, xt, router_w, router_b, w1, b1, w2, b2):
    with ExitStack() as ctx:
        def sb(name, shape, dt=F32):
            return ctx.enter_context(nc.sbuf_tensor(f"m0_{name}", shape, dt))
        rw = sb("rw", [P, DC, E0])
        rb = sb("rb", [P, E0])
        b1s = sb("b1", [P, E0 * HC0])
        b2s = sb("b2", [E0, D])
        rws = split_tile(ctx, nc, "m0_rws", [P, DC, E0])
        raw = [sb("raw_w1", [P, DC, F0]), sb("raw_w2", [P, HC0, D])]
        w1s = [split_tile(ctx, nc, f"m0_w1_{i}", [P, DC, F0]) for i in range(2)]
        w2s = [split_tile(ctx, nc, f"m0_w2_{i}", [P, HC0, D]) for i in range(2)]
        act_out = [sb(f"act_out{i}", [P, HC0, NB]) for i in range(2)]
        ht = [split_tile(ctx, nc, f"m0_ht{i}", [P, HC0, NB]) for i in range(2)]
        lg = sb("lg", [P, NT, E0])
        ex = sb("ex", [P, NT, E0])
        top = sb("top", [P, NT, 8])
        idx = sb("idx", [P, NT, 8], U32)
        idf = sb("idf", [P, NT, 8])
        sel = sb("sel", [P, NT, E0])
        sel2 = sb("sel2", [P, NT, E0])
        col = sb("col", [P, NT])
        R = sb("R", [P, E0 * NT])
        RT = sb("RT", [E0, N])
        psh = [ctx.enter_context(nc.psum_tensor(f"m0_h{i}", [P, NB], F32)) for i in range(4)]
        pso = [ctx.enter_context(nc.psum_tensor(f"m0_o{i}", [P, NB], F32)) for i in range(4)]
        s = lambda name: c.semaphore(f"m0_{name}")
        small_in, logits, chain, expd = s("small_in"), s("logits"), s("chain"), s("expd")
        turned, rt_ready = s("turned"), s("rt_ready")
        w_in = [s("w_in0"), s("w_in1")]
        h_ready, gelued, hh_ready, h_done, o_ready, o_free = (s(n) for n in ("h_ready", "gelued", "hh_ready", "h_done", "o_ready", "o_free"))
        rh_ready, rl_ready, wh_ready, wl_ready = (s(n) for n in ("rh_ready", "rl_ready", "wh_ready", "wl_ready"))
        NBS = N // NB
        TPB = NB // P
        STEPS = 2 * NBS
        with nc.Block() as block:

            @block.sync
            def _(sp):
                sp.dma_start(rw[:, :, :], router_w.rearrange("(k p) e -> p k e", p=P)).then_inc(small_in, 16)
                sp.dma_start(rb[:, :], router_b.rearrange("(a e) -> a e", a=1).broadcast_to([P, E0])).then_inc(small_in, 16)
                sp.dma_start(b1s[:, :], b1).then_inc(small_in, 16)
                sp.dma_start(b2s[:, :], b2).then_inc(small_in, 16)

                def load(e, j):
                    rows = (D, F0)[j]
                    sp.dma_start(raw[j][:, :, :], (w1, w2)[j][bass.ds(e * rows, rows), :].rearrange("(k p) f -> p k f", p=P)).then_inc(w_in[j], 16)

                load(0, 0)
                load(0, 1)
                with sp.Fori(0, E0 - 1) as e:
                    for j in range(2):
                        sp.wait_ge(wl_ready, 2 * e + j + 1)
                        load(e + 1, j)

            @block.tensor
            def _(pe):
                pe.wait_ge(small_in, 64)
                pe.wait_ge(rl_ready, 1)
                lgp = psh[0][:, 0:NT * E0].rearrange("p (t e) -> p t e", e=E0)
                for t in range(NT):
                    for k in range(DC):
                        mm = product(pe, lgp[:, t, :], lambda a: xt[a][:, k, t * P:(t + 1) * P], lambda b: rws[b][:, k, :],
                                     k == 0, k == DC - 1)
                mm.then_inc(logits, 1)
                pe.wait_ge(chain, 13)
                for t in range(NT):
                    mm = pe.transpose(psh[t // TPB][0:E0, (t % TPB) * P:(t % TPB + 1) * P],
                                      R[:, :].rearrange("p (e t) -> p t e", t=NT)[:, t, :], c.ident[:, :])
                mm.then_inc(turned, 1)
                pe.wait_ge(rt_ready, 1)
                for t in range(NT):
                    pe.wait_ge(o_free, t + 1)
                    pe.matmul(pso[t % 4][:, :], RT[:, t * P:(t + 1) * P], b2s[:, :],
                              start=True, stop=True).then_inc(o_ready, 1)

                def hidden(i, v):
                    u, nb = v // NBS, v % NBS
                    if nb == 0:
                        pe.wait_ge(wl_ready, 2 * (2 * i + u) + 2)
                    for h in range(HC0):
                        pe.wait_ge(gelued, (STEPS * i + v) * HC0 + h + 1)
                        for k in range(DC):
                            mm = product(pe, psh[(v % 2) * HC0 + h][:, :], lambda a: w1s[u][a][:, k, h * P:(h + 1) * P],
                                         lambda b: xt[b][:, k, nb * NB:(nb + 1) * NB], k == 0, k == DC - 1)
                        mm.then_inc(h_ready, 1)

                def outs(i, v):
                    u, nb = v // NBS, v % NBS
                    pe.wait_ge(h_done, (STEPS * i + v + 1) * HC0)
                    for j in range(TPB):
                        pe.wait_ge(o_free, NT + (STEPS * i + v) * TPB + j + 1)
                        for h in range(HC0):
                            mm = product(pe, pso[j][:, :], lambda a: ht[v % 2][a][:, h, j * P:(j + 1) * P],
                                         lambda b: w2s[u][b][:, h, :], h == 0, h == HC0 - 1)
                        mm.then_inc(o_ready, 1)

                with pe.Fori(0, E0 // 2) as i:
                    for v in range(STEPS):
                        hidden(i, v)
                        if v:
                            outs(i, v - 1)
                    outs(i, STEPS - 1)

            @block.scalar
            def _(act):
                act.wait_ge(small_in, 64)
                act.activation(rws[0][:, :, :], rw[:, :, :], ACT.Copy).then_inc(rh_ready, 1)
                act.wait_ge(chain, 3)
                act.activation(ex[:, :, :], lg[:, :, :], ACT.Exp).then_inc(expd, 1)
                act.wait_ge(turned, 1)
                for q in range(4):
                    ins = act.activation(RT[:, q * NB:(q + 1) * NB], psh[q][0:E0, :], ACT.Copy)
                ins.then_inc(rt_ready, 1)
                act.sem_inc(gelued, 2 * HC0)

                def high(i, u, j):
                    act.wait_ge(w_in[j], 16 * (2 * i + u) + 16)
                    act.activation((w1s, w2s)[j][u][0][:, :, :], raw[j][:, :, :], ACT.Copy).then_inc(wh_ready, 1)

                def body(i, last):
                    for v in range(STEPS):
                        g = STEPS * i + v
                        for h in range(HC0):
                            act.wait_ge(small_in, 64)
                            act.wait_ge(h_ready, g * HC0 + h + 1)
                            act.sem_inc(c.passed, 1)
                            bias = b1s[:, bass.ds((2 * i + v // NBS) * HC0 + h, 1)]
                            act.activation(act_out[v % 2][:, h, :], psh[(v % 2) * HC0 + h][:, :], ACT.Gelu,
                                           bias=bias).then_inc(gelued, 1)
                        u, j = v // NBS, v % NBS - 1
                        if j in (0, 1) and not (last and u):
                            act.wait_ge(o_ready, NT + (g - j - 1) * TPB)
                            high(i + u, 1 - u, j)

                high(0, 0, 0)
                high(0, 0, 1)
                with act.Fori(0, E0 // 2 - 1) as i:
                    body(i, False)
                body(E0 // 2 - 1, True)

            @block.vector
            def _(dve):
                dve.sem_inc(o_free, 4)
                n = [0]

                def link(ins):
                    n[0] += 1
                    ins.then_inc(chain, 1)
                    dve.wait_ge(chain, n[0])

                dve.wait_ge(rh_ready, 1)
                dve.tensor_tensor(rws[1][:, :, :], rw[:, :, :], rws[0][:, :, :].bitcast(F32), ALU.subtract).then_inc(rl_ready, 1)
                dve.wait_ge(small_in, 64)
                dve.wait_ge(logits, 1)
                link(dve.tensor_tensor(lg[:, :, :], psh[0][:, 0:NT * E0].rearrange("p (t e) -> p t e", e=E0),
                                       rb[:, :].unsqueeze(1).broadcast_to([P, NT, E0]), ALU.add))
                link(dve.tensor_reduce(col[:, :], lg[:, :, :], AX, ALU.max))
                link(dve.tensor_tensor(lg[:, :, :], lg[:, :, :], col[:, :].unsqueeze(2).broadcast_to([P, NT, E0]), ALU.subtract))
                dve.wait_ge(expd, 1)
                for t in range(NT):
                    ins = dve.max(top[:, t, :], ex[:, t, :])
                link(ins)
                for t in range(NT):
                    ins = dve.max_index(idx[:, t, :], top[:, t, :], ex[:, t, :])
                link(ins)
                link(dve.tensor_copy(idf[:, :, :], idx[:, :, :]))
                iota = c.iota[:, 0:E0].unsqueeze(1).broadcast_to([P, NT, E0])
                link(dve.tensor_tensor(sel[:, :, :], iota, idf[:, :, 0:1].broadcast_to([P, NT, E0]), ALU.is_equal))
                link(dve.tensor_tensor(sel2[:, :, :], iota, idf[:, :, 1:2].broadcast_to([P, NT, E0]), ALU.is_equal))
                link(dve.tensor_tensor(sel[:, :, :], sel[:, :, :], sel2[:, :, :], ALU.add))
                link(dve.tensor_tensor(sel[:, :, :], sel[:, :, :], ex[:, :, :], ALU.mult))
                link(dve.tensor_tensor(col[:, :], top[:, :, 0], top[:, :, 1], ALU.add))
                link(dve.reciprocal(col[:, :], col[:, :]))
                link(dve.tensor_tensor(R[:, :].rearrange("p (e t) -> p t e", t=NT), sel[:, :, :],
                                       col[:, :].unsqueeze(2).broadcast_to([P, NT, E0]), ALU.mult))
                assert n[0] == 13
                for t in range(NT):
                    dve.wait_ge(o_ready, t + 1)
                    dve.tensor_tensor(c.X[:, t, :], pso[t % 4][:, :], c.X[:, t, :], ALU.add).then_inc(o_free, 1)

                def low(i, u, j):
                    dve.wait_ge(wh_ready, 2 * (2 * i + u) + j + 1)
                    parts = (w1s, w2s)[j][u]
                    dve.tensor_tensor(parts[1][:, :, :], raw[j][:, :, :], parts[0][:, :, :].bitcast(F32), ALU.subtract).then_inc(wl_ready, 1)

                def parts(i, v):
                    g = STEPS * i + v
                    high, rest = ht[v % 2]
                    for h in range(HC0):
                        dve.wait_ge(gelued, (g + 2) * HC0 + h + 1)
                        dve.wait_ge(o_ready, NT + (g - 1) * TPB)
                        dve.tensor_copy(high[:, h, :], act_out[v % 2][:, h, :]).then_inc(hh_ready, 1)
                        dve.wait_ge(hh_ready, g * HC0 + h + 1)
                        dve.tensor_tensor(rest[:, h, :], act_out[v % 2][:, h, :], high[:, h, :].bitcast(F32), ALU.subtract).then_inc(h_done, 1)

                def add(i, v):
                    for j in range(TPB):
                        t = (v % NBS) * TPB + j
                        at = NT + (STEPS * i + v) * TPB + j
                        dve.wait_ge(o_ready, at + 1)
                        dve.wait_ge(o_free, at + 4 - NT + 1)
                        dve.scalar_tensor_tensor(out=c.X[:, t, :], in0=pso[j][:, :],
                                                 scalar=R[:, bass.ds((2 * i + v // NBS) * NT + t, 1)],
                                                 in1=c.X[:, t, :], op0=ALU.mult, op1=ALU.add).then_inc(o_free, 1)

                def body(i, last):
                    for v in range(STEPS):
                        parts(i, v)
                        if v:
                            add(i, v - 1)
                        u, j = v // NBS, v % NBS - 1
                        if j in (0, 1) and not (last and u):
                            low(i + u, 1 - u, j)
                    add(i, STEPS - 1)

                low(0, 0, 0)
                low(0, 0, 1)
                with dve.Fori(0, E0 // 2 - 1) as i:
                    body(i, False)
                body(E0 // 2 - 1, True)


def project_block(nc, c, xt, w, a_rows, wh, src, dst):
    with ExitStack() as ctx:
        raw = ctx.enter_context(nc.sbuf_tensor("pr_raw", [P, DC, D], F32))
        ws = split_tile(ctx, nc, "pr_w", [P, DC, D])
        ar = ctx.enter_context(nc.sbuf_tensor("pr_a", [P, 2, D], F32))
        prod = [ctx.enter_context(nc.sbuf_tensor(f"pr_prod{i}", [P, D], F32)) for i in range(2)]
        ps = [ctx.enter_context(nc.psum_tensor(f"pr_ps{i}", [P, D], F32)) for i in range(4)]
        arrived, done, copied = (c.semaphore(f"pr_{n}") for n in ("arrived", "done", "copied"))
        multiplied, reduced = (c.semaphore(f"pr_{n}") for n in ("multiplied", "reduced"))
        high_ready, low_ready = (c.semaphore(f"pr_{n}") for n in ("high_ready", "low_ready"))
        with nc.Block() as block:

            @block.sync
            def _(sp):
                sp.dma_start(raw[:, :, :], w.rearrange("(k p) f -> p k f", p=P)).then_inc(arrived, 16)
                for j in range(2):
                    sp.dma_start(ar[:, j, :], a_rows[j:j + 1, :].broadcast_to([P, D])).then_inc(arrived, 16)

            @block.tensor
            def _(pe):
                pe.wait_ge(low_ready, 1)
                for t in range(NT):
                    if t >= 4:
                        pe.wait_ge(copied, t - 3)
                    for k in range(DC):
                        mm = product(pe, ps[t % 4][:, :], lambda a: xt[a][:, k, t * P:(t + 1) * P], lambda b: ws[b][:, k, :],
                                     k == 0, k == DC - 1)
                    mm.then_inc(done, 1)

            @block.scalar
            def _(act):
                act.wait_ge(arrived, 48)
                act.activation(ws[0][:, :, :], raw[:, :, :], ACT.Copy).then_inc(high_ready, 1)
                for t in range(NT):
                    act.wait_ge(done, t + 1)
                    act.activation(wh[:, t, 0:D], ps[t % 4][:, :], ACT.Copy)
                    act.activation(wh[:, t, D:D + HID], ps[t % 4][:, 0:HID], ACT.Copy).then_inc(copied, 1)

            @block.vector
            def _(dve):
                dve.wait_ge(high_ready, 1)
                dve.tensor_tensor(ws[1][:, :, :], raw[:, :, :], ws[0][:, :, :].bitcast(F32), ALU.subtract).then_inc(low_ready, 1)
                for t in range(NT):
                    dve.wait_ge(copied, t + 1)
                    for j, to in enumerate((src, dst)):
                        m = 2 * t + j
                        if m >= 2:
                            dve.wait_ge(reduced, m - 1)
                        dve.tensor_tensor(prod[j][:, :], wh[:, t, 0:D], ar[:, j, :], ALU.mult).then_inc(multiplied, 1)
                    for j, to in enumerate((src, dst)):
                        dve.wait_ge(multiplied, 2 * t + j + 1)
                        dve.tensor_reduce(to[:, :, t], prod[j][:, :].rearrange("p (h d) -> p h d", d=HID), AX,
                                          ALU.add).then_inc(reduced, 1)


def rows_out(nc, c, ctx, tag, parts):
    sbs = [ctx.enter_context(nc.sbuf_tensor(f"rows{tag}{j}", [f.shape[1], N], dt)) for j, (f, dt, _) in enumerate(parts)]
    banks = [ctx.enter_context(nc.psum_tensor(f"rows{tag}_ps{i}", [32, NB], F32)) for i in range(4)]
    turned, copied, stored = (c.semaphore(f"rows{tag}_{n}") for n in ("turned", "copied", "stored"))
    with nc.Block() as block:

        @block.tensor
        def _(pe):
            for j, (f, _, _) in enumerate(parts):
                r = f.shape[1]
                for q in range(N // NB):
                    if j:
                        pe.wait_ge(copied, (j - 1) * (N // NB) + q + 1)
                    for m in range(NB // P):
                        mm = pe.transpose(banks[q][0:r, m * P:(m + 1) * P], f[:, :, q * (NB // P) + m], c.ident[:, :])
                    mm.then_inc(turned, 1)

        @block.vector
        def _(dve):
            for j, (f, _, _) in enumerate(parts):
                r = f.shape[1]
                for q in range(N // NB):
                    dve.wait_ge(turned, j * (N // NB) + q + 1)
                    dve.tensor_copy(sbs[j][:, q * NB:(q + 1) * NB], banks[q][0:r, :]).then_inc(copied, 1)

        @block.sync
        def _(sp):
            for j, (_, _, to) in enumerate(parts):
                sp.wait_ge(copied, (j + 1) * (N // NB))
                sp.dma_start(to, sbs[j][:, :]).then_inc(stored, 16)
            sp.wait_ge(stored, 16 * len(parts))


def neighbour_max_block(nc, c, adj, dst_rows, maxd):
    with ExitStack() as ctx:
        dst_bc = ctx.enter_context(nc.sbuf_tensor("nm_dst", [P, HEADS, N], F32))
        a = [ctx.enter_context(nc.sbuf_tensor(f"nm_a{i}", [P, N], F32)) for i in range(2)]
        masks = [ctx.enter_context(nc.sbuf_tensor(f"nm_mask{i}", [P, N], F32)) for i in range(2)]
        sums = ctx.enter_context(nc.sbuf_tensor("nm_sums", [P, N], F32))
        acc = [ctx.enter_context(nc.sbuf_tensor(f"nm_acc{i}", [P, HEADS], F32)) for i in range(2)]
        dst_in = c.semaphore("nm_dst_in")
        a_in = [c.semaphore(f"nm_a_in{i}") for i in range(2)]
        masked, maxed, kept = (c.semaphore(f"nm_{n}") for n in ("masked", "maxed", "kept"))
        with nc.Block() as block:

            @block.sync
            def _(sp):
                def load(t, s):
                    sp.dma_start(a[s][:, :], adj[bass.ds(t * P, P), :]).then_inc(a_in[s], 16)

                load(0, 0)
                load(1, 1)
                for h in range(HEADS):
                    sp.dma_start(dst_bc[:, h, :], dst_rows[h:h + 1, :].broadcast_to([P, N])).then_inc(dst_in, 16)
                with sp.Fori(0, NT // 2 - 1) as i:
                    for s in range(2):
                        sp.wait_ge(masked, 2 * i + s + 1)
                        load(2 * i + 2 + s, s)

            @block.vector
            def _(dve):
                dve.wait_ge(dst_in, 16 * HEADS)
                with dve.Fori(0, NT // 2) as i:
                    for s in range(2):
                        dve.wait_ge(a_in[s], 16 * i + 16)
                        dve.tensor_scalar(masks[s][:, :], a[s][:, :], 0.0, -BIG / ALPHA, ALU.is_le, ALU.mult).then_inc(masked, 1)
                        for h in range(HEADS):
                            dve.wait_ge(dst_in, 16 * HEADS)
                            if h:
                                dve.wait_ge(maxed, (2 * i + s) * HEADS + h)
                            else:
                                dve.wait_ge(masked, 2 * i + s + 1)
                            dve.sem_inc(c.passed, 1)
                            dve.tensor_tensor_reduce(out=sums[:, :], in0=dst_bc[:, h, :], in1=masks[s][:, :], scale=1.0,
                                                     scalar=-3.0e38, op0=ALU.add, op1=ALU.max,
                                                     accum_out=acc[s][:, h:h + 1]).then_inc(maxed, 1)
                        dve.wait_ge(maxed, (2 * i + s + 1) * HEADS)
                        dve.tensor_copy(maxd[:, :, bass.ds(2 * i + s, 1)], acc[s][:, :].unsqueeze(2)).then_inc(kept, 1)


def row_terms_block(nc, c, src, dst, maxd, s8, d8, v):
    with ExitStack() as ctx:
        s = ctx.enter_context(nc.sbuf_tensor("rt_s", [P, HEADS, NT], F32))
        m = ctx.enter_context(nc.sbuf_tensor("rt_m", [P, HEADS, NT], F32))
        chain = c.semaphore("rt_chain")
        with nc.Block() as block:

            @block.vector
            def _(dve):
                n = [0]

                def link(ins):
                    n[0] += 1
                    ins.then_inc(chain, 1)
                    dve.wait_ge(chain, n[0])

                al = lambda t: t[:, :, :]
                link(dve.tensor_tensor(al(s), al(src), al(maxd), ALU.add))
                link(dve.scalar_tensor_tensor(out=al(m), in0=al(s), scalar=ALPHA, in1=al(s), op0=ALU.mult, op1=ALU.max))
                link(dve.scalar_tensor_tensor(out=al(v), in0=al(src), scalar=ALPHA, in1=al(m), op0=ALU.mult, op1=ALU.subtract))
                link(dve.tensor_scalar(al(s8), al(src), 1.0 - ALPHA, None, ALU.mult))
                link(dve.tensor_scalar(al(d8), al(dst), ALPHA - 1.0, None, ALU.mult))


def attention_block(nc, c, adj_t, wh, dst, d8, s8_rows, v_rows, sums, weights):
    MASK_STEPS = 4
    POOLED = MASK_STEPS - 1
    TAIL_AT, NEXT_AT = 6, 8
    with ExitStack() as ctx:
        def sb(name, shape, dt=F32):
            return ctx.enter_context(nc.sbuf_tensor(f"at_{name}", shape, dt))
        mask = sb("mask", [P, NT, N], BF16)
        work = sb("work", [P, 8, NW])
        arg = [work[:, i, :] for i in range(4)]
        pr = [work[:, 4 + i, :] for i in range(4)]
        at = [work[:, 2 * i:2 * i + 2, :].rearrange("p a n -> p (a n)") for i in range(2)]
        whc = [sb(f"whc{i}", [P, NT, P]) for i in range(2)]
        s8 = [sb(f"s8_{i}", [P, NW]) for i in range(2)]
        vb = [sb(f"v{i}", [P, NW]) for i in range(2)]
        stage = [sb(f"stage{i}", [P, NW]) for i in range(2)]
        pso = [ctx.enter_context(nc.psum_tensor(f"at_pso{i}", [P, NW], F32)) for i in range(2)]
        s = lambda name: c.semaphore(f"at_{name}")
        at_in = [s("at_in0"), s("at_in1")]
        rows_in = [s("rows_in0"), s("rows_in1")]
        mask_ready, ones_ready, whc_ready = s("mask_ready"), s("ones_ready"), s("whc_ready")
        arg_ready, pooled, self_masked, pr_ready, pr_used = s("arg_ready"), s("pooled"), s("self_masked"), s("pr_ready"), s("pr_used")
        pso_free, staged, stage_free, stored = s("pso_free"), s("staged"), s("stage_free"), s("stored")
        NBW = N // NW
        W2 = NW // NB
        PAIR = 2 * NT
        order = [(b, h) for b in range(NBW) for h in range(HEADS)]
        flat = lambda a: a[:, :, :].rearrange("p h t -> p (h t)")
        with nc.Block() as block:

            @block.sync
            def _(sp):
                sp.sem_inc(stage_free, 3)
                for t in range(NT):
                    if t >= 2:
                        sp.wait_ge(mask_ready, t - 1)
                    sp.dma_start(at[t % 2], adj_t[t * P:(t + 1) * P, :]).then_inc(at_in[t % 2], 16)

                def store(n):
                    b, h = order[n]
                    mine, other = (n % 2) * HID, (1 - n % 2) * HID
                    sp.wait_ge(staged, n + 2)
                    sp.dma_start(sums[n * HID:(n + 1) * HID, :], stage[n % 2][mine:mine + HID, :]).then_inc(stored, 16)
                    sp.dma_start(weights[n:n + 1, :], stage[n % 2][other:other + 1, :]).then_inc(stored, 16)
                    sp.wait_ge(stored, 32 * (n + 1))
                    sp.sem_inc(stage_free, 1)

                for n, (b, h) in enumerate(order):
                    if n >= 2:
                        sp.wait_ge(arg_ready, NT * (n - 1))
                    cols = slice(b * NW, (b + 1) * NW)
                    sp.dma_start(s8[n % 2][:, :], s8_rows[h:h + 1, cols].broadcast_to([P, NW])).then_inc(rows_in[n % 2], 16)
                    sp.dma_start(vb[n % 2][:, :], v_rows[h:h + 1, cols].broadcast_to([P, NW])).then_inc(rows_in[n % 2], 16)
                    if n >= 2:
                        store(n - 2)
                for n in range(len(order) - 2, len(order)):
                    store(n)

            @block.gpsimd
            def _(pool):
                pool.memset(whc[0][:, :, HID:P], 1.0).then_inc(ones_ready, 1)
                pool.memset(whc[1][:, :, 0:HID], 1.0).then_inc(ones_ready, 1)
                pool.wait_ge(mask_ready, NT)
                with pool.Fori(0, NBW) as b:
                    with pool.Fori(0, HP) as i:
                        for k in range(PAIR):
                            if k % MASK_STEPS == POOLED:
                                continue
                            pool.wait_ge(arg_ready, PAIR * (HP * b + i) + k + 1)
                            pool.sem_inc(c.passed, 1)
                            pool.tensor_tensor(arg[k % 4], arg[k % 4], mask[:, k % NT, bass.ds(b * NW, NW)], ALU.add).then_inc(pooled, 1)

            @block.tensor
            def _(pe):
                pe.wait_ge(ones_ready, 2)
                with pe.Fori(0, NBW) as b:
                    with pe.Fori(0, HP) as i:
                        for k in range(PAIR):
                            u, t = k // NT, k % NT
                            if t == 0:
                                pe.wait_ge(whc_ready, 2 * (HP * b + i) + u + 1)
                                pe.wait_ge(pso_free, 2 * (HP * b + i) + u + 1)
                            pe.wait_ge(pr_ready, PAIR * (HP * b + i) + k + 5)
                            for q in range(W2):
                                at_q = slice(q * NB, (q + 1) * NB)
                                mm = pe.matmul(pso[u][:, at_q], whc[u][:, t, :], pr[k % 4][:, at_q],
                                               start=(t == 0), stop=(t == NT - 1))
                            mm.then_inc(pr_used, 1)

            @block.scalar
            def _(act):
                act.sem_inc(pr_ready, 4)

                def take(u, head):
                    act.activation(whc[u][:, :, u * HID:(u + 1) * HID], wh[:, :, bass.ds(head * HID, HID)],
                                   ACT.Copy).then_inc(whc_ready, 1)

                def tail(u, count):
                    act.wait_ge(pr_used, NT * count + 4)
                    act.wait_ge(stage_free, count + 1)
                    act.activation(stage[u][:, :], pso[u][:, :], ACT.Copy).then_inc(pso_free, 1)

                act.activation(whc[0][:, :, 0:HID], wh[:, :, 0:HID], ACT.Copy).then_inc(whc_ready, 1)
                act.wait_ge(mask_ready, NT + 1)
                with act.Fori(0, NBW) as b:
                    with act.Fori(0, HP) as i:
                        for k in range(PAIR):
                            u, t = k // NT, k % NT
                            pair = HP * b + i
                            if k % MASK_STEPS == POOLED:
                                act.wait_ge(self_masked, (PAIR // MASK_STEPS) * pair + k // MASK_STEPS + 1)
                            else:
                                act.wait_ge(pooled, (PAIR - PAIR // MASK_STEPS) * pair + k - k // MASK_STEPS + 1)
                            act.wait_ge(pr_used, PAIR * pair + k + 1)
                            act.sem_inc(c.passed, 1)
                            act.activation(pr[k % 4], arg[k % 4], ACT.Exp,
                                           bias=flat(dst)[:, bass.ds((2 * i + u) * NT + t, 1)]).then_inc(pr_ready, 1)
                            if t == TAIL_AT:
                                tail(1 - u, 2 * pair + u)
                                act.wait_ge(pso_free, 2 * pair + u + 2)
                                act.sem_inc(staged, 1)
                            if t == NEXT_AT:
                                act.wait_ge(pso_free, 2 * pair + u + 2)
                                act.sem_inc(c.passed, 1)
                                take(1 - u, 2 * i + u + 1)
                tail(1, HEADS * NBW)
                act.wait_ge(pso_free, HEADS * NBW + 2)
                act.sem_inc(staged, 1)

            @block.vector
            def _(dve):
                dve.sem_inc(pr_used, 4)
                dve.sem_inc(pso_free, 1)
                for t in range(NT):
                    dve.wait_ge(at_in[t % 2], 16 * (t // 2 + 1))
                    dve.tensor_scalar(mask[:, t, :], at[t % 2], 0.0, -BIG, ALU.is_le, ALU.mult).then_inc(mask_ready, 1)
                dve.memset(pso[1][:, :], 0.0).then_inc(mask_ready, 1)
                dve.wait_ge(mask_ready, NT + 1)
                with dve.Fori(0, NBW) as b:
                    with dve.Fori(0, HP) as i:
                        for k in range(PAIR):
                            g = PAIR * (HP * b + i) + k
                            u = k // NT
                            dve.wait_ge(pr_ready, g + 1)
                            if k % NT == 0:
                                dve.wait_ge(rows_in[u], 32 * (HP * b + i) + 32)
                            dve.scalar_tensor_tensor(
                                out=arg[k % 4], in0=s8[u][:, :], scalar=flat(d8)[:, bass.ds((2 * i + u) * NT + k % NT, 1)],
                                in1=vb[u][:, :], op0=ALU.max, op1=ALU.add).then_inc(arg_ready, 1)
                            if k % MASK_STEPS == POOLED:
                                dve.wait_ge(arg_ready, g + 1)
                                dve.tensor_tensor(arg[k % 4], arg[k % 4], mask[:, k % NT, bass.ds(b * NW, NW)], ALU.add).then_inc(self_masked, 1)


def encoder_block(nc, c, sums, weights, reciprocals, ws, bs):
    TILES = N // NW * HP
    dims = (D, M1, M2, M3)
    with ExitStack() as ctx:
        encs = ctx.enter_context(nc.sbuf_tensor("en_enc", [P, TILES, NW], F32))
        rec = ctx.enter_context(nc.sbuf_tensor("en_rec", [P, TILES, NW], F32))
        low = [ctx.enter_context(nc.sbuf_tensor(f"en_low{i}", [P, NW], F32)) for i in range(2)]
        den = ctx.enter_context(nc.sbuf_tensor("en_den", [P, N // NW * HEADS * NW // P], F32))
        w = [ctx.enter_context(nc.sbuf_tensor(f"en_w{j}", [P, dims[j] // P, dims[j + 1] if j < 3 else D], F32)) for j in range(4)]
        bias = [ctx.enter_context(nc.sbuf_tensor(f"en_b{j}", [P, dims[j + 1] // P], F32)) for j in range(3)]
        b4 = ctx.enter_context(nc.sbuf_tensor("en_b4", [P, D], F32))
        hid = [ctx.enter_context(nc.sbuf_tensor(f"en_h{j}", [P, dims[j + 1] // P, NB], F32)) for j in range(3)]
        psh = [ctx.enter_context(nc.psum_tensor(f"en_ph{i}", [P, NB], F32)) for i in range(2)]
        pso = [ctx.enter_context(nc.psum_tensor(f"en_po{i}", [P, NB], F32)) for i in range(4)]
        s = lambda name: c.semaphore(f"en_{name}")
        arrived, h_ready, h_done, o_ready, o_free, biased = (s(n) for n in ("arrived", "h_ready", "h_done", "o_ready", "o_free", "biased"))
        den_in, inverted, rec_out, mean, halves, exped = (s(n) for n in ("den_in", "inverted", "rec_out", "mean", "halves", "exped"))
        rec_in = [s("rec_in0"), s("rec_in1")]
        enc_ready = s("enc_ready")
        hidden = [(j, o) for j in range(3) for o in range(dims[j + 1] // P)]
        TPB = NB // P
        with nc.Block() as block:

            @block.sync
            def _(sp):
                sp.dma_start(den[:, :], weights.rearrange("r (a n) -> (r a) n", n=den.shape[1])).then_inc(den_in, 16)
                sp.dma_start(encs[:, :, :], sums.rearrange("(a p) n -> p a n", p=P)).then_inc(arrived, 16)
                sp.wait_ge(inverted, 1)
                sp.dma_start(reciprocals.rearrange("r (a n) -> (r a) n", n=den.shape[1]), den[:, :]).then_inc(rec_out, 16)
                sp.wait_ge(rec_out, 16)
                for j in range(TILES):
                    if j >= 2:
                        sp.wait_ge(mean, j - 1)
                    for u in range(2):
                        r = 2 * j + u
                        sp.dma_start(rec[u * HID:(u + 1) * HID, j, :], reciprocals[r:r + 1, :].broadcast_to([HID, NW])).then_inc(rec_in[j % 2], 16)
                for j in range(4):
                    sp.dma_start(w[j][:, :, :], ws[j].rearrange("(k p) o -> p k o", p=P)).then_inc(arrived, 16)
                for j in range(3):
                    sp.dma_start(bias[j][:, :], bs[j]).then_inc(arrived, 16)
                sp.dma_start(b4[:, :], bs[3].rearrange("(a n) -> a n", a=1).broadcast_to([P, D])).then_inc(arrived, 16)

            @block.tensor
            def _(pe):
                pe.wait_ge(arrived, 144)
                for q in range(N // NB):
                    if q % (NW // NB) == 0:
                        pe.wait_ge(enc_ready, (q // (NW // NB) + 1) * HP)
                    b, at_q = q // (NW // NB), slice((q % (NW // NB)) * NB, (q % (NW // NB) + 1) * NB)
                    for x, (j, o) in enumerate(hidden):
                        m = q * len(hidden) + x
                        need = max(m - 1, q * len(hidden) + (0 if j == 0 else [h[0] for h in hidden].index(j)))
                        if need:
                            pe.wait_ge(h_done, need)
                        for k in range(dims[j] // P):
                            rhs = encs[:, b * HP + k, at_q] if j == 0 else hid[j - 1][:, k, :]
                            mm = pe.matmul(psh[m % 2][:, :], w[j][:, k, o * P:(o + 1) * P], rhs,
                                           start=(k == 0), stop=(k == dims[j] // P - 1))
                        mm.then_inc(h_ready, 1)
                    pe.wait_ge(h_done, (q + 1) * len(hidden))
                    for t in range(TPB):
                        pe.wait_ge(o_free, q * TPB + t + 1)
                        for k in range(M3 // P):
                            mm = pe.matmul(pso[t][:, :], hid[2][:, k, t * P:(t + 1) * P], w[3][:, k, :],
                                           start=(k == 0), stop=(k == M3 // P - 1))
                        mm.then_inc(o_ready, 1)

            @block.scalar
            def _(act):
                for j in range(TILES):
                    act.wait_ge(halves, j + 1)
                    act.activation(low[j % 2][:, :], low[j % 2][:, :], ACT.Exp).then_inc(exped, 1)
                act.wait_ge(arrived, 144)
                for q in range(N // NB):
                    for x, (j, o) in enumerate(hidden):
                        m = q * len(hidden) + x
                        act.wait_ge(h_ready, m + 1)
                        act.activation(hid[j][:, o, :], psh[m % 2][:, :], ACT.Relu, bias=bias[j][:, o:o + 1]).then_inc(h_done, 1)

            @block.vector
            def _(dve):
                dve.sem_inc(o_free, 4)
                dve.wait_ge(den_in, 16)
                dve.reciprocal(den[:, :], den[:, :]).then_inc(inverted, 1)
                dve.wait_ge(arrived, 16)

                def elu_end(j):
                    dve.wait_ge(exped, j + 1)
                    dve.scalar_tensor_tensor(out=encs[:, j, :], in0=low[j % 2][:, :], scalar=-1.0, in1=encs[:, j, :],
                                             op0=ALU.add, op1=ALU.max).then_inc(enc_ready, 1)

                for j in range(TILES):
                    dve.wait_ge(rec_in[j % 2], 32 * (j // 2 + 1))
                    dve.tensor_tensor(encs[:, j, :], encs[:, j, :], rec[:, j, :], ALU.mult).then_inc(mean, 1)
                    if j:
                        elu_end(j - 1)
                    dve.wait_ge(mean, j + 1)
                    if j >= 2:
                        dve.wait_ge(enc_ready, j - 1)
                    dve.tensor_scalar(low[j % 2][:, :], encs[:, j, :], 0.0, None, ALU.min).then_inc(halves, 1)
                elu_end(TILES - 1)
                dve.wait_ge(arrived, 144)
                for t in range(NT):
                    dve.tensor_tensor(c.X[:, t, :], c.X[:, t, :], b4[:, :], ALU.add).then_inc(biased, 1)
                for t in range(NT):
                    dve.wait_ge(biased, t + 1)
                    dve.wait_ge(o_ready, t + 1)
                    dve.tensor_tensor(c.X[:, t, :], pso[t % 4][:, :], c.X[:, t, :], ALU.add).then_inc(o_free, 1)


def attention_stage(nc, c, dram):
    with ExitStack() as st:
        def sb(name, shape):
            return st.enter_context(nc.sbuf_tensor(f"ga_{name}", shape, F32))
        dst_rows = nc.dram_tensor("ga_dst_rows", [HEADS, N], F32).ap()
        s8_rows = nc.dram_tensor("ga_s8_rows", [HEADS, N], F32).ap()
        v_rows = nc.dram_tensor("ga_v_rows", [HEADS, N], F32).ap()
        sums = nc.dram_tensor("ga_sums", [N // NW * D, NW], F32).ap()
        weights, reciprocals = (nc.dram_tensor(f"ga_{n}", [N // NW * HEADS, NW], F32).ap() for n in ("weights", "reciprocals"))
        src, dst, maxd = (sb(n, [P, HEADS, NT]) for n in ("src", "dst", "maxd"))
        s8, d8 = (sb(n, [P, HEADS, NT]) for n in ("s8", "d8"))
        v = sb("v", [P, HEADS, NT])
        with ExitStack() as whs:
            wh = whs.enter_context(nc.sbuf_tensor("ga_wh", [P, NT, D + HID], F32))
            with ExitStack() as pre:
                xt = split_tile(pre, nc, "ga_xt", [P, DC, N])
                layernorm_block(nc, c, "2", xt)
                project_block(nc, c, xt, dram["w_heads"], dram["a_rows"], wh, src, dst)
            with ExitStack() as pre:
                rows_out(nc, c, pre, "d", [(dst, F32, dst_rows)])
            neighbour_max_block(nc, c, dram["adj"], dst_rows, maxd)
            row_terms_block(nc, c, src, dst, maxd, s8, d8, v)
            with ExitStack() as pre:
                rows_out(nc, c, pre, "s", [(s8, F32, s8_rows), (v, F32, v_rows)])
            attention_block(nc, c, dram["adj_t"], wh, dst, d8, s8_rows, v_rows, sums, weights)
        encoder_block(nc, c, sums, weights, reciprocals, [dram[f"enc_w{j}"] for j in range(4)], [dram[f"enc_b{j}"] for j in range(4)])


def route_block(nc, c, xt, dram, oe, slot_tokens, dest, weight):
    with ExitStack() as ctx:
        def sb(name, shape, dt=F32):
            return ctx.enter_context(nc.sbuf_tensor(f"r_{name}", shape, dt))
        wg = sb("wg", [P, DC, E1])
        before, ones, first_slot = sb("before", [P, P]), sb("ones", [P, P]), sb("first_slot", [P, E1])
        tokens = sb("tokens", [P, NT])
        zero = sb("zero", [1, D])
        sc, hot, mask, places = sb("sc", [P, NT, E1]), sb("hot", [P, K1, NT, E1]), sb("mask", [P, NT, E1]), sb("places", [P, NT, E1])
        tmp = sb("tmp", [P, NT, E1])
        col, gm, keep, kept = sb("col", [P, NT]), sb("gm", [P, NT, G1]), sb("keep", [P, NT, G1]), sb("kept", [P, KG, NT, G1])
        top, idx, idf = sb("top", [P, NT, 8]), sb("idx", [P, NT, 8], U32), sb("idf", [P, NT, 8])
        carry = sb("carry", [P, NT, E1])
        destf = sb("destf", [P, K1, NT])
        wgs = split_tile(ctx, nc, "r_wgs", [P, DC, E1])
        raw = sb("raw", [P, DC, D])
        sw = [split_tile(ctx, nc, f"r_sw{j}", [P, DC, D]) for j in range(3)]
        gate = [sb(f"gate{i}", [P, NB]) for i in range(2)]
        hf = [sb(f"hf{i}", [P, NB]) for i in range(2)]
        hid = split_tile(ctx, nc, "r_hid", [P, DC, NB])
        psl = ctx.enter_context(nc.psum_tensor("r_psl", [P, NT, E1], F32))
        pst = ctx.enter_context(nc.psum_tensor("r_pst", [P, NT, E1], F32))
        ps1 = [ctx.enter_context(nc.psum_tensor(f"r_ps1_{i}", [P, NB], F32)) for i in range(2)]
        ps3 = [ctx.enter_context(nc.psum_tensor(f"r_ps3_{i}", [P, NB], F32)) for i in range(2)]
        pso = [ctx.enter_context(nc.psum_tensor(f"r_pso{i}", [P, NB], F32)) for i in range(2)]
        s = lambda name: c.semaphore(f"r_{name}")
        small_in, sw_in, stored, filled, scattered = s("small_in"), s("sw_in"), s("stored"), s("filled"), s("scattered")
        logits, expd, chain, counted, zeroed = s("logits"), s("expd"), s("chain"), s("counted"), s("zeroed")
        h_ready, gated, h_done, o_ready, o_free = s("h_ready"), s("gated"), s("h_done"), s("o_ready"), s("o_free")
        gh_ready, gl_ready, swh_ready, swl_ready, multiplied, hh_ready = (
            s(n) for n in ("gh_ready", "gl_ready", "swh_ready", "swl_ready", "multiplied", "hh_ready"))
        TPB = NB // P
        BLOCKS = N // NB
        with nc.Block() as block:

            @block.sync
            def _(sp):
                sp.dma_start(wg[:, :, :], dram["wg_t"].rearrange("(k p) e -> p k e", p=P)).then_inc(small_in, 16)
                for t, n in ((before, "c_before"), (ones, "c_ones"), (first_slot, "c_first_slot"), (tokens, "c_tokens")):
                    sp.dma_start(t[:, :], dram[n]).then_inc(small_in, 16)
                sp.dma_start(slot_tokens, dram["c_no_token"]).then_inc(filled, 16)
                for j, n in enumerate(("sw1", "sw3", "sw2")):
                    if j:
                        sp.wait_ge(swl_ready, j)
                    sp.dma_start(raw[:, :, :], dram[n].rearrange("(k p) f -> p k f", p=P)).then_inc(sw_in, 16)
                sp.wait_ge(zeroed, 1)
                sp.dma_start(oe[SLOTS:SLOTS + 1, :], zero[:, :]).then_inc(stored, 16)
                sp.wait_ge(stored, 16)

            @block.gpsimd
            def _(pool):
                pool.memset(zero[:, :], 0.0).then_inc(zeroed, 1)
                pool.wait_ge(filled, 16)
                pool.wait_ge(small_in, 80)
                pool.wait_ge(chain, DEST_AT)
                for k in range(K1):
                    for t in range(NT):
                        pool.indirect_dma_start(out=slot_tokens, out_offset=bass.IndirectOffsetOnAxis(ap=dest[:, k, t:t + 1], axis=0),
                                                in_=tokens[:, t:t + 1], in_offset=None, bounds_check=SLOTS - 1,
                                                oob_is_err=False).then_inc(scattered, 16)
                pool.wait_ge(scattered, 16 * K1 * NT)

            @block.tensor
            def _(pe):
                pe.wait_ge(small_in, 80)
                pe.wait_ge(gl_ready, 1)
                for t in range(NT):
                    for k in range(DC):
                        mm = product(pe, psl[:, t, :], lambda a: xt[a][:, k, t * P:(t + 1) * P], lambda b: wgs[b][:, k, :],
                                     k == 0, k == DC - 1)
                mm.then_inc(logits, 1)

                def hidden(q):
                    for f in range(DC):
                        m = q * DC + f
                        if m >= 2:
                            pe.wait_ge(multiplied, m - 1)
                        for j, ps in enumerate((ps1, ps3)):
                            for k in range(DC):
                                mm = product(pe, ps[m % 2][:, :], lambda a: sw[j][a][:, k, f * P:(f + 1) * P],
                                             lambda b: xt[b][:, k, q * NB:(q + 1) * NB], k == 0, k == DC - 1)
                        mm.then_inc(h_ready, 1)

                def outs(q):
                    pe.wait_ge(h_done, (q + 1) * DC)
                    for t in range(TPB):
                        pe.wait_ge(o_free, q * TPB + t + 1)
                        for f in range(DC):
                            mm = product(pe, pso[t % 2][:, :], lambda a: hid[a][:, f, t * P:(t + 1) * P], lambda b: sw[2][b][:, f, :],
                                         f == 0, f == DC - 1)
                        mm.then_inc(o_ready, 1)

                pe.wait_ge(chain, MASK_AT)
                flat = mask[:, :, :].rearrange("p t e -> p (t e)")
                pe.matmul(psl[:, :, :].rearrange("p t e -> p (t e)"), before[:, :], flat, start=True, stop=True)
                pe.matmul(pst[:, :, :].rearrange("p t e -> p (t e)"), ones[:, :], flat, start=True, stop=True).then_inc(counted, 1)
                pe.wait_ge(swl_ready, 3)
                for q in range(BLOCKS):
                    hidden(q)
                    outs(q)

            @block.scalar
            def _(act):
                def high(j):
                    act.wait_ge(sw_in, 16 * (j + 1))
                    act.activation(sw[j][0][:, :, :], raw[:, :, :], ACT.Copy).then_inc(swh_ready, 1)

                act.wait_ge(small_in, 80)
                act.activation(wgs[0][:, :, :], wg[:, :, :], ACT.Copy).then_inc(gh_ready, 1)
                high(0)
                act.wait_ge(chain, 2)
                act.activation(sc[:, :, :], sc[:, :, :], ACT.Exp).then_inc(expd, 1)
                high(1)
                high(2)
                for m in range(BLOCKS * DC):
                    act.wait_ge(h_ready, m + 1)
                    if m >= 2:
                        act.wait_ge(multiplied, m - 1)
                    act.activation(gate[m % 2][:, :], ps1[m % 2][:, :], ACT.Silu).then_inc(gated, 1)

            @block.vector
            def _(dve):
                dve.sem_inc(o_free, 2)
                n = [0]

                def link(ins):
                    n[0] += 1
                    ins.then_inc(chain, 1)
                    dve.wait_ge(chain, n[0])

                def over(ap, e):
                    return ap.unsqueeze(2).broadcast_to([P, NT, e])

                def one_hot(out, e, column):
                    link(dve.tensor_tensor(out, c.iota[:, 0:e].unsqueeze(1).broadcast_to([P, NT, e]), over(column, e), ALU.is_equal))

                def top8(values):
                    for t in range(NT):
                        ins = dve.max(top[:, t, :], values[:, t, :])
                    link(ins)
                    for t in range(NT):
                        ins = dve.max_index(idx[:, t, :], top[:, t, :], values[:, t, :])
                    link(ins)
                    link(dve.tensor_copy(idf[:, :, :], idx[:, :, :]))

                def low(j):
                    dve.wait_ge(swh_ready, j + 1)
                    dve.tensor_tensor(sw[j][1][:, :, :], raw[:, :, :], sw[j][0][:, :, :].bitcast(F32), ALU.subtract).then_inc(swl_ready, 1)

                dve.wait_ge(gh_ready, 1)
                dve.tensor_tensor(wgs[1][:, :, :], wg[:, :, :], wgs[0][:, :, :].bitcast(F32), ALU.subtract).then_inc(gl_ready, 1)
                dve.wait_ge(small_in, 80)
                low(0)
                dve.wait_ge(logits, 1)
                link(dve.tensor_reduce(col[:, :], psl[:, :, :], AX, ALU.max))
                link(dve.tensor_tensor(sc[:, :, :], psl[:, :, :], over(col[:, :], E1), ALU.subtract))
                dve.wait_ge(expd, 1)
                link(dve.tensor_reduce(col[:, :], sc[:, :, :], AX, ALU.add))
                link(dve.reciprocal(col[:, :], col[:, :]))
                link(dve.tensor_tensor(sc[:, :, :], sc[:, :, :], over(col[:, :], E1), ALU.mult))
                link(dve.tensor_reduce(gm[:, :, :], sc[:, :, :].rearrange("p t (g e) -> p t g e", e=EG), AX, ALU.max))
                top8(gm)
                for k in range(KG):
                    one_hot(kept[:, k, :, :], G1, idf[:, :, k])
                link(dve.tensor_tensor(keep[:, :, :], kept[:, 0, :, :], kept[:, 1, :, :], ALU.add))
                for k in range(2, KG):
                    link(dve.tensor_tensor(keep[:, :, :], keep[:, :, :], kept[:, k, :, :], ALU.add))
                spread = lambda a: a[:, :, :].rearrange("p t g -> p (t g)").unsqueeze(2).broadcast_to([P, NT * G1, EG])
                grouped = lambda a: a[:, :, :].rearrange("p t (g e) -> p (t g) e", e=EG)
                link(dve.tensor_tensor(grouped(tmp), grouped(sc), spread(keep), ALU.mult))
                link(dve.tensor_scalar(keep[:, :, :], keep[:, :, :], -1.0, None, ALU.add))
                link(dve.tensor_tensor(grouped(tmp), grouped(tmp), spread(keep), ALU.add))
                top8(tmp)
                for k in range(K1):
                    one_hot(hot[:, k, :, :], E1, idf[:, :, k])
                link(dve.tensor_tensor(mask[:, :, :], hot[:, 0, :, :], hot[:, 1, :, :], ALU.add))
                for k in range(2, K1):
                    link(dve.tensor_tensor(mask[:, :, :], mask[:, :, :], hot[:, k, :, :], ALU.add))
                assert n[0] == MASK_AT
                low(1)
                link(dve.tensor_reduce(col[:, :], top[:, :, 0:K1], AX, ALU.add))
                link(dve.tensor_scalar(col[:, :], col[:, :], 1e-9, None, ALU.add))
                link(dve.reciprocal(col[:, :], col[:, :]))
                link(dve.tensor_tensor(weight[:, :, :].rearrange("p k t -> p t k"), top[:, :, 0:K1], over(col[:, :], K1), ALU.mult))
                dve.wait_ge(counted, 1)
                link(dve.memset(carry[:, 0, :], 0.0))
                for t in range(1, NT):
                    link(dve.tensor_tensor(carry[:, t, :], pst[:, t - 1, :], carry[:, t - 1, :], ALU.add))
                link(dve.tensor_tensor(places[:, :, :], psl[:, :, :], carry[:, :, :], ALU.add))
                link(dve.tensor_scalar(tmp[:, :, :], places[:, :, :], float(CAP), None, ALU.is_lt))
                slots = first_slot[:, :].unsqueeze(1).broadcast_to([P, NT, E1])
                link(dve.tensor_tensor(places[:, :, :], places[:, :, :], slots, ALU.add))
                link(dve.scalar_tensor_tensor(out=places[:, :, :], in0=places[:, :, :], scalar=-float(SLOTS), in1=tmp[:, :, :], op0=ALU.add, op1=ALU.mult))
                link(dve.tensor_scalar(places[:, :, :], places[:, :, :], float(SLOTS), None, ALU.add))
                for k in range(K1):
                    link(dve.tensor_tensor(hot[:, k, :, :], hot[:, k, :, :], places[:, :, :], ALU.mult))
                    link(dve.tensor_reduce(destf[:, k, :], hot[:, k, :, :], AX, ALU.add))
                link(dve.tensor_copy(dest[:, :, :], destf[:, :, :]))
                assert n[0] == DEST_AT
                low(2)

                for q in range(BLOCKS):
                    for f in range(DC):
                        m = q * DC + f
                        dve.wait_ge(gated, m + 1)
                        dve.tensor_tensor(hf[m % 2][:, :], ps3[m % 2][:, :], gate[m % 2][:, :], ALU.mult).then_inc(multiplied, 1)
                        dve.wait_ge(multiplied, m + 1)
                        if f == 0 and q:
                            dve.wait_ge(o_ready, q * TPB)
                        dve.tensor_copy(hid[0][:, f, :], hf[m % 2][:, :]).then_inc(hh_ready, 1)
                        dve.wait_ge(hh_ready, m + 1)
                        dve.tensor_tensor(hid[1][:, f, :], hf[m % 2][:, :], hid[0][:, f, :].bitcast(F32), ALU.subtract).then_inc(h_done, 1)
                    for t in range(TPB):
                        dve.wait_ge(o_ready, q * TPB + t + 1)
                        dve.tensor_tensor(c.X[:, q * TPB + t, :], pso[t % 2][:, :], c.X[:, q * TPB + t, :], ALU.add).then_inc(o_free, 1)


MASK_AT = 6 + 3 + KG + (KG - 1) + 3 + 3 + K1 + (K1 - 1)
DEST_AT = MASK_AT + 4 + NT + 5 + 2 * K1 + 1


def experts_block(nc, c, dram, xp, oe, slot_tokens):
    with ExitStack() as ctx:
        def sb(name, shape, dt=F32):
            return ctx.enter_context(nc.sbuf_tensor(f"e_{name}", shape, dt))
        idx = sb("idx", [P, NCT, E1], U32)
        tok = sb("tok", [E1, CAP])
        idn = [sb(f"idn{u}", [P, NCT], U32) for u in range(2)]
        xe = [sb(f"xe{u}", [P, NCT, D]) for u in range(2)]
        raw = [sb(f"raw{j}", [P, DC, D]) for j in range(3)]
        w13 = [[split_tile(ctx, nc, f"e_w{j}_{u}", [P, DC, D]) for j in (1, 3)] for u in range(2)]
        w2 = split_tile(ctx, nc, "e_w2", [P, DC, D])
        xet = [split_tile(ctx, nc, f"e_xet{u}", [P, DC, CAP]) for u in range(2)]
        hid = split_tile(ctx, nc, "e_hid", [P, DC, NCT * P])
        gate = [sb(f"gate{i}", [P, CAP]) for i in range(2)]
        hf = [sb(f"hf{i}", [P, CAP]) for i in range(2)]
        res = [sb(f"res{u}", [P, NCT, D]) for u in range(2)]
        pst = [ctx.enter_context(nc.psum_tensor(f"e_pst{i}", [P, DC, P], F32)) for i in range(2)]
        ps1 = [ctx.enter_context(nc.psum_tensor(f"e_ps1_{i}", [P, NB], F32)) for i in range(2)]
        ps3 = [ctx.enter_context(nc.psum_tensor(f"e_ps3_{i}", [P, NB], F32)) for i in range(2)]
        pso = [ctx.enter_context(nc.psum_tensor(f"e_pso{i}", [P, D], F32)) for i in range(2)]
        s = lambda name: c.semaphore(f"e_{name}")
        tok_in, tok_turned, idx_ready, idn_ready = s("tok_in"), s("tok_turned"), s("idx_ready"), s("idn_ready")
        w_in = [s("w_in0"), s("w_in1"), s("w_in2")]
        x_in = [s("x_in0"), s("x_in1")]
        res_out, res_free = [s("res_out0"), s("res_out1")], s("res_free")
        turned, xh_ready, xl_ready, wh_ready, wl_ready = s("turned"), s("xh_ready"), s("xl_ready"), s("wh_ready"), s("wl_ready")
        h_ready, gated, multiplied, hh_ready, h_done, o_ready, o_done = (
            s(n) for n in ("h_ready", "gated", "multiplied", "hh_ready", "h_done", "o_ready", "o_done"))
        HALF = E1 // 2
        W_NAMES = ("w1_1", "w3_1", "w2_1")
        whole = CAP // P

        with nc.Block() as block:

            @block.sync
            def _(sp):
                sp.dma_start(tok[:, :], slot_tokens.rearrange("(e s) a -> e (s a)", s=CAP)).then_inc(tok_in, 16)

                def load(e, j):
                    src = dram[W_NAMES[j]][bass.ds(e * D, D), :].rearrange("(k p) f -> p k f", p=P)
                    sp.dma_start(raw[j][:, :, :], src).then_inc(w_in[j], 16)

                def store(i, u):
                    e = 2 * i + u
                    sp.wait_ge(o_done, 2 + (e + 1) * NCT)
                    sp.dma_start(oe[bass.ds(e * CAP, whole * P), :].rearrange("(j p) d -> p j d", p=P), res[u][:, 0:whole, :]).then_inc(res_out[u], 16)
                    sp.dma_start(oe[bass.ds(e * CAP + whole * P, CAP - whole * P), :], res[u][0:CT[-1], whole, :]).then_inc(res_out[u], 16)
                    sp.wait_ge(res_out[u], 32 * i + 32)
                    sp.sem_inc(res_free, 1)

                sp.sem_inc(res_free, 2)
                for j in range(3):
                    load(0, j)

                def again(e, j, done):
                    sp.wait_ge(wl_ready, done)
                    load(e, j)

                def step(i, u, last):
                    e = 2 * i + u
                    again(e + 1, 2, 3 * e + 3)
                    if not last:
                        again(e + 2, 0, 3 * e + 4)
                        again(e + 2, 1, 3 * e + 5)
                    store(i, u)

                again(1, 0, 1)
                again(1, 1, 2)
                with sp.Fori(0, HALF - 1) as i:
                    step(i, 0, False)
                    step(i, 1, False)
                step(HALF - 1, 0, True)
                store(HALF - 1, 1)

            @block.gpsimd
            def _(pool):
                pool.wait_ge(idx_ready, NCT)

                def gather(i, u):
                    e = 2 * i + u
                    for j, r in enumerate(CT):
                        pool.tensor_copy(idn[u][0:r, j:j + 1], idx[0:r, j, bass.ds(e, 1)]).then_inc(idn_ready, 1)
                    for j, r in enumerate(CT):
                        pool.wait_ge(idx_ready, NCT)
                        pool.wait_ge(idn_ready, e * NCT + j + 1)
                        pool.sem_inc(c.passed, 1)
                        pool.indirect_dma_start(out=xe[u][0:r, j, :], out_offset=None, in_=xp,
                                                in_offset=bass.IndirectOffsetOnAxis(ap=idn[u][0:r, j:j + 1], axis=0)).then_inc(x_in[u], 16)

                gather(0, 0)
                gather(0, 1)
                with pool.Fori(0, HALF - 1) as i:
                    for u in range(2):
                        pool.wait_ge(turned, (2 * i + u + 1) * NCT)
                        gather(i + 1, u)

            @block.tensor
            def _(pe):
                pe.wait_ge(tok_in, 16)
                for j, r in enumerate(CT):
                    mm = pe.transpose(ps1[0][0:r, j * P:j * P + E1], tok[:, j * P:j * P + r], c.ident[0:E1, 0:E1])
                mm.then_inc(tok_turned, 1)

                def turn(i, u):
                    for j, r in enumerate(CT):
                        pe.wait_ge(tok_in, 16)
                        if j == 0:
                            pe.wait_ge(x_in[u], 16 * NCT * i + 16 * NCT)
                        pe.wait_ge(xl_ready, (2 * i + u) * NCT + j + 1)
                        pe.sem_inc(c.passed, 1)
                        for k in range(DC):
                            mm = pe.transpose(pst[(u * NCT + j) % 2][:, k, 0:r], xe[u][0:r, j, k * P:(k + 1) * P], c.ident[0:r, 0:r])
                        mm.then_inc(turned, 1)

                def hidden(i, u):
                    e = 2 * i + u
                    pe.wait_ge(wl_ready, 3 * e + 2)
                    pe.wait_ge(xl_ready, 2 + (e + 1) * NCT)
                    for f in range(DC):
                        pe.wait_ge(multiplied, e * DC + f + 1)
                        for j, ps in enumerate((ps1, ps3)):
                            for k in range(DC):
                                mm = product(pe, ps[f % 2][:, 0:CAP], lambda a: w13[u][j][a][:, k, f * P:(f + 1) * P],
                                            lambda b: xet[u][b][:, k, :], k == 0, k == DC - 1)
                        mm.then_inc(h_ready, 1)

                def outs(i, u):
                    e = 2 * i + u
                    pe.wait_ge(wl_ready, 3 * e + 3)
                    for j in range(NCT):
                        pe.wait_ge(o_done, e * NCT + j + 1)
                        for f in range(DC):
                            if j == 0:
                                pe.wait_ge(h_done, e * DC + f + 1)
                            mm = product(pe, pso[(u * NCT + j) % 2][:, :], lambda a: hid[a][:, f, j * P:(j + 1) * P],
                                        lambda b: w2[b][:, f, :], f == 0, f == DC - 1)
                        mm.then_inc(o_ready, 1)

                def step(i, u, last):
                    hidden(i, u)
                    if not last:
                        turn(i + u, 1 - u)
                    outs(i, u)

                turn(0, 0)
                with pe.Fori(0, HALF - 1) as i:
                    step(i, 0, False)
                    step(i, 1, False)
                step(HALF - 1, 0, False)
                step(HALF - 1, 1, True)

            @block.scalar
            def _(act):
                act.sem_inc(o_ready, 1)

                def high(i, u, j):
                    e = 2 * i + u
                    act.wait_ge(w_in[j], 16 * e + 16)
                    if j == 2:
                        act.wait_ge(o_ready, e * NCT + 1)
                    act.activation((w13[u][j] if j < 2 else w2)[0][:, :, :], raw[j][:, :, :], ACT.Copy).then_inc(wh_ready, 1)

                def rows(i, u):
                    for j, r in enumerate(CT):
                        act.wait_ge(turned, (2 * i + u) * NCT + j + 1)
                        act.activation(xet[u][0][:, :, j * P:j * P + r], pst[(u * NCT + j) % 2][:, :, 0:r], ACT.Copy).then_inc(xh_ready, 1)

                def step(i, u, last):
                    high(i, u, 2)
                    for f in range(DC):
                        act.wait_ge(h_ready, (2 * i + u) * DC + f + 1)
                        act.activation(gate[f % 2][:, :], ps1[f % 2][:, 0:CAP], ACT.Silu).then_inc(gated, 1)
                        if f < 2 and not last:
                            high(i + u, 1 - u, f)
                    if not last:
                        rows(i + u, 1 - u)

                high(0, 0, 0)
                high(0, 0, 1)
                rows(0, 0)
                with act.Fori(0, HALF - 1) as i:
                    step(i, 0, False)
                    step(i, 1, False)
                step(HALF - 1, 0, False)
                step(HALF - 1, 1, True)

            @block.vector
            def _(dve):
                dve.wait_ge(tok_turned, 1)
                for j, r in enumerate(CT):
                    dve.tensor_copy(idx[0:r, j, :], ps1[0][0:r, j * P:j * P + E1]).then_inc(idx_ready, 1)
                pad = NCT * P - CAP
                dve.memset(gate[0][:, 0:DC * pad], 0.0).then_inc(idx_ready, 1)
                dve.wait_ge(idx_ready, NCT + 1)
                for part in range(2):
                    dve.tensor_copy(hid[part][:, :, CAP:NCT * P], gate[0][:, 0:DC * pad].rearrange("p (k n) -> p k n", n=pad)).then_inc(idx_ready, 1)
                dve.wait_ge(idx_ready, NCT + 3)
                dve.sem_inc(multiplied, 2)
                dve.sem_inc(xl_ready, 2)
                dve.sem_inc(o_done, 2)

                def low(i, u, j):
                    dve.wait_ge(wh_ready, 3 * (2 * i + u) + j + 1)
                    parts = w13[u][j] if j < 2 else w2
                    dve.tensor_tensor(parts[1][:, :, :], raw[j][:, :, :], parts[0][:, :, :].bitcast(F32), ALU.subtract).then_inc(wl_ready, 1)

                def rows(i, u):
                    for j, r in enumerate(CT):
                        dve.wait_ge(xh_ready, (2 * i + u) * NCT + j + 1)
                        at = slice(j * P, j * P + r)
                        dve.tensor_tensor(xet[u][1][:, :, at], pst[(u * NCT + j) % 2][:, :, 0:r], xet[u][0][:, :, at].bitcast(F32),
                                          ALU.subtract).then_inc(xl_ready, 1)

                def step(i, u, last):
                    e = 2 * i + u
                    low(i, u, 2)
                    for f in range(DC):
                        dve.wait_ge(gated, e * DC + f + 1)
                        dve.tensor_tensor(hf[f % 2][:, :], ps3[f % 2][:, 0:CAP], gate[f % 2][:, :], ALU.mult).then_inc(multiplied, 1)
                        dve.wait_ge(multiplied, e * DC + f + 3)
                        if f == 0:
                            dve.wait_ge(o_ready, e * NCT + 1)
                        dve.tensor_copy(hid[0][:, f, 0:CAP], hf[f % 2][:, :]).then_inc(hh_ready, 1)
                        dve.wait_ge(hh_ready, e * DC + f + 1)
                        dve.tensor_tensor(hid[1][:, f, 0:CAP], hf[f % 2][:, :], hid[0][:, f, 0:CAP].bitcast(F32), ALU.subtract).then_inc(h_done, 1)
                        if f < 2 and not last:
                            low(i + u, 1 - u, f)
                    if not last:
                        rows(i + u, 1 - u)
                    dve.wait_ge(res_free, e + 1)
                    for j, r in enumerate(CT):
                        dve.wait_ge(o_ready, e * NCT + j + 2)
                        dve.tensor_copy(res[u][0:r, j, :], pso[(u * NCT + j) % 2][0:r, :]).then_inc(o_done, 1)

                low(0, 0, 0)
                low(0, 0, 1)
                rows(0, 0)
                with dve.Fori(0, HALF - 1) as i:
                    step(i, 0, False)
                    step(i, 1, False)
                step(HALF - 1, 0, False)
                step(HALF - 1, 1, True)


def combine_block(nc, c, oe, dest, weight, out):
    RING = 8
    with ExitStack() as ctx:
        got = [ctx.enter_context(nc.sbuf_tensor(f"c_got{i}", [P, D], F32)) for i in range(RING)]
        got_in = [c.semaphore(f"c_got_in{i}") for i in range(RING)]
        added, stored = c.semaphore("c_added"), c.semaphore("c_stored")
        with nc.Block() as block:

            @block.gpsimd
            def _(pool):
                for m in range(NT * K1):
                    t, k = m // K1, m % K1
                    if m >= RING:
                        pool.wait_ge(added, m - RING + 1)
                    pool.indirect_dma_start(out=got[m % RING][:, :], out_offset=None, in_=oe,
                                            in_offset=bass.IndirectOffsetOnAxis(ap=dest[:, k, t:t + 1], axis=0)).then_inc(got_in[m % RING], 16)

            @block.vector
            def _(dve):
                for m in range(NT * K1):
                    t, k = m // K1, m % K1
                    dve.wait_ge(got_in[m % RING], 16 * (m // RING + 1))
                    if k:
                        dve.wait_ge(added, m)
                    dve.scalar_tensor_tensor(out=c.X[:, t, :], in0=got[m % RING][:, :], scalar=weight[:, k, t:t + 1],
                                             in1=c.X[:, t, :], op0=ALU.mult, op1=ALU.add).then_inc(added, 1)

            @block.sync
            def _(sp):
                for t in range(NT):
                    sp.wait_ge(added, K1 * (t + 1))
                    sp.dma_start(out[t * P:(t + 1) * P, :], c.X[:, t, :]).then_inc(stored, 16)
                sp.wait_ge(stored, 16 * NT)


def moe1_stage(nc, c, dram, out):
    xp = nc.dram_tensor("m1_xp", [N + 1, D], F32).ap()
    oe = nc.dram_tensor("m1_oe", [SLOTS + 1, D], F32).ap()
    slot_tokens = nc.dram_tensor("m1_slot_tokens", [SLOTS, 1], F32).ap()
    with ExitStack() as st:
        dest = st.enter_context(nc.sbuf_tensor("m1_dest", [P, K1, NT], U32))
        weight = st.enter_context(nc.sbuf_tensor("m1_weight", [P, K1, NT], F32))
        with ExitStack() as pre:
            xt = split_tile(pre, nc, "m1_xt", [P, DC, N])
            layernorm_block(nc, c, "3", xt, store=xp)
            route_block(nc, c, xt, dram, oe, slot_tokens, dest, weight)
        experts_block(nc, c, dram, xp, oe, slot_tokens)
        combine_block(nc, c, oe, dest, weight, out)


class Shared:

    def __init__(self, nc):
        self.nc = nc
        self.semaphores = []

    def semaphore(self, name):
        self.semaphores.append(self.nc.alloc_semaphore(name))
        return self.semaphores[-1]

    def stage_ends(self):
        self.nc.clear_and_free_semaphores(self.semaphores)
        self.nc.all_engine_barrier()
        self.semaphores = []


def build(nc, dram, out):
    c = Shared(nc)
    with ExitStack() as ctx:
        def sb(name, shape, dt=F32):
            return ctx.enter_context(nc.sbuf_tensor(name, shape, dt))
        c.X = sb("X", [P, NT, D])
        c.ident = sb("ident", [P, P])
        c.iota = sb("iota", [P, E1])
        c.passed = nc.alloc_semaphore("passed")
        load_block(nc, c, dram["x"], [(c.ident, dram["c_ident"]), (c.iota, dram["c_iota"])])
        with ExitStack() as st:
            xn = st.enter_context(nc.sbuf_tensor("g0_xn", [P, NT, D], F32))
            y = st.enter_context(nc.sbuf_tensor("g0_y", [P, NT, D], F32))
            dinv = st.enter_context(nc.sbuf_tensor("g0_dinv", [P, NT], F32))
            layernorm_block(nc, c, "0", None, xn)
            degree_block(nc, c, dram["adj"], xn, dinv)
            mix_block(nc, c, dram["adj"], dram["adj_t"], xn, y, dinv)
            mix_block(nc, c, dram["adj"], dram["adj_t"], None, y, dinv)
        with ExitStack() as st:
            xt = split_tile(st, nc, "m0_xt", [P, DC, N])
            layernorm_block(nc, c, "1", xt)
            moe0_block(nc, c, xt, dram["L0_ffn_router_w"], dram["L0_ffn_router_b"], dram["w1_0"],
                       dram["b1_0"], dram["w2_0"], dram["L0_ffn_b2"])
        attention_stage(nc, c, dram)
        c.stage_ends()
        moe1_stage(nc, c, dram, out)


def layouts(np, inp):
    a = {k: np.ascontiguousarray(inp[k]) for k in ("x", "adj", "L0_ffn_router_w", "L0_ffn_router_b", "L0_ffn_b2")}
    a["adj_t"] = np.ascontiguousarray(inp["adj"].T)
    a["w1_0"] = np.ascontiguousarray(inp["L0_ffn_W1"]).reshape(E0 * D, F0)
    a["w2_0"] = np.ascontiguousarray(inp["L0_ffn_W2"]).reshape(E0 * F0, D)
    a["b1_0"] = np.ascontiguousarray(inp["L0_ffn_b1"].reshape(E0 * HC0, P).T)
    a["c_ident"] = np.eye(P, dtype=np.float32)
    a["c_iota"] = np.tile(np.arange(E1, dtype=np.float32), (P, 1))
    a["w_heads"] = np.ascontiguousarray(inp["L1_gnn_W"].transpose(1, 0, 2)).reshape(D, HEADS * HID)
    a["a_rows"] = np.stack([inp["L1_gnn_a1"].reshape(-1), inp["L1_gnn_a2"].reshape(-1)])
    for j in range(4):
        a[f"enc_w{j}"] = np.ascontiguousarray(inp[f"L1_gnn_W{j + 1}"].T)
        b = inp[f"L1_gnn_b{j + 1}"]
        a[f"enc_b{j}"] = np.ascontiguousarray(b.reshape(-1, P).T) if j < 3 else np.ascontiguousarray(b)
    a["wg_t"] = np.ascontiguousarray(inp["L1_ffn_wg"].T)
    for j in (1, 2, 3):
        a[f"w{j}_1"] = np.ascontiguousarray(inp[f"L1_ffn_w{j}"]).reshape(E1 * D, D)
        a[f"sw{j}"] = np.ascontiguousarray(inp[f"L1_ffn_sw{j}"])
    a["c_before"] = np.triu(np.ones((P, P), np.float32), 1)
    a["c_ones"] = np.ones((P, P), np.float32)
    a["c_first_slot"] = np.tile(np.arange(E1, dtype=np.float32) * CAP, (P, 1))
    a["c_tokens"] = (np.arange(NT) * P + np.arange(P)[:, None]).astype(np.float32)
    a["c_no_token"] = np.full((SLOTS, 1), N, np.float32)
    return a


def kernel(**inputs):
    import numpy as _np
    import concourse.bacc as _bacc
    from concourse import mybir as _mybir
    from concourse.bass_utils import run_bass_kernel_spmd as _run

    nc = _bacc.Bacc("TRN2", target_bir_lowering=False, num_devices=1)
    arrays = {f"in_{k}": v for k, v in layouts(_np, {k: _np.asarray(v) for k, v in inputs.items()}).items()}
    dram = {k[3:]: nc.dram_tensor(k, v.shape, _mybir.dt.from_np(v.dtype), kind="ExternalInput").ap() for k, v in arrays.items()}
    out = nc.dram_tensor("out_dram", (N, D), _mybir.dt.float32, kind="ExternalOutput").ap()
    build(nc, dram, out)
    return _run(nc, [arrays], core_ids=[0]).results[0]["out_dram"]
```

```python
from contextlib import ExitStack

import numpy as np

import concourse.bass as bass
from concourse import mybir

ALU = mybir.AluOpType
ACT = mybir.ActivationFunctionType
AX = mybir.AxisListType.X
F32 = mybir.dt.float32
F32R = mybir.dt.float32r
BF16 = mybir.dt.bfloat16
U32 = mybir.dt.uint32

P = 128
N, D = 2048, 512
NT = N // P
DC = D // P
NB = 512
EPS = 1e-5

E0, F0 = 8, 256
HC0 = F0 // P
HEADS, HID = 8, 64
HP = HEADS // 2
ALPHA = 0.2
BIG = float(2**53)
NW = 1024
M1, M2, M3 = 256, 128, 256
E1, K1, G1, KG = 32, 4, 8, 4
EG = E1 // G1
LOGIT_ROWS = 32
CAP = int(1.25 * N * K1 / E1)
SLOTS = E1 * CAP
CT = [min(P, CAP - j) for j in range(0, CAP, P)]
NCT = len(CT)


PASSES = ((0, 0), (0, 1), (1, 0))


def product(pe, out, left, right, first, last):
    for n, (a, b) in enumerate(PASSES):
        mm = pe.matmul(out, left(a), right(b), start=first and n == 0, stop=last and n == len(PASSES) - 1)
    return mm


def split_tile(ctx, nc, name, shape):
    return [ctx.enter_context(nc.sbuf_tensor(f"{name}_{part}", shape, F32R)) for part in ("high", "low")]


def layernorm_block(nc, c, tag, turned_to, rows=None, store=None, zero_row=None):
    with ExitStack() as ctx:
        mv = ctx.enter_context(nc.sbuf_tensor(f"ln_mv{tag}", [P, NT, 2], F32))
        std = ctx.enter_context(nc.sbuf_tensor(f"ln_std{tag}", [P, NT], F32))
        rstd = ctx.enter_context(nc.sbuf_tensor(f"ln_rstd{tag}", [P, NT], F32))
        if rows is None:
            rows = ctx.enter_context(nc.sbuf_tensor(f"ln_rows{tag}", [P, NT, D], F32))
        banks = [ctx.enter_context(nc.psum_tensor(f"ln_ps{tag}{i}", [P, DC, P], F32)) for i in range(4)]
        var_ready = c.semaphore(f"ln_var_ready{tag}")
        std_ready = c.semaphore(f"ln_std_ready{tag}")
        rstd_ready = c.semaphore(f"ln_rstd_ready{tag}")
        rows_ready = c.semaphore(f"ln_rows_ready{tag}")
        if turned_to is not None:
            turned = c.semaphore(f"ln_turned{tag}")
            high_ready = c.semaphore(f"ln_high_ready{tag}")
            bank_free = c.semaphore(f"ln_bank_free{tag}")
        if store is not None:
            zero = ctx.enter_context(nc.sbuf_tensor(f"ln_zero{tag}", [1, D], F32))
            stored = c.semaphore(f"ln_stored{tag}")
            zeroed = c.semaphore(f"ln_zeroed{tag}")
        X = c.X
        with nc.Block() as block:

            @block.vector
            def _(dve):
                for t in range(NT):
                    dve.bn_aggr(mv[:, t, :], c.stats[:, t, :]).then_inc(var_ready, 1)
                dve.wait_ge(var_ready, NT)
                dve.tensor_scalar(std[:, :], mv[:, :, 1], EPS, None, ALU.add).then_inc(var_ready, 1)
                dve.wait_ge(std_ready, 1)
                dve.reciprocal(rstd[:, :], std[:, :]).then_inc(rstd_ready, 1)
                dve.wait_ge(rstd_ready, 1)

                def low(t):
                    dve.wait_ge(high_ready, t + 1)
                    at = slice(t * P, (t + 1) * P)
                    dve.tensor_tensor(turned_to[1][:, :, at], banks[t % 4][:, :, :], turned_to[0][:, :, at].bitcast(F32),
                                      ALU.subtract).then_inc(bank_free, 1)

                for t in range(NT):
                    dve.tensor_scalar(rows[:, t, :], X[:, t, :], mv[:, t, 0:1], rstd[:, t:t + 1],
                                      ALU.subtract, ALU.mult).then_inc(rows_ready, 1)
                    if turned_to is not None and t >= 3:
                        low(t - 3)
                if turned_to is not None:
                    for t in range(NT - 3, NT):
                        low(t)

            @block.scalar
            def _(act):
                act.wait_ge(var_ready, NT + 1)
                act.activation(std[:, :], std[:, :], ACT.Sqrt).then_inc(std_ready, 1)
                if turned_to is None:
                    return
                for t in range(NT):
                    act.wait_ge(turned, t + 1)
                    act.activation(turned_to[0][:, :, t * P:(t + 1) * P], banks[t % 4][:, :, :],
                                   ACT.Copy).then_inc(high_ready, 1)

            @block.tensor
            def _(pe):
                if turned_to is None:
                    return
                for t in range(NT):
                    pe.wait_ge(rows_ready, t + 1)
                    if t >= 4:
                        pe.wait_ge(bank_free, t - 3)
                    for k in range(DC):
                        mm = pe.transpose(banks[t % 4][:, k, :], rows[:, t, k * P:(k + 1) * P], c.ident[:, :])
                    mm.then_inc(turned, 1)

            @block.sync
            def _(sp):
                if store is None:
                    return
                for q in range(4):
                    a, b = q * NT // 4, (q + 1) * NT // 4
                    sp.wait_ge(rows_ready, b)
                    sp.dma_start(store[a * P:b * P, :].rearrange("(t p) d -> p t d", p=P), rows[:, a:b, :]).then_inc(stored, 16)
                sp.wait_ge(zeroed, 1)
                sp.dma_start(store[N:N + 1, :], zero[:, :]).then_inc(stored, 16)
                sp.dma_start(zero_row, zero[:, :]).then_inc(stored, 16)
                sp.wait_ge(stored, 96)

            @block.gpsimd
            def _(pool):
                if store is not None:
                    pool.memset(zero[:, :], 0.0).then_inc(zeroed, 1)


def start_block(nc, c, x, adj, adj_t, consts, mean, scale, dinv, pa, pb, panel_in):
    RING = 3
    PARTS = 4
    tiles = NT // PARTS
    with ExitStack() as ctx:
        a = [ctx.enter_context(nc.sbuf_tensor(f"deg_a{i}", [P, N], F32)) for i in range(RING)]
        ones = ctx.enter_context(nc.sbuf_tensor("deg_ones", [P, 1], F32))
        rows = ctx.enter_context(nc.sbuf_tensor("deg_rows", [P, NT], F32))
        column_row = ctx.enter_context(nc.sbuf_tensor("deg_column_row", [1, N], F32))
        mv = ctx.enter_context(nc.sbuf_tensor("deg_mv", [P, NT, 2], F32))
        small = ctx.enter_context(nc.sbuf_tensor("deg_small", [P, 2, NT], F32))
        pair = [ctx.enter_context(nc.sbuf_tensor(f"deg_pair{i}", [P, 2, NT], F32)) for i in range(3)]
        ps = [ctx.enter_context(nc.psum_tensor(f"deg_ps{i}", [1, NB], F32)) for i in range(N // NB)]
        columns = ctx.enter_context(nc.psum_tensor("deg_columns", [P, NT], F32))
        arrived = [c.semaphore(f"deg_arrived{i}") for i in range(RING)]
        x_in = [c.semaphore(f"deg_x_in{q}") for q in range(PARTS)]
        consts_in = c.semaphore("deg_consts_in")
        summed, columned, row_ready, turned = (c.semaphore(f"deg_{n}") for n in ("summed", "columned", "row_ready", "turned"))
        ready, chain, root, stats_ready = (c.semaphore(f"deg_{n}") for n in ("ready", "chain", "root", "stats_ready"))
        with nc.Block() as block:

            @block.sync
            def _(sp):
                for t in range(NT):
                    if t >= RING:
                        sp.wait_ge(summed, t - RING + 1)
                        sp.wait_ge(columned, t - RING + 1)
                    sp.dma_start(a[t % RING][:, :], adj[t * P:(t + 1) * P, :]).then_inc(arrived[t % RING], 16)
                    if t < PARTS:
                        at = slice(t * tiles, (t + 1) * tiles)
                        sp.dma_start(c.X[:, at, :], x.rearrange("(t p) d -> p t d", p=P)[:, at, :]).then_inc(x_in[t], 16)
                for sb, dram in consts:
                    sp.dma_start(sb[:, :], dram).then_inc(consts_in, 16)
                sp.dma_start(pa[0][:, :, :], panel_view(adj_t)[:, :, 0:P]).then_inc(panel_in[0], 16)
                sp.dma_start(pb[0][:, :, :], panel_view(adj)[:, :, 0:P]).then_inc(panel_in[0], 16)
                sp.wait_ge(consts_in, 16 * len(consts))

            @block.tensor
            def _(pe):
                pe.wait_ge(ready, 1)
                for t in range(NT):
                    pe.wait_ge(arrived[t % RING], 16 * (t // RING + 1))
                    for j in range(N // NB):
                        mm = pe.matmul(ps[j][:, :], ones[:, :], a[t % RING][:, j * NB:(j + 1) * NB], start=(t == 0), stop=(t == NT - 1))
                    mm.then_inc(columned, 1)
                pe.wait_ge(row_ready, 1)
                for j in range(NT):
                    mm = pe.matmul(columns[:, j:j + 1], column_row[:, j * P:(j + 1) * P], ones[0:1, :], start=True, stop=True)
                mm.then_inc(turned, 1)

            @block.scalar
            def _(act):
                act.wait_ge(columned, NT)
                for j in range(N // NB):
                    ins = act.activation(column_row[:, j * NB:(j + 1) * NB], ps[j][:, :], ACT.Copy)
                ins.then_inc(row_ready, 1)
                act.wait_ge(chain, ROOTS_AT)
                act.activation(pair[1][:, :, :], pair[0][:, :, :], ACT.Sqrt).then_inc(root, 1)

            @block.vector
            def _(dve):
                n = [0]

                def link(ins):
                    n[0] += 1
                    ins.then_inc(chain, 1)
                    dve.wait_ge(chain, n[0])

                dve.memset(ones[:, :], 1.0).then_inc(ready, 1)
                for t in range(NT):
                    dve.wait_ge(arrived[t % RING], 16 * (t // RING + 1))
                    dve.tensor_reduce(rows[:, t:t + 1], a[t % RING][:, :], AX, ALU.add).then_inc(summed, 1)
                    dve.wait_ge(x_in[t // tiles], 16)
                    dve.bn_stats(c.stats[:, t, :], c.X[:, t, :]).then_inc(stats_ready, 1)
                dve.wait_ge(stats_ready, NT)
                for t in range(NT):
                    ins = dve.bn_aggr(mv[:, t, :], c.stats[:, t, :])
                link(ins)
                link(dve.tensor_copy(mean[:, :], mv[:, :, 0]))
                link(dve.tensor_scalar(pair[0][:, 0, :], mv[:, :, 1], EPS, None, ALU.add))
                dve.wait_ge(summed, NT)
                dve.wait_ge(turned, 1)
                deg, above = small[:, 0, :], small[:, 1, :]
                link(dve.tensor_tensor(deg, columns[:, :], rows[:, :], ALU.add))
                link(dve.tensor_scalar(deg, deg, 0.5, 1.0, ALU.mult, ALU.add))
                link(dve.tensor_scalar(pair[0][:, 1, :], deg, 1e-30, None, ALU.max))
                assert n[0] == ROOTS_AT
                link(dve.tensor_scalar(above, deg, 0.0, None, ALU.is_gt))
                dve.wait_ge(root, 1)
                link(dve.reciprocal(pair[2][:, :, :], pair[1][:, :, :]))
                link(dve.tensor_tensor(dinv[:, :], pair[2][:, 1, :], above, ALU.mult))
                link(dve.tensor_tensor(scale[:, :], pair[2][:, 0, :], dinv[:, :], ALU.mult))


ROOTS_AT = 6


def panel_view(a):
    return a.rearrange("(k p) m -> p k m", p=P)


def symmetric_mix_block(nc, c, adj, adj_t, mean, scale, y, dinv, pa, pb, arrived, next_in):
    with ExitStack() as ctx:
        z = split_tile(ctx, nc, "ms_z", [P, NT, D])
        zf = [ctx.enter_context(nc.sbuf_tensor(f"ms_zf{i}", [P, D], F32)) for i in range(2)]
        panel = [split_tile(ctx, nc, f"ms_panel{i}", [P, NT, P]) for i in range(2)]
        half = [ctx.enter_context(nc.sbuf_tensor(f"ms_half{i}", [P, D], F32)) for i in range(2)]
        ps = [ctx.enter_context(nc.psum_tensor(f"ms_ps{i}", [P, D], F32)) for i in range(2)]
        z_ready, z_high, z_low = (c.semaphore(f"ms_{n}") for n in ("z_ready", "z_high", "z_low"))
        summed, high_ready, low_ready, multiplied, halved, added, half_free = (
            c.semaphore(f"ms_{n}") for n in ("summed", "high_ready", "low_ready", "multiplied", "halved", "added", "half_free"))
        a_v, at_v = panel_view(adj), panel_view(adj_t)
        HALF = NT // 2
        with nc.Block() as block:

            @block.sync
            def _(sp):
                def load(i, s):
                    cols = bass.ds((2 * i + s) * P, P)
                    sp.dma_start(pa[s][:, :, :], at_v[:, :, cols]).then_inc(arrived[s], 16)
                    sp.dma_start(pb[s][:, :, :], a_v[:, :, cols]).then_inc(arrived[s], 16)

                load(0, 1)
                with sp.Fori(0, HALF - 1) as i:
                    for s in range(2):
                        sp.wait_ge(low_ready, 2 * i + s + 1)
                        load(i + 1, s)
                for s in range(2):
                    sp.wait_ge(low_ready, NT - 1 + s)
                    sp.dma_start(pa[s][:, :, :], at_v[:, :, s * P:(s + 1) * P]).then_inc(next_in[s], 16)

            @block.vector
            def _(dve):
                def prepare(i, s):
                    dve.wait_ge(arrived[s], 32 * i + 32)
                    dve.tensor_tensor(pa[s][:, :, :], pa[s][:, :, :], pb[s][:, :, :], ALU.add).then_inc(summed, 1)
                    dve.wait_ge(high_ready, 2 * i + s + 1)
                    dve.tensor_tensor(panel[s][1][:, :, :], pa[s][:, :, :], panel[s][0][:, :, :].bitcast(F32), ALU.subtract).then_inc(low_ready, 1)

                def finish(i, s):
                    t = 2 * i + s
                    dve.wait_ge(multiplied, t + 1)
                    dve.wait_ge(half_free, t + 1)
                    dve.scalar_tensor_tensor(out=half[s][:, :], in0=ps[s][:, :], scalar=0.5, in1=z[1][:, t, :].bitcast(F32),
                                             op0=ALU.mult, op1=ALU.add).then_inc(halved, 1)
                    dve.wait_ge(halved, t + 1)
                    dve.tensor_tensor(half[s][:, :], half[s][:, :], z[0][:, t, :].bitcast(F32), ALU.add).then_inc(added, 1)

                def rest(t):
                    dve.wait_ge(z_high, t + 1)
                    dve.tensor_tensor(z[1][:, t, :], zf[t % 2][:, :], z[0][:, t, :].bitcast(F32), ALU.subtract).then_inc(z_low, 1)

                prepare(0, 0)
                for t in range(NT):
                    if t >= 2:
                        dve.wait_ge(z_low, t - 1)
                    dve.tensor_scalar(zf[t % 2][:, :], c.X[:, t, :], mean[:, t:t + 1], scale[:, t:t + 1],
                                      ALU.subtract, ALU.mult).then_inc(z_ready, 1)
                    if t:
                        rest(t - 1)
                rest(NT - 1)
                prepare(0, 1)
                with dve.Fori(0, HALF - 1) as i:
                    for s in range(2):
                        finish(i, s)
                        prepare(i + 1, s)
                for s in range(2):
                    finish(HALF - 1, s)

            @block.scalar
            def _(act):
                act.sem_inc(half_free, 2)

                def high(i, s):
                    act.wait_ge(summed, 2 * i + s + 1)
                    act.activation(panel[s][0][:, :, :], pa[s][:, :, :], ACT.Copy).then_inc(high_ready, 1)

                def scale_rows(i, s):
                    act.wait_ge(arrived[s], 32)
                    act.wait_ge(added, 2 * i + s + 1)
                    act.sem_inc(c.passed, 1)
                    act.activation(y[:, 2 * i + s, :], half[s][:, :], ACT.Copy,
                                   scale=dinv[:, bass.ds(2 * i + s, 1)]).then_inc(half_free, 1)

                high(0, 0)
                for t in range(NT):
                    act.wait_ge(z_ready, t + 1)
                    act.activation(z[0][:, t, :], zf[t % 2][:, :], ACT.Copy).then_inc(z_high, 1)
                high(0, 1)
                with act.Fori(0, HALF - 1) as i:
                    for s in range(2):
                        scale_rows(i, s)
                        high(i + 1, s)
                for s in range(2):
                    scale_rows(HALF - 1, s)

            @block.tensor
            def _(pe):
                def column(i, s, first):
                    pe.wait_ge(low_ready, 2 * i + s + 1)
                    for k in range(NT):
                        if first:
                            pe.wait_ge(z_low, k + 1)
                        mm = product(pe, ps[s][:, :], lambda a: panel[s][a][:, k, :], lambda b: z[b][:, k, :], k == 0, k == NT - 1)
                    mm.then_inc(multiplied, 1)

                column(0, 0, True)
                column(0, 1, False)
                with pe.Fori(1, HALF) as i:
                    for s in range(2):
                        column(i, s, False)


def mix_block(nc, c, adj_t, y, raw, arrived):
    with ExitStack() as ctx:
        panel = [split_tile(ctx, nc, f"ma_panel{i}", [P, NT, P]) for i in range(2)]
        ys = split_tile(ctx, nc, "ma_y", [P, NT, D])
        ps = [ctx.enter_context(nc.psum_tensor(f"ma_ps{i}", [P, D], F32)) for i in range(2)]
        y_high, y_low, high_ready, low_ready, multiplied, bank_free, stats_ready = (
            c.semaphore(f"ma_{n}") for n in ("y_high", "y_low", "high_ready", "low_ready", "multiplied", "bank_free", "stats_ready"))
        at_v = panel_view(adj_t)
        HALF = NT // 2
        with nc.Block() as block:

            @block.sync
            def _(sp):
                def load(i, s):
                    sp.dma_start(raw[s][:, :, :], at_v[:, :, bass.ds((2 * i + s) * P, P)]).then_inc(arrived[s], 16)

                with sp.Fori(0, HALF - 1) as i:
                    for s in range(2):
                        sp.wait_ge(low_ready, 2 * i + s + 1)
                        load(i + 1, s)

            @block.vector
            def _(dve):
                def low(i, s):
                    dve.wait_ge(high_ready, 2 * i + s + 1)
                    dve.tensor_tensor(panel[s][1][:, :, :], raw[s][:, :, :], panel[s][0][:, :, :].bitcast(F32), ALU.subtract).then_inc(low_ready, 1)

                def add(i, s):
                    dve.wait_ge(multiplied, 2 * i + s + 1)
                    dve.tensor_tensor(c.X[:, 2 * i + s, :], ps[s][:, :], c.X[:, 2 * i + s, :], ALU.add).then_inc(bank_free, 1)

                low(0, 0)
                for t in range(NT):
                    dve.wait_ge(y_high, t + 1)
                    dve.tensor_tensor(ys[1][:, t, :], y[:, t, :], ys[0][:, t, :].bitcast(F32), ALU.subtract).then_inc(y_low, 1)
                low(0, 1)
                with dve.Fori(0, HALF - 1) as i:
                    for s in range(2):
                        add(i, s)
                        low(i + 1, s)
                dve.wait_ge(bank_free, NT - 2)
                for t in range(NT - 2):
                    dve.bn_stats(c.stats[:, t, :], c.X[:, t, :]).then_inc(stats_ready, 1)
                for s in range(2):
                    add(HALF - 1, s)
                    dve.wait_ge(bank_free, NT - 1 + s)
                    dve.bn_stats(c.stats[:, NT - 2 + s, :], c.X[:, NT - 2 + s, :]).then_inc(stats_ready, 1)

            @block.scalar
            def _(act):
                def high(i, s):
                    act.wait_ge(arrived[s], 16 * i + 16)
                    act.activation(panel[s][0][:, :, :], raw[s][:, :, :], ACT.Copy).then_inc(high_ready, 1)

                high(0, 0)
                for t in range(NT):
                    act.activation(ys[0][:, t, :], y[:, t, :], ACT.Copy).then_inc(y_high, 1)
                high(0, 1)
                with act.Fori(0, HALF - 1) as i:
                    for s in range(2):
                        act.wait_ge(multiplied, 2 * i + s + 1)
                        high(i + 1, s)

            @block.tensor
            def _(pe):
                def column(i, s, first):
                    pe.wait_ge(low_ready, 2 * i + s + 1)
                    for k in range(NT):
                        if first:
                            pe.wait_ge(y_low, k + 1)
                        mm = product(pe, ps[s][:, :], lambda a: panel[s][a][:, k, :], lambda b: ys[b][:, k, :], k == 0, k == NT - 1)
                    mm.then_inc(multiplied, 1)

                column(0, 0, True)
                column(0, 1, False)
                with pe.Fori(1, HALF) as i:
                    for s in range(2):
                        column(i, s, False)


def logits_pe(pe, c, w, w_ready, xt, banks, product_ready, turned_sb, copied, out, ready):
    pe.wait_ge(w_ready, 1)
    for q in range(N // NB):
        for k in range(DC):
            mm = product(pe, banks[q][:, :], lambda a: w[a][:, k, :], lambda b: xt[b][:, k, q * NB:(q + 1) * NB], k == 0, k == DC - 1)
        mm.then_inc(product_ready, 1)
    for t in range(NT):
        pe.wait_ge(copied, t // (NB // P) + 1)
        to = out[:, t * LOGIT_ROWS:(t + 1) * LOGIT_ROWS]
        mm = pe.transpose(to, turned_sb[:, t * P:(t + 1) * P], c.ident[0:LOGIT_ROWS, 0:LOGIT_ROWS])
    mm.then_inc(ready, 1)


def logits_act(act, banks, product_ready, turned_sb, copied):
    for q in range(N // NB):
        act.wait_ge(product_ready, q + 1)
        act.activation(turned_sb[:, q * NB:(q + 1) * NB], banks[q][0:LOGIT_ROWS, :], ACT.Copy).then_inc(copied, 1)


def moe0_block(nc, c, xt, router_w, router_b, w1, b1, w2, b2):
    with ExitStack() as ctx:
        def sb(name, shape, dt=F32):
            return ctx.enter_context(nc.sbuf_tensor(f"m0_{name}", shape, dt))
        rw = sb("rw", [P, DC, P])
        rb = sb("rb", [P, E0])
        b1s = sb("b1", [P, E0 * HC0])
        b2s = sb("b2", [E0, D])
        rws = split_tile(ctx, nc, "m0_rws", [P, DC, P])
        raw = [sb("raw_w1", [P, DC, F0]), sb("raw_w2", [P, HC0, D])]
        w1s = [split_tile(ctx, nc, f"m0_w1_{i}", [P, DC, F0]) for i in range(2)]
        w2s = [split_tile(ctx, nc, f"m0_w2_{i}", [P, HC0, D]) for i in range(2)]
        act_out = [sb(f"act_out{i}", [P, HC0, NB]) for i in range(2)]
        ht = [split_tile(ctx, nc, f"m0_ht{i}", [P, HC0, NB]) for i in range(2)]
        lg = sb("lg", [P, NT, E0])
        ex = sb("ex", [P, NT, E0])
        top = sb("top", [P, NT, 8])
        idx = sb("idx", [P, NT, 8], U32)
        idf = sb("idf", [P, NT, 8])
        sel = sb("sel", [P, NT, E0])
        sel2 = sb("sel2", [P, NT, E0])
        col = sb("col", [P, NT])
        R = sb("R", [P, E0 * NT])
        RT = sb("RT", [LOGIT_ROWS, N])
        psh = [ctx.enter_context(nc.psum_tensor(f"m0_h{i}", [P, NB], F32)) for i in range(4)]
        pso = [ctx.enter_context(nc.psum_tensor(f"m0_o{i}", [P, NB], F32)) for i in range(4)]
        s = lambda name: c.semaphore(f"m0_{name}")
        small_in, logits, chain, expd = s("small_in"), s("logits"), s("chain"), s("expd")
        turned, rt_ready = s("turned"), s("rt_ready")
        w_in = [s("w_in0"), s("w_in1")]
        h_ready, gelued, hh_ready, h_done, o_ready, o_free = (s(n) for n in ("h_ready", "gelued", "hh_ready", "h_done", "o_ready", "o_free"))
        stats_ready, rw_zeroed, logits_t, lt_copied = s("stats_ready"), s("rw_zeroed"), s("logits_t"), s("lt_copied")
        rh_ready, rl_ready, wh_ready, wl_ready = (s(n) for n in ("rh_ready", "rl_ready", "wh_ready", "wl_ready"))
        NBS = N // NB
        TPB = NB // P
        STEPS = 2 * NBS
        with nc.Block() as block:

            @block.sync
            def _(sp):
                sp.wait_ge(rw_zeroed, 1)
                sp.dma_start(rw[:, :, 0:E0], router_w.rearrange("(k p) e -> p k e", p=P)).then_inc(small_in, 16)
                sp.dma_start(rb[:, :], router_b.rearrange("(a e) -> a e", a=1).broadcast_to([P, E0])).then_inc(small_in, 16)
                sp.dma_start(b1s[:, :], b1).then_inc(small_in, 16)
                sp.dma_start(b2s[:, :], b2).then_inc(small_in, 16)

                def load(e, j):
                    rows = (D, F0)[j]
                    sp.dma_start(raw[j][:, :, :], (w1, w2)[j][bass.ds(e * rows, rows), :].rearrange("(k p) f -> p k f", p=P)).then_inc(w_in[j], 16)

                load(0, 0)
                load(0, 1)
                with sp.Fori(0, E0 - 1) as e:
                    for j in range(2):
                        sp.wait_ge(wl_ready, 2 * e + j + 1)
                        load(e + 1, j)

            @block.tensor
            def _(pe):
                pe.wait_ge(small_in, 64)
                logits_pe(pe, c, rws, rl_ready, xt, psh, logits_t, RT, lt_copied, pso[0], logits)
                pe.wait_ge(chain, 13)
                for t in range(NT):
                    mm = pe.transpose(psh[t // TPB][0:E0, (t % TPB) * P:(t % TPB + 1) * P],
                                      R[:, :].rearrange("p (e t) -> p t e", t=NT)[:, t, :], c.ident[:, :])
                mm.then_inc(turned, 1)
                pe.wait_ge(rt_ready, 1)
                for t in range(NT):
                    pe.wait_ge(o_free, t + 1)
                    pe.matmul(pso[t % 4][:, :], RT[0:E0, t * P:(t + 1) * P], b2s[:, :],
                              start=True, stop=True).then_inc(o_ready, 1)

                def hidden(i, v):
                    u, nb = v // NBS, v % NBS
                    if nb == 0:
                        pe.wait_ge(wl_ready, 2 * (2 * i + u) + 2)
                    for h in range(HC0):
                        pe.wait_ge(gelued, (STEPS * i + v) * HC0 + h + 1)
                        for k in range(DC):
                            mm = product(pe, psh[(v % 2) * HC0 + h][:, :], lambda a: w1s[u][a][:, k, h * P:(h + 1) * P],
                                         lambda b: xt[b][:, k, nb * NB:(nb + 1) * NB], k == 0, k == DC - 1)
                        mm.then_inc(h_ready, 1)

                def outs(i, v):
                    u, nb = v // NBS, v % NBS
                    pe.wait_ge(h_done, (STEPS * i + v + 1) * HC0)
                    for j in range(TPB):
                        pe.wait_ge(o_free, NT + (STEPS * i + v) * TPB + j + 1)
                        for h in range(HC0):
                            mm = product(pe, pso[j][:, :], lambda a: ht[v % 2][a][:, h, j * P:(j + 1) * P],
                                         lambda b: w2s[u][b][:, h, :], h == 0, h == HC0 - 1)
                        mm.then_inc(o_ready, 1)

                with pe.Fori(0, E0 // 2) as i:
                    for v in range(STEPS):
                        hidden(i, v)
                        if v:
                            outs(i, v - 1)
                    outs(i, STEPS - 1)

            @block.scalar
            def _(act):
                act.wait_ge(small_in, 64)
                act.activation(rws[0][:, :, :], rw[:, :, :], ACT.Copy).then_inc(rh_ready, 1)
                logits_act(act, psh, logits_t, RT, lt_copied)
                act.wait_ge(chain, 3)
                act.activation(ex[:, :, :], lg[:, :, :], ACT.Exp).then_inc(expd, 1)
                act.wait_ge(turned, 1)
                for q in range(4):
                    ins = act.activation(RT[0:E0, q * NB:(q + 1) * NB], psh[q][0:E0, :], ACT.Copy)
                ins.then_inc(rt_ready, 1)
                act.sem_inc(gelued, 2 * HC0)

                def high(i, u, j):
                    act.wait_ge(w_in[j], 16 * (2 * i + u) + 16)
                    act.activation((w1s, w2s)[j][u][0][:, :, :], raw[j][:, :, :], ACT.Copy).then_inc(wh_ready, 1)

                def body(i, last):
                    for v in range(STEPS):
                        g = STEPS * i + v
                        for h in range(HC0):
                            act.wait_ge(small_in, 64)
                            act.wait_ge(h_ready, g * HC0 + h + 1)
                            act.sem_inc(c.passed, 1)
                            bias = b1s[:, bass.ds((2 * i + v // NBS) * HC0 + h, 1)]
                            act.activation(act_out[v % 2][:, h, :], psh[(v % 2) * HC0 + h][:, :], ACT.Gelu,
                                           bias=bias).then_inc(gelued, 1)
                        u, j = v // NBS, v % NBS - 1
                        if j in (0, 1) and not (last and u):
                            act.wait_ge(o_ready, NT + (g - j - 1) * TPB)
                            high(i + u, 1 - u, j)

                high(0, 0, 0)
                high(0, 0, 1)
                with act.Fori(0, E0 // 2 - 1) as i:
                    body(i, False)
                body(E0 // 2 - 1, True)

            @block.vector
            def _(dve):
                dve.sem_inc(o_free, 4)
                n = [0]

                def link(ins):
                    n[0] += 1
                    ins.then_inc(chain, 1)
                    dve.wait_ge(chain, n[0])

                dve.memset(rw[:, :, :], 0.0).then_inc(rw_zeroed, 1)
                dve.wait_ge(rh_ready, 1)
                dve.tensor_tensor(rws[1][:, :, :], rw[:, :, :], rws[0][:, :, :].bitcast(F32), ALU.subtract).then_inc(rl_ready, 1)
                dve.wait_ge(small_in, 64)
                dve.wait_ge(logits, 1)
                link(dve.tensor_tensor(lg[:, :, :], pso[0][:, :].rearrange("p (t e) -> p t e", e=LOGIT_ROWS)[:, :, 0:E0],
                                       rb[:, :].unsqueeze(1).broadcast_to([P, NT, E0]), ALU.add))
                link(dve.tensor_reduce(col[:, :], lg[:, :, :], AX, ALU.max))
                link(dve.tensor_tensor(lg[:, :, :], lg[:, :, :], col[:, :].unsqueeze(2).broadcast_to([P, NT, E0]), ALU.subtract))
                dve.wait_ge(expd, 1)
                for t in range(NT):
                    ins = dve.max(top[:, t, :], ex[:, t, :])
                link(ins)
                for t in range(NT):
                    ins = dve.max_index(idx[:, t, :], top[:, t, :], ex[:, t, :])
                link(ins)
                link(dve.tensor_copy(idf[:, :, :], idx[:, :, :]))
                iota = c.iota[:, 0:E0].unsqueeze(1).broadcast_to([P, NT, E0])
                link(dve.tensor_tensor(sel[:, :, :], iota, idf[:, :, 0:1].broadcast_to([P, NT, E0]), ALU.is_equal))
                link(dve.tensor_tensor(sel2[:, :, :], iota, idf[:, :, 1:2].broadcast_to([P, NT, E0]), ALU.is_equal))
                link(dve.tensor_tensor(sel[:, :, :], sel[:, :, :], sel2[:, :, :], ALU.add))
                link(dve.tensor_tensor(sel[:, :, :], sel[:, :, :], ex[:, :, :], ALU.mult))
                link(dve.tensor_tensor(col[:, :], top[:, :, 0], top[:, :, 1], ALU.add))
                link(dve.reciprocal(col[:, :], col[:, :]))
                link(dve.tensor_tensor(R[:, :].rearrange("p (e t) -> p t e", t=NT), sel[:, :, :],
                                       col[:, :].unsqueeze(2).broadcast_to([P, NT, E0]), ALU.mult))
                assert n[0] == 13
                for t in range(NT):
                    dve.wait_ge(o_ready, t + 1)
                    dve.tensor_tensor(c.X[:, t, :], pso[t % 4][:, :], c.X[:, t, :], ALU.add).then_inc(o_free, 1)

                def low(i, u, j):
                    dve.wait_ge(wh_ready, 2 * (2 * i + u) + j + 1)
                    parts = (w1s, w2s)[j][u]
                    dve.tensor_tensor(parts[1][:, :, :], raw[j][:, :, :], parts[0][:, :, :].bitcast(F32), ALU.subtract).then_inc(wl_ready, 1)

                def parts(i, v):
                    g = STEPS * i + v
                    high, rest = ht[v % 2]
                    for h in range(HC0):
                        dve.wait_ge(gelued, (g + 2) * HC0 + h + 1)
                        dve.wait_ge(o_ready, NT + (g - 1) * TPB)
                        dve.tensor_copy(high[:, h, :], act_out[v % 2][:, h, :]).then_inc(hh_ready, 1)
                        dve.wait_ge(hh_ready, g * HC0 + h + 1)
                        dve.tensor_tensor(rest[:, h, :], act_out[v % 2][:, h, :], high[:, h, :].bitcast(F32), ALU.subtract).then_inc(h_done, 1)

                def add(i, v):
                    for j in range(TPB):
                        t = (v % NBS) * TPB + j
                        at = NT + (STEPS * i + v) * TPB + j
                        dve.wait_ge(o_ready, at + 1)
                        dve.wait_ge(o_free, at + 4 - NT + 1)
                        dve.scalar_tensor_tensor(out=c.X[:, t, :], in0=pso[j][:, :],
                                                 scalar=R[:, bass.ds((2 * i + v // NBS) * NT + t, 1)],
                                                 in1=c.X[:, t, :], op0=ALU.mult, op1=ALU.add).then_inc(o_free, 1)

                def statistics(nb):
                    dve.wait_ge(o_free, NT + (STEPS * (E0 // 2 - 1) + NBS + nb + 1) * TPB + 4)
                    for t in range(nb * TPB, (nb + 1) * TPB):
                        dve.bn_stats(c.stats[:, t, :], c.X[:, t, :]).then_inc(stats_ready, 1)

                def body(i, last):
                    for v in range(STEPS):
                        parts(i, v)
                        if v:
                            add(i, v - 1)
                        if last and v > NBS:
                            statistics(v - 1 - NBS)
                        u, j = v // NBS, v % NBS - 1
                        if j in (0, 1) and not (last and u):
                            low(i + u, 1 - u, j)
                    add(i, STEPS - 1)

                low(0, 0, 0)
                low(0, 0, 1)
                with dve.Fori(0, E0 // 2 - 1) as i:
                    body(i, False)
                body(E0 // 2 - 1, True)
                statistics(NBS - 1)


def project_block(nc, c, xt, w, a_rows, wh, wh_dram, src, dst):
    with ExitStack() as ctx:
        raw = ctx.enter_context(nc.sbuf_tensor("pr_raw", [P, DC, D], F32))
        ws = split_tile(ctx, nc, "pr_w", [P, DC, D])
        ar = ctx.enter_context(nc.sbuf_tensor("pr_a", [P, 2, D], F32))
        prod = [ctx.enter_context(nc.sbuf_tensor(f"pr_prod{i}", [P, D], F32)) for i in range(2)]
        ps = [ctx.enter_context(nc.psum_tensor(f"pr_ps{i}", [P, D], F32)) for i in range(4)]
        arrived, done, copied = (c.semaphore(f"pr_{n}") for n in ("arrived", "done", "copied"))
        multiplied, reduced = (c.semaphore(f"pr_{n}") for n in ("multiplied", "reduced"))
        high_ready, low_ready, stored = (c.semaphore(f"pr_{n}") for n in ("high_ready", "low_ready", "stored"))
        with nc.Block() as block:

            @block.sync
            def _(sp):
                sp.dma_start(raw[:, :, :], w.rearrange("(k p) f -> p k f", p=P)).then_inc(arrived, 16)
                for j in range(2):
                    sp.dma_start(ar[:, j, :], a_rows[j:j + 1, :].broadcast_to([P, D])).then_inc(arrived, 16)
                for q in range(4):
                    a, b = q * NT // 4, (q + 1) * NT // 4
                    sp.wait_ge(copied, b)
                    sp.dma_start(wh_dram.rearrange("(t p) d -> p t d", p=P)[:, a:b, :], wh[:, a:b, :]).then_inc(stored, 16)
                sp.wait_ge(stored, 64)

            @block.tensor
            def _(pe):
                pe.wait_ge(low_ready, 1)
                for t in range(NT):
                    if t >= 4:
                        pe.wait_ge(copied, t - 3)
                    for k in range(DC):
                        mm = product(pe, ps[t % 4][:, :], lambda a: xt[a][:, k, t * P:(t + 1) * P], lambda b: ws[b][:, k, :],
                                     k == 0, k == DC - 1)
                    mm.then_inc(done, 1)

            @block.scalar
            def _(act):
                act.wait_ge(arrived, 48)
                act.activation(ws[0][:, :, :], raw[:, :, :], ACT.Copy).then_inc(high_ready, 1)
                for t in range(NT):
                    act.wait_ge(done, t + 1)
                    act.activation(wh[:, t, 0:D], ps[t % 4][:, :], ACT.Copy)
                    act.activation(wh[:, t, D:D + HID], ps[t % 4][:, 0:HID], ACT.Copy).then_inc(copied, 1)

            @block.vector
            def _(dve):
                dve.wait_ge(high_ready, 1)
                dve.tensor_tensor(ws[1][:, :, :], raw[:, :, :], ws[0][:, :, :].bitcast(F32), ALU.subtract).then_inc(low_ready, 1)
                for t in range(NT):
                    dve.wait_ge(copied, t + 1)
                    for j, to in enumerate((src, dst)):
                        m = 2 * t + j
                        if m >= 2:
                            dve.wait_ge(reduced, m - 1)
                        dve.tensor_tensor(prod[j][:, :], wh[:, t, 0:D], ar[:, j, :], ALU.mult).then_inc(multiplied, 1)
                    for j, to in enumerate((src, dst)):
                        dve.wait_ge(multiplied, 2 * t + j + 1)
                        dve.tensor_reduce(to[:, :, t], prod[j][:, :].rearrange("p (h d) -> p h d", d=HID), AX,
                                          ALU.add).then_inc(reduced, 1)


def rows_out(nc, c, ctx, tag, parts):
    sbs = [ctx.enter_context(nc.sbuf_tensor(f"rows{tag}{j}", [f.shape[1], N], dt)) for j, (f, dt, _) in enumerate(parts)]
    banks = [ctx.enter_context(nc.psum_tensor(f"rows{tag}_ps{i}", [32, NB], F32)) for i in range(4)]
    turned, copied, stored = (c.semaphore(f"rows{tag}_{n}") for n in ("turned", "copied", "stored"))
    with nc.Block() as block:

        @block.tensor
        def _(pe):
            for j, (f, _, _) in enumerate(parts):
                r = f.shape[1]
                for q in range(N // NB):
                    if j:
                        pe.wait_ge(copied, (j - 1) * (N // NB) + q + 1)
                    for m in range(NB // P):
                        mm = pe.transpose(banks[q][0:r, m * P:(m + 1) * P], f[:, :, q * (NB // P) + m], c.ident[:, :])
                    mm.then_inc(turned, 1)

        @block.vector
        def _(dve):
            for j, (f, _, _) in enumerate(parts):
                r = f.shape[1]
                for q in range(N // NB):
                    dve.wait_ge(turned, j * (N // NB) + q + 1)
                    dve.tensor_copy(sbs[j][:, q * NB:(q + 1) * NB], banks[q][0:r, :]).then_inc(copied, 1)

        @block.sync
        def _(sp):
            for j, (_, _, to) in enumerate(parts):
                sp.wait_ge(copied, (j + 1) * (N // NB))
                sp.dma_start(to, sbs[j][:, :]).then_inc(stored, 16)
            sp.wait_ge(stored, 16 * len(parts))


def neighbour_max_block(nc, c, adj, adj_t, dst_rows, maxd, mask):
    with ExitStack() as ctx:
        dst_bc = ctx.enter_context(nc.sbuf_tensor("nm_dst", [P, HEADS, N], F32))
        a = [ctx.enter_context(nc.sbuf_tensor(f"nm_a{i}", [P, N], F32)) for i in range(2)]
        at = [ctx.enter_context(nc.sbuf_tensor(f"nm_at{i}", [P, N], F32)) for i in range(2)]
        masks = [ctx.enter_context(nc.sbuf_tensor(f"nm_mask{i}", [P, N], BF16)) for i in range(2)]
        sums = [ctx.enter_context(nc.psum_tensor(f"nm_sums{i}", [P, N], F32)) for i in range(2)]
        acc = [ctx.enter_context(nc.sbuf_tensor(f"nm_acc{i}", [P, HEADS], F32)) for i in range(2)]
        dst_in = [c.semaphore(f"nm_dst_in{h}") for h in range(HEADS)]
        a_in = [c.semaphore(f"nm_a_in{i}") for i in range(2)]
        at_in = [c.semaphore(f"nm_at_in{i}") for i in range(2)]
        signed, masked, signed_t, masked_t, maxed, kept = (
            c.semaphore(f"nm_{n}") for n in ("signed", "masked", "signed_t", "masked_t", "maxed", "kept"))
        with nc.Block() as block:

            @block.sync
            def _(sp):
                def load(t, s):
                    sp.dma_start(a[s][:, :], adj[bass.ds(t * P, P), :]).then_inc(a_in[s], 16)

                def load_t(t, s):
                    sp.dma_start(at[s][:, :], adj_t[bass.ds(t * P, P), :]).then_inc(at_in[s], 16)

                load(0, 0)
                for h in range(HEADS):
                    sp.dma_start(dst_bc[:, h, :], dst_rows[h:h + 1, :].broadcast_to([P, N])).then_inc(dst_in[h], 16)
                    if h == HEADS // 2:
                        load(1, 1)
                load_t(0, 0)
                load_t(1, 1)
                with sp.Fori(0, NT // 2 - 1) as i:
                    for s in range(2):
                        sp.wait_ge(signed, 2 * i + s + 1)
                        load(2 * i + 2 + s, s)
                        sp.wait_ge(signed_t, 2 * i + s + 1)
                        load_t(2 * i + 2 + s, s)

            @block.scalar
            def _(act):
                act.sem_inc(maxed, 2 * HEADS)

                def mask_rows(i, s):
                    t = 2 * i + s
                    act.wait_ge(maxed, HEADS * (t + 1))
                    act.sem_inc(c.passed, 1)
                    act.wait_ge(a_in[s], 16 * i + 16)
                    act.activation(masks[s][:, :], a[s][:, :], ACT.Sign).then_inc(signed, 1)
                    act.wait_ge(signed, t + 1)
                    act.activation(masks[s][:, :], masks[s][:, :], ACT.Copy, scale=BIG / ALPHA, bias=-BIG / ALPHA).then_inc(masked, 1)

                def mask_columns(i, s):
                    t = 2 * i + s
                    act.wait_ge(at_in[s], 16 * i + 16)
                    act.sem_inc(c.passed, 1)
                    act.activation(mask[:, bass.ds(t, 1), :], at[s][:, :].unsqueeze(1), ACT.Sign).then_inc(signed_t, 1)
                    act.wait_ge(signed_t, t + 1)
                    act.sem_inc(c.passed, 1)
                    act.activation(mask[:, bass.ds(t, 1), :], mask[:, bass.ds(t, 1), :], ACT.Copy, scale=BIG, bias=-BIG).then_inc(masked_t, 1)

                mask_rows(0, 0)
                with act.Fori(0, NT // 2 - 1) as i:
                    mask_rows(i, 1)
                    mask_columns(i, 0)
                    mask_rows(i + 1, 0)
                    mask_columns(i, 1)
                mask_rows(NT // 2 - 1, 1)
                mask_columns(NT // 2 - 1, 0)
                mask_columns(NT // 2 - 1, 1)

            @block.vector
            def _(dve):
                with dve.Fori(0, NT // 2) as i:
                    for s in range(2):
                        t = 2 * i + s
                        for h in range(HEADS):
                            dve.wait_ge(dst_in[h], 16)
                            if h == 0:
                                dve.wait_ge(masked, t + 1)
                            dve.wait_ge(maxed, (t + 2) * HEADS + h - 1)
                            dve.sem_inc(c.passed, 1)
                            dve.tensor_tensor_reduce(out=sums[h % 2][:, :], in0=dst_bc[:, h, :], in1=masks[s][:, :], scale=1.0,
                                                     scalar=-3.0e38, op0=ALU.add, op1=ALU.max,
                                                     accum_out=acc[s][:, h:h + 1]).then_inc(maxed, 1)
                        dve.wait_ge(maxed, (t + 3) * HEADS)
                        dve.tensor_copy(maxd[:, :, bass.ds(t, 1)], acc[s][:, :].unsqueeze(2)).then_inc(kept, 1)


def row_terms_block(nc, c, src, dst, maxd, s8, d8, v, wh_dram, wh, wh_in):
    with ExitStack() as ctx:
        s = ctx.enter_context(nc.sbuf_tensor("rt_s", [P, HEADS, NT], F32))
        m = ctx.enter_context(nc.sbuf_tensor("rt_m", [P, HEADS, NT], F32))
        chain = c.semaphore("rt_chain")
        with nc.Block() as block:

            @block.sync
            def _(sp):
                sp.dma_start(wh[:, :, :], wh_dram.rearrange("(t p) d -> p t d", p=P)).then_inc(wh_in, 16)

            @block.vector
            def _(dve):
                n = [0]

                def link(ins):
                    n[0] += 1
                    ins.then_inc(chain, 1)
                    dve.wait_ge(chain, n[0])

                al = lambda t: t[:, :, :]
                link(dve.tensor_tensor(al(s), al(src), al(maxd), ALU.add))
                link(dve.scalar_tensor_tensor(out=al(m), in0=al(s), scalar=ALPHA, in1=al(s), op0=ALU.mult, op1=ALU.max))
                link(dve.scalar_tensor_tensor(out=al(v), in0=al(src), scalar=ALPHA, in1=al(m), op0=ALU.mult, op1=ALU.subtract))
                link(dve.tensor_scalar(al(s8), al(src), 1.0 - ALPHA, None, ALU.mult))
                link(dve.tensor_scalar(al(d8), al(dst), ALPHA - 1.0, None, ALU.mult))


def attention_block(nc, c, mask, wh, wh_in, dst, d8, s8_rows, v_rows, sums, weights):
    MASK_STEPS = 4
    POOLED = MASK_STEPS - 1
    TAIL_AT, NEXT_AT = 6, 8
    with ExitStack() as ctx:
        def sb(name, shape, dt=F32):
            return ctx.enter_context(nc.sbuf_tensor(f"at_{name}", shape, dt))
        arg = [sb(f"arg{i}", [P, NW])[:, :] for i in range(4)]
        pr = [sb(f"pr{i}", [P, NW])[:, :] for i in range(4)]
        whc = [sb(f"whc{i}", [P, NT, P]) for i in range(2)]
        s8 = [sb(f"s8_{i}", [P, NW]) for i in range(2)]
        vb = [sb(f"v{i}", [P, NW]) for i in range(2)]
        stage = [sb(f"stage{i}", [P, NW]) for i in range(2)]
        pso = [ctx.enter_context(nc.psum_tensor(f"at_pso{i}", [P, NW], F32)) for i in range(2)]
        s = lambda name: c.semaphore(f"at_{name}")
        rows_in = [s("rows_in0"), s("rows_in1")]
        zero_ready, ones_ready, whc_ready = s("zero_ready"), s("ones_ready"), s("whc_ready")
        arg_ready, pooled, self_masked, pr_ready, pr_used = s("arg_ready"), s("pooled"), s("self_masked"), s("pr_ready"), s("pr_used")
        pso_free, staged, stage_free, stored = s("pso_free"), s("staged"), s("stage_free"), s("stored")
        NBW = N // NW
        W2 = NW // NB
        PAIR = 2 * NT
        order = [(b, h) for b in range(NBW) for h in range(HEADS)]
        flat = lambda a: a[:, :, :].rearrange("p h t -> p (h t)")
        with nc.Block() as block:

            @block.sync
            def _(sp):
                sp.sem_inc(stage_free, 3)

                def store(n):
                    b, h = order[n]
                    mine, other = (n % 2) * HID, (1 - n % 2) * HID
                    sp.wait_ge(staged, n + 2)
                    sp.dma_start(sums[n * HID:(n + 1) * HID, :], stage[n % 2][mine:mine + HID, :]).then_inc(stored, 16)
                    sp.dma_start(weights[n:n + 1, :], stage[n % 2][other:other + 1, :]).then_inc(stored, 16)
                    sp.wait_ge(stored, 32 * (n + 1))
                    sp.sem_inc(stage_free, 1)

                for n, (b, h) in enumerate(order):
                    if n >= 2:
                        sp.wait_ge(arg_ready, NT * (n - 1))
                    cols = slice(b * NW, (b + 1) * NW)
                    sp.dma_start(s8[n % 2][:, :], s8_rows[h:h + 1, cols].broadcast_to([P, NW])).then_inc(rows_in[n % 2], 16)
                    sp.dma_start(vb[n % 2][:, :], v_rows[h:h + 1, cols].broadcast_to([P, NW])).then_inc(rows_in[n % 2], 16)
                    if n >= 2:
                        store(n - 2)
                for n in range(len(order) - 2, len(order)):
                    store(n)

            @block.gpsimd
            def _(pool):
                pool.memset(whc[0][:, :, HID:P], 1.0).then_inc(ones_ready, 1)
                pool.memset(whc[1][:, :, 0:HID], 1.0).then_inc(ones_ready, 1)
                with pool.Fori(0, NBW) as b:
                    with pool.Fori(0, HP) as i:
                        for k in range(PAIR):
                            if k % MASK_STEPS == POOLED:
                                continue
                            pool.wait_ge(arg_ready, PAIR * (HP * b + i) + k + 1)
                            pool.sem_inc(c.passed, 1)
                            pool.tensor_tensor(arg[k % 4], arg[k % 4], mask[:, k % NT, bass.ds(b * NW, NW)], ALU.add).then_inc(pooled, 1)

            @block.tensor
            def _(pe):
                pe.wait_ge(ones_ready, 2)
                with pe.Fori(0, NBW) as b:
                    with pe.Fori(0, HP) as i:
                        for k in range(PAIR):
                            u, t = k // NT, k % NT
                            if t == 0:
                                pe.wait_ge(whc_ready, 2 * (HP * b + i) + u + 1)
                                pe.wait_ge(pso_free, 2 * (HP * b + i) + u + 1)
                            pe.wait_ge(pr_ready, PAIR * (HP * b + i) + k + 5)
                            for q in range(W2):
                                at_q = slice(q * NB, (q + 1) * NB)
                                mm = pe.matmul(pso[u][:, at_q], whc[u][:, t, :], pr[k % 4][:, at_q],
                                               start=(t == 0), stop=(t == NT - 1))
                            mm.then_inc(pr_used, 1)

            @block.scalar
            def _(act):
                act.sem_inc(pr_ready, 4)

                def take(u, head):
                    act.activation(whc[u][:, :, u * HID:(u + 1) * HID], wh[:, :, bass.ds(head * HID, HID)],
                                   ACT.Copy).then_inc(whc_ready, 1)

                def tail(u, count):
                    act.wait_ge(pr_used, NT * count + 4)
                    act.wait_ge(stage_free, count + 1)
                    act.activation(stage[u][:, :], pso[u][:, :], ACT.Copy).then_inc(pso_free, 1)

                act.wait_ge(wh_in, 16)
                act.activation(whc[0][:, :, 0:HID], wh[:, :, 0:HID], ACT.Copy).then_inc(whc_ready, 1)
                act.wait_ge(zero_ready, 1)
                with act.Fori(0, NBW) as b:
                    with act.Fori(0, HP) as i:
                        for k in range(PAIR):
                            u, t = k // NT, k % NT
                            pair = HP * b + i
                            if k % MASK_STEPS == POOLED:
                                act.wait_ge(self_masked, (PAIR // MASK_STEPS) * pair + k // MASK_STEPS + 1)
                            else:
                                act.wait_ge(pooled, (PAIR - PAIR // MASK_STEPS) * pair + k - k // MASK_STEPS + 1)
                            act.wait_ge(pr_used, PAIR * pair + k + 1)
                            act.sem_inc(c.passed, 1)
                            act.activation(pr[k % 4], arg[k % 4], ACT.Exp,
                                           bias=flat(dst)[:, bass.ds((2 * i + u) * NT + t, 1)]).then_inc(pr_ready, 1)
                            if t == TAIL_AT:
                                tail(1 - u, 2 * pair + u)
                                act.wait_ge(pso_free, 2 * pair + u + 2)
                                act.sem_inc(staged, 1)
                            if t == NEXT_AT:
                                act.wait_ge(pso_free, 2 * pair + u + 2)
                                act.sem_inc(c.passed, 1)
                                take(1 - u, 2 * i + u + 1)
                tail(1, HEADS * NBW)
                act.wait_ge(pso_free, HEADS * NBW + 2)
                act.sem_inc(staged, 1)

            @block.vector
            def _(dve):
                dve.sem_inc(pr_used, 4)
                dve.sem_inc(pso_free, 1)
                dve.memset(pso[1][:, :], 0.0).then_inc(zero_ready, 1)
                with dve.Fori(0, NBW) as b:
                    with dve.Fori(0, HP) as i:
                        for k in range(PAIR):
                            g = PAIR * (HP * b + i) + k
                            u = k // NT
                            dve.wait_ge(pr_ready, g + 1)
                            if k % NT == 0:
                                dve.wait_ge(rows_in[u], 32 * (HP * b + i) + 32)
                            dve.scalar_tensor_tensor(
                                out=arg[k % 4], in0=s8[u][:, :], scalar=flat(d8)[:, bass.ds((2 * i + u) * NT + k % NT, 1)],
                                in1=vb[u][:, :], op0=ALU.max, op1=ALU.add).then_inc(arg_ready, 1)
                            if k % MASK_STEPS == POOLED:
                                dve.wait_ge(arg_ready, g + 1)
                                dve.tensor_tensor(arg[k % 4], arg[k % 4], mask[:, k % NT, bass.ds(b * NW, NW)], ALU.add).then_inc(self_masked, 1)


def encoder_block(nc, c, sums, weights, reciprocals, ws, bs):
    TILES = N // NW * HP
    dims = (D, M1, M2, M3)
    with ExitStack() as ctx:
        encs = ctx.enter_context(nc.sbuf_tensor("en_enc", [P, TILES, NW], F32))
        rec = ctx.enter_context(nc.sbuf_tensor("en_rec", [P, TILES, NW], F32))
        low = [ctx.enter_context(nc.sbuf_tensor(f"en_low{i}", [P, NW], F32)) for i in range(2)]
        den = ctx.enter_context(nc.sbuf_tensor("en_den", [P, N // NW * HEADS * NW // P], F32))
        w = [ctx.enter_context(nc.sbuf_tensor(f"en_w{j}", [P, dims[j] // P, dims[j + 1] if j < 3 else D], F32)) for j in range(4)]
        bias = [ctx.enter_context(nc.sbuf_tensor(f"en_b{j}", [P, dims[j + 1] // P], F32)) for j in range(3)]
        b4 = ctx.enter_context(nc.sbuf_tensor("en_b4", [P, D], F32))
        hid = [ctx.enter_context(nc.sbuf_tensor(f"en_h{j}", [P, dims[j + 1] // P, NB], F32)) for j in range(3)]
        psh = [ctx.enter_context(nc.psum_tensor(f"en_ph{i}", [P, NB], F32)) for i in range(2)]
        pso = [ctx.enter_context(nc.psum_tensor(f"en_po{i}", [P, NB], F32)) for i in range(4)]
        s = lambda name: c.semaphore(f"en_{name}")
        arrived, h_ready, h_done, o_ready, o_free, biased = (s(n) for n in ("arrived", "h_ready", "h_done", "o_ready", "o_free", "biased"))
        den_in, inverted, rec_out, mean, halves, exped = (s(n) for n in ("den_in", "inverted", "rec_out", "mean", "halves", "exped"))
        tile_in = [s("tile_in0"), s("tile_in1")]
        enc_ready, stats_ready = s("enc_ready"), s("stats_ready")
        hidden = [(j, o) for j in range(3) for o in range(dims[j + 1] // P)]
        TPB = NB // P
        with nc.Block() as block:

            @block.sync
            def _(sp):
                sp.dma_start(den[:, :], weights.rearrange("r (a n) -> (r a) n", n=den.shape[1])).then_inc(den_in, 16)
                for j in range(4):
                    sp.dma_start(w[j][:, :, :], ws[j].rearrange("(k p) o -> p k o", p=P)).then_inc(arrived, 16)
                for j in range(3):
                    sp.dma_start(bias[j][:, :], bs[j]).then_inc(arrived, 16)
                sp.dma_start(b4[:, :], bs[3].rearrange("(a n) -> a n", a=1).broadcast_to([P, D])).then_inc(arrived, 16)
                sp.wait_ge(inverted, 1)
                sp.dma_start(reciprocals.rearrange("r (a n) -> (r a) n", n=den.shape[1]), den[:, :]).then_inc(rec_out, 16)
                sp.wait_ge(rec_out, 16)
                for j in range(TILES):
                    if j >= 2:
                        sp.wait_ge(mean, j - 1)
                    sp.dma_start(encs[:, j, :], sums[j * P:(j + 1) * P, :]).then_inc(tile_in[j % 2], 16)
                    for u in range(2):
                        r = 2 * j + u
                        sp.dma_start(rec[u * HID:(u + 1) * HID, j, :], reciprocals[r:r + 1, :].broadcast_to([HID, NW])).then_inc(tile_in[j % 2], 16)

            @block.tensor
            def _(pe):
                pe.wait_ge(arrived, 128)
                for q in range(N // NB):
                    b, at_q = q // (NW // NB), slice((q % (NW // NB)) * NB, (q % (NW // NB) + 1) * NB)
                    for x, (j, o) in enumerate(hidden):
                        m = q * len(hidden) + x
                        need = max(m - 1, q * len(hidden) + (0 if j == 0 else [h[0] for h in hidden].index(j)))
                        if need:
                            pe.wait_ge(h_done, need)
                        for k in range(dims[j] // P):
                            if x == 0 and q % (NW // NB) == 0:
                                pe.wait_ge(enc_ready, b * HP + k + 1)
                            rhs = encs[:, b * HP + k, at_q] if j == 0 else hid[j - 1][:, k, :]
                            mm = pe.matmul(psh[m % 2][:, :], w[j][:, k, o * P:(o + 1) * P], rhs,
                                           start=(k == 0), stop=(k == dims[j] // P - 1))
                        mm.then_inc(h_ready, 1)
                    pe.wait_ge(h_done, (q + 1) * len(hidden))
                    for t in range(TPB):
                        pe.wait_ge(o_free, q * TPB + t + 1)
                        for k in range(M3 // P):
                            mm = pe.matmul(pso[t][:, :], hid[2][:, k, t * P:(t + 1) * P], w[3][:, k, :],
                                           start=(k == 0), stop=(k == M3 // P - 1))
                        mm.then_inc(o_ready, 1)

            @block.scalar
            def _(act):
                for j in range(TILES):
                    act.wait_ge(halves, j + 1)
                    act.activation(low[j % 2][:, :], low[j % 2][:, :], ACT.Exp).then_inc(exped, 1)
                act.wait_ge(arrived, 128)
                for q in range(N // NB):
                    for x, (j, o) in enumerate(hidden):
                        m = q * len(hidden) + x
                        act.wait_ge(h_ready, m + 1)
                        act.activation(hid[j][:, o, :], psh[m % 2][:, :], ACT.Relu, bias=bias[j][:, o:o + 1]).then_inc(h_done, 1)

            @block.vector
            def _(dve):
                dve.sem_inc(o_free, 4)
                dve.wait_ge(den_in, 16)
                dve.reciprocal(den[:, :], den[:, :]).then_inc(inverted, 1)

                def elu_end(j):
                    dve.wait_ge(exped, j + 1)
                    dve.scalar_tensor_tensor(out=encs[:, j, :], in0=low[j % 2][:, :], scalar=-1.0, in1=encs[:, j, :],
                                             op0=ALU.add, op1=ALU.max).then_inc(enc_ready, 1)

                for j in range(TILES):
                    dve.wait_ge(tile_in[j % 2], 48 * (j // 2 + 1))
                    dve.tensor_tensor(encs[:, j, :], encs[:, j, :], rec[:, j, :], ALU.mult).then_inc(mean, 1)
                    if j:
                        elu_end(j - 1)
                    dve.wait_ge(mean, j + 1)
                    if j >= 2:
                        dve.wait_ge(enc_ready, j - 1)
                    dve.tensor_scalar(low[j % 2][:, :], encs[:, j, :], 0.0, None, ALU.min).then_inc(halves, 1)
                elu_end(TILES - 1)
                dve.wait_ge(arrived, 128)
                for t in range(NT):
                    dve.tensor_tensor(c.X[:, t, :], c.X[:, t, :], b4[:, :], ALU.add).then_inc(biased, 1)
                for t in range(NT):
                    dve.wait_ge(biased, t + 1)
                    dve.wait_ge(o_ready, t + 1)
                    dve.tensor_tensor(c.X[:, t, :], pso[t % 4][:, :], c.X[:, t, :], ALU.add).then_inc(o_free, 1)
                    dve.wait_ge(o_free, t + 5)
                    dve.bn_stats(c.stats[:, t, :], c.X[:, t, :]).then_inc(stats_ready, 1)


def attention_stage(nc, c, dram):
    with ExitStack() as st:
        def sb(name, shape):
            return st.enter_context(nc.sbuf_tensor(f"ga_{name}", shape, F32))
        dst_rows = nc.dram_tensor("ga_dst_rows", [HEADS, N], F32).ap()
        s8_rows = nc.dram_tensor("ga_s8_rows", [HEADS, N], F32).ap()
        v_rows = nc.dram_tensor("ga_v_rows", [HEADS, N], F32).ap()
        sums = nc.dram_tensor("ga_sums", [N // NW * D, NW], F32).ap()
        weights, reciprocals = (nc.dram_tensor(f"ga_{n}", [N // NW * HEADS, NW], F32).ap() for n in ("weights", "reciprocals"))
        src, dst, maxd = (sb(n, [P, HEADS, NT]) for n in ("src", "dst", "maxd"))
        d8 = sb("d8", [P, HEADS, NT])
        s8, v = src, maxd
        wh_dram = nc.dram_tensor("ga_wh_dram", [N, D + HID], F32).ap()
        with ExitStack() as pre:
            wh = pre.enter_context(nc.sbuf_tensor("ga_wh0", [P, NT, D + HID], F32))
            xt = split_tile(pre, nc, "ga_xt", [P, DC, N])
            layernorm_block(nc, c, "2", xt)
            project_block(nc, c, xt, dram["w_heads"], dram["a_rows"], wh, wh_dram, src, dst)
        with ExitStack() as pre:
            rows_out(nc, c, pre, "d", [(dst, F32, dst_rows)])
        with ExitStack() as att:
            mask = att.enter_context(nc.sbuf_tensor("ga_mask", [P, NT, N], BF16))
            neighbour_max_block(nc, c, dram["adj"], dram["adj_t"], dst_rows, maxd, mask)
            wh = att.enter_context(nc.sbuf_tensor("ga_wh", [P, NT, D + HID], F32))
            wh_in = c.semaphore("ga_wh_in")
            row_terms_block(nc, c, src, dst, maxd, s8, d8, v, wh_dram, wh, wh_in)
            with ExitStack() as pre:
                rows_out(nc, c, pre, "s", [(s8, F32, s8_rows), (v, F32, v_rows)])
            attention_block(nc, c, mask, wh, wh_in, dst, d8, s8_rows, v_rows, sums, weights)
        encoder_block(nc, c, sums, weights, reciprocals, [dram[f"enc_w{j}"] for j in range(4)], [dram[f"enc_b{j}"] for j in range(4)])


def route_block(nc, c, xt, dram, slot_tokens, dest, weight):
    with ExitStack() as ctx:
        def sb(name, shape, dt=F32):
            return ctx.enter_context(nc.sbuf_tensor(f"r_{name}", shape, dt))
        wg = sb("wg", [P, DC, P])
        before, ones, first_slot = sb("before", [P, P]), sb("ones", [P, P]), sb("first_slot", [P, E1])
        tokens = sb("tokens", [P, NT])
        sc, hot, mask, places = sb("sc", [P, NT, E1]), sb("hot", [P, K1, NT, E1]), sb("mask", [P, NT, E1]), sb("places", [P, NT, E1])
        tmp = sb("tmp", [P, NT, E1])
        col, gm, keep, kept = sb("col", [P, NT]), sb("gm", [P, NT, G1]), sb("keep", [P, NT, G1]), sb("kept", [P, KG, NT, G1])
        top, idx, idf = sb("top", [P, NT, 8]), sb("idx", [P, NT, 8], U32), sb("idf", [P, NT, 8])
        carry = sb("carry", [P, NT, E1])
        destf = sb("destf", [P, K1, NT])
        wgs = split_tile(ctx, nc, "r_wgs", [P, DC, P])
        raw = sb("raw", [P, DC, D])
        sw = [split_tile(ctx, nc, f"r_sw{j}", [P, DC, D]) for j in range(3)]
        gate = [sb(f"gate{i}", [P, NB]) for i in range(2)]
        hf = [sb(f"hf{i}", [P, NB]) for i in range(2)]
        up = [raw[:, i, :] for i in range(2)]
        ostage = [raw[:, 2 + i, :] for i in range(2)]
        logits_sb = hot[0:LOGIT_ROWS, :, :, :].rearrange("p k t e -> p (k t e)")
        hid = split_tile(ctx, nc, "r_hid", [P, DC, NB])
        psl = ctx.enter_context(nc.psum_tensor("r_psl", [P, NT, E1], F32))
        pst = ctx.enter_context(nc.psum_tensor("r_pst", [P, NT, E1], F32))
        ps1 = [ctx.enter_context(nc.psum_tensor(f"r_ps1_{i}", [P, NB], F32)) for i in range(2)]
        ps3 = [ctx.enter_context(nc.psum_tensor(f"r_ps3_{i}", [P, NB], F32)) for i in range(2)]
        pso = [ctx.enter_context(nc.psum_tensor(f"r_pso{i}", [P, NB], F32)) for i in range(2)]
        s = lambda name: c.semaphore(f"r_{name}")
        small_in, sw_in, filled, scattered = s("small_in"), s("sw_in"), s("filled"), s("scattered")
        logits, expd, chain, counted = s("logits"), s("expd"), s("chain"), s("counted")
        h_ready, gated, h_done, o_ready, o_free = s("h_ready"), s("gated"), s("h_done"), s("o_ready"), s("o_free")
        wg_zeroed, logits_t, lt_copied, bank_free, out_taken = (
            s(n) for n in ("wg_zeroed", "logits_t", "lt_copied", "bank_free", "out_taken"))
        gh_ready, gl_ready, swh_ready, swl_ready, multiplied, hh_ready = (
            s(n) for n in ("gh_ready", "gl_ready", "swh_ready", "swl_ready", "multiplied", "hh_ready"))
        TPB = NB // P
        BLOCKS = N // NB
        POOLED = 2
        with nc.Block() as block:

            @block.sync
            def _(sp):
                sp.wait_ge(wg_zeroed, 1)
                sp.dma_start(wg[:, :, 0:E1], dram["wg_t"].rearrange("(k p) e -> p k e", p=P)).then_inc(small_in, 16)
                for t, n in ((before, "c_before"), (ones, "c_ones"), (first_slot, "c_first_slot"), (tokens, "c_tokens")):
                    sp.dma_start(t[:, :], dram[n]).then_inc(small_in, 16)
                sp.dma_start(slot_tokens, dram["c_no_token"]).then_inc(filled, 16)
                for j, n in enumerate(("sw1", "sw3", "sw2")):
                    if j:
                        sp.wait_ge(swl_ready, j)
                    sp.dma_start(raw[:, :, :], dram[n].rearrange("(k p) f -> p k f", p=P)).then_inc(sw_in, 16)

            @block.gpsimd
            def _(pool):
                for q in range(POOLED):
                    for f in range(DC):
                        m = q * DC + f
                        pool.wait_ge(bank_free, m + 1)
                        if m >= 2:
                            pool.wait_ge(h_done, m - 1)
                        pool.tensor_tensor(hf[m % 2][:, :], up[m % 2], gate[m % 2][:, :], ALU.mult).then_inc(multiplied, 1)
                        pool.wait_ge(hh_ready, m + 1)
                        pool.tensor_tensor(hid[1][:, f, :], hf[m % 2][:, :], hid[0][:, f, :].bitcast(F32), ALU.subtract).then_inc(h_done, 1)
                    for t in range(q * TPB, (q + 1) * TPB):
                        pool.wait_ge(o_free, t + 3)
                        pool.tensor_tensor(c.X[:, t, :], c.X[:, t, :], ostage[t % 2], ALU.add).then_inc(out_taken, 1)
                pool.wait_ge(filled, 16)
                pool.wait_ge(small_in, 80)
                pool.wait_ge(chain, DEST_AT)
                for k in range(K1):
                    for t in range(NT):
                        pool.indirect_dma_start(out=slot_tokens, out_offset=bass.IndirectOffsetOnAxis(ap=dest[:, k, t:t + 1], axis=0),
                                                in_=tokens[:, t:t + 1], in_offset=None, bounds_check=SLOTS - 1,
                                                oob_is_err=False).then_inc(scattered, 16)
                pool.wait_ge(scattered, 16 * K1 * NT)

            @block.tensor
            def _(pe):
                pe.wait_ge(small_in, 80)
                logits_pe(pe, c, wgs, gl_ready, xt, ps1 + ps3, logits_t, logits_sb, lt_copied,
                          psl[:, :, :].rearrange("p t e -> p (t e)"), logits)

                def hidden(q):
                    for f in range(DC):
                        m = q * DC + f
                        if m >= 2:
                            pe.wait_ge(bank_free, m - 1)
                        for j, ps in enumerate((ps1, ps3)):
                            for k in range(DC):
                                mm = product(pe, ps[m % 2][:, :], lambda a: sw[j][a][:, k, f * P:(f + 1) * P],
                                             lambda b: xt[b][:, k, q * NB:(q + 1) * NB], k == 0, k == DC - 1)
                        mm.then_inc(h_ready, 1)

                def outs(q):
                    pe.wait_ge(h_done, (q + 1) * DC)
                    for t in range(TPB):
                        pe.wait_ge(o_free, q * TPB + t + 1)
                        for f in range(DC):
                            mm = product(pe, pso[t % 2][:, :], lambda a: hid[a][:, f, t * P:(t + 1) * P], lambda b: sw[2][b][:, f, :],
                                         f == 0, f == DC - 1)
                        mm.then_inc(o_ready, 1)

                def count():
                    pe.wait_ge(chain, MASK_AT)
                    flat = mask[:, :, :].rearrange("p t e -> p (t e)")
                    pe.matmul(psl[:, :, :].rearrange("p t e -> p (t e)"), before[:, :], flat, start=True, stop=True)
                    pe.matmul(pst[:, :, :].rearrange("p t e -> p (t e)"), ones[:, :], flat, start=True, stop=True).then_inc(counted, 1)

                pe.wait_ge(swl_ready, 3)
                for q in range(BLOCKS):
                    if q == 1:
                        count()
                    hidden(q)
                    outs(q)

            @block.scalar
            def _(act):
                def high(j):
                    act.wait_ge(sw_in, 16 * (j + 1))
                    act.activation(sw[j][0][:, :, :], raw[:, :, :], ACT.Copy).then_inc(swh_ready, 1)

                act.wait_ge(small_in, 80)
                act.activation(wgs[0][:, :, :], wg[:, :, :], ACT.Copy).then_inc(gh_ready, 1)
                high(0)
                high(1)
                logits_act(act, ps1 + ps3, logits_t, logits_sb, lt_copied)
                high(2)
                act.wait_ge(chain, 2)
                act.activation(sc[:, :, :], sc[:, :, :], ACT.Exp).then_inc(expd, 1)

                def round_hidden(m):
                    act.wait_ge(multiplied, m + 1)
                    if m % DC == 0 and m:
                        act.wait_ge(o_ready, m // DC * TPB)
                    act.activation(hid[0][:, m % DC, :], hf[m % 2][:, :], ACT.Copy).then_inc(hh_ready, 1)

                for q in range(BLOCKS):
                    for f in range(DC):
                        m = q * DC + f
                        act.wait_ge(h_ready, m + 1)
                        if m >= 2:
                            act.wait_ge(multiplied, m - 1)
                        act.activation(gate[m % 2][:, :], ps1[m % 2][:, :], ACT.Silu).then_inc(gated, 1)
                        if q < POOLED:
                            act.activation(up[m % 2], ps3[m % 2][:, :], ACT.Copy).then_inc(bank_free, 1)
                            if f:
                                round_hidden(m - 1)
                    if q < POOLED:
                        round_hidden(q * DC + DC - 1)
                        for t in range(q * TPB, (q + 1) * TPB):
                            act.wait_ge(o_ready, t + 1)
                            if t >= 2:
                                act.wait_ge(out_taken, t - 1)
                            act.activation(ostage[t % 2], pso[t % 2][:, :], ACT.Copy).then_inc(o_free, 1)

            @block.vector
            def _(dve):
                dve.sem_inc(o_free, 2)
                n = [0]

                def link(ins):
                    n[0] += 1
                    ins.then_inc(chain, 1)
                    dve.wait_ge(chain, n[0])

                def over(ap, e):
                    return ap.unsqueeze(2).broadcast_to([P, NT, e])

                def one_hot(out, e, column):
                    link(dve.tensor_tensor(out, c.iota[:, 0:e].unsqueeze(1).broadcast_to([P, NT, e]), over(column, e), ALU.is_equal))

                def top8(values):
                    for t in range(NT):
                        ins = dve.max(top[:, t, :], values[:, t, :])
                    link(ins)
                    for t in range(NT):
                        ins = dve.max_index(idx[:, t, :], top[:, t, :], values[:, t, :])
                    link(ins)
                    link(dve.tensor_copy(idf[:, :, :], idx[:, :, :]))

                def low(j):
                    dve.wait_ge(swh_ready, j + 1)
                    dve.tensor_tensor(sw[j][1][:, :, :], raw[:, :, :], sw[j][0][:, :, :].bitcast(F32), ALU.subtract).then_inc(swl_ready, 1)

                dve.memset(wg[:, :, :], 0.0).then_inc(wg_zeroed, 1)
                dve.wait_ge(gh_ready, 1)
                dve.tensor_tensor(wgs[1][:, :, :], wg[:, :, :], wgs[0][:, :, :].bitcast(F32), ALU.subtract).then_inc(gl_ready, 1)
                dve.wait_ge(small_in, 80)
                low(0)
                low(1)
                dve.wait_ge(logits, 1)
                link(dve.tensor_reduce(col[:, :], psl[:, :, :], AX, ALU.max))
                link(dve.tensor_tensor(sc[:, :, :], psl[:, :, :], over(col[:, :], E1), ALU.subtract))
                low(2)
                dve.wait_ge(expd, 1)
                link(dve.tensor_reduce(col[:, :], sc[:, :, :], AX, ALU.add))
                link(dve.reciprocal(col[:, :], col[:, :]))
                link(dve.tensor_tensor(sc[:, :, :], sc[:, :, :], over(col[:, :], E1), ALU.mult))
                link(dve.tensor_reduce(gm[:, :, :], sc[:, :, :].rearrange("p t (g e) -> p t g e", e=EG), AX, ALU.max))
                top8(gm)
                for k in range(KG):
                    one_hot(kept[:, k, :, :], G1, idf[:, :, k])
                link(dve.tensor_tensor(keep[:, :, :], kept[:, 0, :, :], kept[:, 1, :, :], ALU.add))
                for k in range(2, KG):
                    link(dve.tensor_tensor(keep[:, :, :], keep[:, :, :], kept[:, k, :, :], ALU.add))
                spread = lambda a: a[:, :, :].rearrange("p t g -> p (t g)").unsqueeze(2).broadcast_to([P, NT * G1, EG])
                grouped = lambda a: a[:, :, :].rearrange("p t (g e) -> p (t g) e", e=EG)
                link(dve.tensor_tensor(grouped(tmp), grouped(sc), spread(keep), ALU.mult))
                link(dve.tensor_scalar(keep[:, :, :], keep[:, :, :], -1.0, None, ALU.add))
                link(dve.tensor_tensor(grouped(tmp), grouped(tmp), spread(keep), ALU.add))
                top8(tmp)
                for k in range(K1):
                    one_hot(hot[:, k, :, :], E1, idf[:, :, k])
                link(dve.tensor_tensor(mask[:, :, :], hot[:, 0, :, :], hot[:, 1, :, :], ALU.add))
                for k in range(2, K1):
                    link(dve.tensor_tensor(mask[:, :, :], mask[:, :, :], hot[:, k, :, :], ALU.add))
                assert n[0] == MASK_AT
                link(dve.tensor_reduce(col[:, :], top[:, :, 0:K1], AX, ALU.add))
                link(dve.tensor_scalar(col[:, :], col[:, :], 1e-9, None, ALU.add))
                link(dve.reciprocal(col[:, :], col[:, :]))
                link(dve.tensor_tensor(weight[:, :, :].rearrange("p k t -> p t k"), top[:, :, 0:K1], over(col[:, :], K1), ALU.mult))
                dve.wait_ge(counted, 1)
                link(dve.memset(carry[:, 0, :], 0.0))
                for t in range(1, NT):
                    link(dve.tensor_tensor(carry[:, t, :], pst[:, t - 1, :], carry[:, t - 1, :], ALU.add))
                link(dve.tensor_tensor(places[:, :, :], psl[:, :, :], carry[:, :, :], ALU.add))
                link(dve.tensor_scalar(tmp[:, :, :], places[:, :, :], float(CAP), None, ALU.is_lt))
                slots = first_slot[:, :].unsqueeze(1).broadcast_to([P, NT, E1])
                link(dve.tensor_tensor(places[:, :, :], places[:, :, :], slots, ALU.add))
                link(dve.scalar_tensor_tensor(out=places[:, :, :], in0=places[:, :, :], scalar=-float(SLOTS), in1=tmp[:, :, :], op0=ALU.add, op1=ALU.mult))
                link(dve.tensor_scalar(places[:, :, :], places[:, :, :], float(SLOTS), None, ALU.add))
                for k in range(K1):
                    link(dve.tensor_tensor(hot[:, k, :, :], hot[:, k, :, :], places[:, :, :], ALU.mult))
                    link(dve.tensor_reduce(destf[:, k, :], hot[:, k, :, :], AX, ALU.add))
                link(dve.tensor_copy(dest[:, :, :], destf[:, :, :]))
                assert n[0] == DEST_AT

                dve.wait_ge(h_done, POOLED * DC)
                dve.wait_ge(o_free, POOLED * TPB + 2)
                for q in range(POOLED, BLOCKS):
                    for f in range(DC):
                        m = q * DC + f
                        dve.wait_ge(gated, m + 1)
                        dve.tensor_tensor(hf[m % 2][:, :], ps3[m % 2][:, :], gate[m % 2][:, :], ALU.mult).then_inc(multiplied, 1)
                        dve.wait_ge(multiplied, m + 1)
                        dve.sem_inc(bank_free, 1)
                        if f == 0 and q:
                            dve.wait_ge(o_ready, q * TPB)
                        dve.tensor_copy(hid[0][:, f, :], hf[m % 2][:, :]).then_inc(hh_ready, 1)
                        dve.wait_ge(hh_ready, m + 1)
                        dve.tensor_tensor(hid[1][:, f, :], hf[m % 2][:, :], hid[0][:, f, :].bitcast(F32), ALU.subtract).then_inc(h_done, 1)
                    for t in range(TPB):
                        dve.wait_ge(o_ready, q * TPB + t + 1)
                        dve.tensor_tensor(c.X[:, q * TPB + t, :], pso[t % 2][:, :], c.X[:, q * TPB + t, :], ALU.add).then_inc(o_free, 1)


MASK_AT = 6 + 3 + KG + (KG - 1) + 3 + 3 + K1 + (K1 - 1)
DEST_AT = MASK_AT + 4 + NT + 5 + 2 * K1 + 1


def experts_block(nc, c, dram, xp, oe, slot_tokens):
    with ExitStack() as ctx:
        def sb(name, shape, dt=F32):
            return ctx.enter_context(nc.sbuf_tensor(f"e_{name}", shape, dt))
        idx = sb("idx", [P, NCT, E1], U32)
        tok = sb("tok", [E1, CAP])
        idn = [sb(f"idn{u}", [P, NCT], U32) for u in range(2)]
        xe = [sb(f"xe{u}", [P, NCT, D]) for u in range(2)]
        raw = [sb(f"raw{j}", [P, DC, D]) for j in range(3)]
        w13 = [[split_tile(ctx, nc, f"e_w{j}_{u}", [P, DC, D]) for j in (1, 3)] for u in range(2)]
        w2 = split_tile(ctx, nc, "e_w2", [P, DC, D])
        xet = [split_tile(ctx, nc, f"e_xet{u}", [P, DC, CAP]) for u in range(2)]
        hid = split_tile(ctx, nc, "e_hid", [P, DC, NCT * P])
        gate = [sb(f"gate{i}", [P, CAP]) for i in range(2)]
        hf = [sb(f"hf{i}", [P, CAP]) for i in range(2)]
        res = [sb(f"res{u}", [P, NCT, D]) for u in range(2)]
        pst = [ctx.enter_context(nc.psum_tensor(f"e_pst{i}", [P, DC, P], F32)) for i in range(2)]
        ps1 = [ctx.enter_context(nc.psum_tensor(f"e_ps1_{i}", [P, NB], F32)) for i in range(2)]
        ps3 = [ctx.enter_context(nc.psum_tensor(f"e_ps3_{i}", [P, NB], F32)) for i in range(2)]
        pso = [ctx.enter_context(nc.psum_tensor(f"e_pso{i}", [P, D], F32)) for i in range(2)]
        s = lambda name: c.semaphore(f"e_{name}")
        tok_in, tok_turned, idx_ready, idn_ready = s("tok_in"), s("tok_turned"), s("idx_ready"), s("idn_ready")
        w_in = [s("w_in0"), s("w_in1"), s("w_in2")]
        x_in = [s("x_in0"), s("x_in1")]
        res_out, res_free = [s("res_out0"), s("res_out1")], s("res_free")
        turned, xh_ready, xl_ready, wh_ready, wl_ready = s("turned"), s("xh_ready"), s("xl_ready"), s("wh_ready"), s("wl_ready")
        h_ready, gated, multiplied, hh_ready, h_done, o_ready, o_done = (
            s(n) for n in ("h_ready", "gated", "multiplied", "hh_ready", "h_done", "o_ready", "o_done"))
        HALF = E1 // 2
        W_NAMES = ("w1_1", "w3_1", "w2_1")
        whole = CAP // P

        with nc.Block() as block:

            @block.sync
            def _(sp):
                sp.dma_start(tok[:, :], slot_tokens.rearrange("(e s) a -> e (s a)", s=CAP)).then_inc(tok_in, 16)

                def load(e, j):
                    src = dram[W_NAMES[j]][bass.ds(e * D, D), :].rearrange("(k p) f -> p k f", p=P)
                    sp.dma_start(raw[j][:, :, :], src).then_inc(w_in[j], 16)

                def store(i, u):
                    e = 2 * i + u
                    sp.wait_ge(o_done, 2 + (e + 1) * NCT)
                    sp.dma_start(oe[bass.ds(e * CAP, whole * P), :].rearrange("(j p) d -> p j d", p=P), res[u][:, 0:whole, :]).then_inc(res_out[u], 16)
                    sp.dma_start(oe[bass.ds(e * CAP + whole * P, CAP - whole * P), :], res[u][0:CT[-1], whole, :]).then_inc(res_out[u], 16)
                    sp.wait_ge(res_out[u], 32 * i + 32)
                    sp.sem_inc(res_free, 1)

                sp.sem_inc(res_free, 2)
                for j in range(3):
                    load(0, j)

                def again(e, j, done):
                    sp.wait_ge(wl_ready, done)
                    load(e, j)

                def step(i, u, last):
                    e = 2 * i + u
                    again(e + 1, 2, 3 * e + 3)
                    if not last:
                        again(e + 2, 0, 3 * e + 4)
                        again(e + 2, 1, 3 * e + 5)
                    store(i, u)

                again(1, 0, 1)
                again(1, 1, 2)
                with sp.Fori(0, HALF - 1) as i:
                    step(i, 0, False)
                    step(i, 1, False)
                step(HALF - 1, 0, True)
                store(HALF - 1, 1)

            @block.gpsimd
            def _(pool):
                pool.wait_ge(idx_ready, NCT)

                def gather(i, u):
                    e = 2 * i + u
                    for j, r in enumerate(CT):
                        pool.tensor_copy(idn[u][0:r, j:j + 1], idx[0:r, j, bass.ds(e, 1)]).then_inc(idn_ready, 1)
                    for j, r in enumerate(CT):
                        pool.wait_ge(idx_ready, NCT)
                        pool.wait_ge(idn_ready, e * NCT + j + 1)
                        pool.sem_inc(c.passed, 1)
                        pool.indirect_dma_start(out=xe[u][0:r, j, :], out_offset=None, in_=xp,
                                                in_offset=bass.IndirectOffsetOnAxis(ap=idn[u][0:r, j:j + 1], axis=0)).then_inc(x_in[u], 16)

                gather(0, 0)
                gather(0, 1)
                with pool.Fori(0, HALF - 1) as i:
                    for u in range(2):
                        pool.wait_ge(turned, (2 * i + u + 1) * NCT)
                        gather(i + 1, u)

            @block.tensor
            def _(pe):
                pe.wait_ge(tok_in, 16)
                for j, r in enumerate(CT):
                    mm = pe.transpose(ps1[0][0:r, j * P:j * P + E1], tok[:, j * P:j * P + r], c.ident[0:E1, 0:E1])
                mm.then_inc(tok_turned, 1)

                def turn(i, u, tiles):
                    for j in tiles:
                        r = CT[j]
                        pe.wait_ge(tok_in, 16)
                        if j == 0:
                            pe.wait_ge(x_in[u], 16 * NCT * i + 16 * NCT)
                        pe.wait_ge(xl_ready, (2 * i + u) * NCT + j + 1)
                        pe.sem_inc(c.passed, 1)
                        for k in range(DC):
                            mm = pe.transpose(pst[(u * NCT + j) % 2][:, k, 0:r], xe[u][0:r, j, k * P:(k + 1) * P], c.ident[0:r, 0:r])
                        mm.then_inc(turned, 1)

                def hidden(i, u):
                    e = 2 * i + u
                    pe.wait_ge(wl_ready, 3 * e + 2)
                    pe.wait_ge(xl_ready, 2 + (e + 1) * NCT)
                    for f in range(DC):
                        pe.wait_ge(multiplied, e * DC + f + 1)
                        for j, ps in enumerate((ps1, ps3)):
                            for k in range(DC):
                                mm = product(pe, ps[f % 2][:, 0:CAP], lambda a: w13[u][j][a][:, k, f * P:(f + 1) * P],
                                            lambda b: xet[u][b][:, k, :], k == 0, k == DC - 1)
                        mm.then_inc(h_ready, 1)

                def outs(i, u, tiles):
                    e = 2 * i + u
                    for j in tiles:
                        if j == 0:
                            pe.wait_ge(wl_ready, 3 * e + 3)
                        pe.wait_ge(o_done, e * NCT + j + 1)
                        for f in range(DC):
                            if j == 0:
                                pe.wait_ge(h_done, e * DC + f + 1)
                            mm = product(pe, pso[(u * NCT + j) % 2][:, :], lambda a: hid[a][:, f, j * P:(j + 1) * P],
                                        lambda b: w2[b][:, f, :], f == 0, f == DC - 1)
                        mm.then_inc(o_ready, 1)

                def step(i, u, last):
                    hidden(i, u)
                    if not last:
                        turn(i + u, 1 - u, (0, 1))
                    outs(i, u, (0,))
                    if not last:
                        turn(i + u, 1 - u, range(2, NCT))
                    outs(i, u, range(1, NCT))

                turn(0, 0, range(NCT))
                with pe.Fori(0, HALF - 1) as i:
                    step(i, 0, False)
                    step(i, 1, False)
                step(HALF - 1, 0, False)
                step(HALF - 1, 1, True)

            @block.scalar
            def _(act):
                act.sem_inc(o_ready, 1)

                def high(i, u, j):
                    e = 2 * i + u
                    act.wait_ge(w_in[j], 16 * e + 16)
                    if j == 2:
                        act.wait_ge(o_ready, e * NCT + 1)
                    act.activation((w13[u][j] if j < 2 else w2)[0][:, :, :], raw[j][:, :, :], ACT.Copy).then_inc(wh_ready, 1)

                def rows(i, u):
                    for j, r in enumerate(CT):
                        act.wait_ge(turned, (2 * i + u) * NCT + j + 1)
                        act.activation(xet[u][0][:, :, j * P:j * P + r], pst[(u * NCT + j) % 2][:, :, 0:r], ACT.Copy).then_inc(xh_ready, 1)

                def step(i, u, last):
                    high(i, u, 2)
                    for f in range(DC):
                        act.wait_ge(h_ready, (2 * i + u) * DC + f + 1)
                        act.activation(gate[f % 2][:, :], ps1[f % 2][:, 0:CAP], ACT.Silu).then_inc(gated, 1)
                        if f < 2 and not last:
                            high(i + u, 1 - u, f)
                    if not last:
                        rows(i + u, 1 - u)

                high(0, 0, 0)
                high(0, 0, 1)
                rows(0, 0)
                with act.Fori(0, HALF - 1) as i:
                    step(i, 0, False)
                    step(i, 1, False)
                step(HALF - 1, 0, False)
                step(HALF - 1, 1, True)

            @block.vector
            def _(dve):
                dve.wait_ge(tok_turned, 1)
                for j, r in enumerate(CT):
                    dve.tensor_copy(idx[0:r, j, :], ps1[0][0:r, j * P:j * P + E1]).then_inc(idx_ready, 1)
                pad = NCT * P - CAP
                dve.memset(gate[0][:, 0:DC * pad], 0.0).then_inc(idx_ready, 1)
                dve.wait_ge(idx_ready, NCT + 1)
                for part in range(2):
                    dve.tensor_copy(hid[part][:, :, CAP:NCT * P], gate[0][:, 0:DC * pad].rearrange("p (k n) -> p k n", n=pad)).then_inc(idx_ready, 1)
                dve.wait_ge(idx_ready, NCT + 3)
                dve.sem_inc(multiplied, 2)
                dve.sem_inc(xl_ready, 2)
                dve.sem_inc(o_done, 2)

                def low(i, u, j):
                    dve.wait_ge(wh_ready, 3 * (2 * i + u) + j + 1)
                    parts = w13[u][j] if j < 2 else w2
                    dve.tensor_tensor(parts[1][:, :, :], raw[j][:, :, :], parts[0][:, :, :].bitcast(F32), ALU.subtract).then_inc(wl_ready, 1)

                def rows(i, u, tiles):
                    for j in tiles:
                        r = CT[j]
                        dve.wait_ge(xh_ready, (2 * i + u) * NCT + j + 1)
                        at = slice(j * P, j * P + r)
                        dve.tensor_tensor(xet[u][1][:, :, at], pst[(u * NCT + j) % 2][:, :, 0:r], xet[u][0][:, :, at].bitcast(F32),
                                          ALU.subtract).then_inc(xl_ready, 1)

                def step(i, u, last):
                    e = 2 * i + u
                    low(i, u, 2)
                    for f in range(DC):
                        dve.wait_ge(gated, e * DC + f + 1)
                        dve.tensor_tensor(hf[f % 2][:, :], ps3[f % 2][:, 0:CAP], gate[f % 2][:, :], ALU.mult).then_inc(multiplied, 1)
                        dve.wait_ge(multiplied, e * DC + f + 3)
                        if f == 0:
                            dve.wait_ge(o_ready, e * NCT + 1)
                        dve.tensor_copy(hid[0][:, f, 0:CAP], hf[f % 2][:, :]).then_inc(hh_ready, 1)
                        dve.wait_ge(hh_ready, e * DC + f + 1)
                        dve.tensor_tensor(hid[1][:, f, 0:CAP], hf[f % 2][:, :], hid[0][:, f, 0:CAP].bitcast(F32), ALU.subtract).then_inc(h_done, 1)
                        if f < 2 and not last:
                            low(i + u, 1 - u, f)
                    if not last:
                        rows(i + u, 1 - u, (0, 1))
                    dve.wait_ge(res_free, e + 1)
                    for j, r in enumerate(CT):
                        if j == 1 and not last:
                            rows(i + u, 1 - u, range(2, NCT))
                        dve.wait_ge(o_ready, e * NCT + j + 2)
                        dve.tensor_copy(res[u][0:r, j, :], pso[(u * NCT + j) % 2][0:r, :]).then_inc(o_done, 1)

                low(0, 0, 0)
                low(0, 0, 1)
                rows(0, 0, range(NCT))
                with dve.Fori(0, HALF - 1) as i:
                    step(i, 0, False)
                    step(i, 1, False)
                step(HALF - 1, 0, False)
                step(HALF - 1, 1, True)


def combine_block(nc, c, oe, dest, weight, out):
    RING = 8
    with ExitStack() as ctx:
        got = [ctx.enter_context(nc.sbuf_tensor(f"c_got{i}", [P, D], F32)) for i in range(RING)]
        got_in = [c.semaphore(f"c_got_in{i}") for i in range(RING)]
        added, stored = c.semaphore("c_added"), c.semaphore("c_stored")
        with nc.Block() as block:

            @block.gpsimd
            def _(pool):
                for m in range(NT * K1):
                    t, k = m // K1, m % K1
                    if m >= RING:
                        pool.wait_ge(added, m - RING + 1)
                    pool.indirect_dma_start(out=got[m % RING][:, :], out_offset=None, in_=oe,
                                            in_offset=bass.IndirectOffsetOnAxis(ap=dest[:, k, t:t + 1], axis=0)).then_inc(got_in[m % RING], 16)

            @block.vector
            def _(dve):
                for m in range(NT * K1):
                    t, k = m // K1, m % K1
                    dve.wait_ge(got_in[m % RING], 16 * (m // RING + 1))
                    if k:
                        dve.wait_ge(added, m)
                    dve.scalar_tensor_tensor(out=c.X[:, t, :], in0=got[m % RING][:, :], scalar=weight[:, k, t:t + 1],
                                             in1=c.X[:, t, :], op0=ALU.mult, op1=ALU.add).then_inc(added, 1)

            @block.sync
            def _(sp):
                for t in range(NT):
                    sp.wait_ge(added, K1 * (t + 1))
                    sp.dma_start(out[t * P:(t + 1) * P, :], c.X[:, t, :]).then_inc(stored, 16)
                sp.wait_ge(stored, 16 * NT)


def moe1_stage(nc, c, dram, out):
    xp = nc.dram_tensor("m1_xp", [N + 1, D], F32).ap()
    oe = nc.dram_tensor("m1_oe", [SLOTS + 1, D], F32).ap()
    slot_tokens = nc.dram_tensor("m1_slot_tokens", [SLOTS, 1], F32).ap()
    with ExitStack() as st:
        dest = st.enter_context(nc.sbuf_tensor("m1_dest", [P, K1, NT], U32))
        weight = st.enter_context(nc.sbuf_tensor("m1_weight", [P, K1, NT], F32))
        with ExitStack() as pre:
            xt = split_tile(pre, nc, "m1_xt", [P, DC, N])
            layernorm_block(nc, c, "3", xt, store=xp, zero_row=oe[SLOTS:SLOTS + 1, :])
            route_block(nc, c, xt, dram, slot_tokens, dest, weight)
        experts_block(nc, c, dram, xp, oe, slot_tokens)
        combine_block(nc, c, oe, dest, weight, out)


class Shared:

    def __init__(self, nc):
        self.nc = nc
        self.semaphores = []

    def semaphore(self, name):
        self.semaphores.append(self.nc.alloc_semaphore(name))
        return self.semaphores[-1]

    def stage_ends(self):
        self.nc.clear_and_free_semaphores(self.semaphores)
        self.nc.all_engine_barrier()
        self.semaphores = []


def build(nc, dram, out):
    c = Shared(nc)
    with ExitStack() as ctx:
        def sb(name, shape, dt=F32):
            return ctx.enter_context(nc.sbuf_tensor(name, shape, dt))
        c.X = sb("X", [P, NT, D])
        c.ident = sb("ident", [P, P])
        c.iota = sb("iota", [P, E1])
        c.stats = sb("stats", [P, NT, 6])
        c.passed = nc.alloc_semaphore("passed")
        with ExitStack() as st:
            y = st.enter_context(nc.sbuf_tensor("g0_y", [P, NT, D], F32))
            mean, scale, dinv = (st.enter_context(nc.sbuf_tensor(f"g0_{n}", [P, NT], F32)) for n in ("mean", "scale", "dinv"))
            pa = [st.enter_context(nc.sbuf_tensor(f"g0_pa{i}", [P, NT, P], F32)) for i in range(2)]
            panel_in = [c.semaphore(f"g0_panel_in{i}") for i in range(2)]
            again_in = [c.semaphore(f"g0_again_in{i}") for i in range(2)]
            with ExitStack() as first:
                pb = [first.enter_context(nc.sbuf_tensor(f"g0_pb{i}", [P, NT, P], F32)) for i in range(2)]
                start_block(nc, c, dram["x"], dram["adj"], dram["adj_t"], [(c.ident, dram["c_ident"]), (c.iota, dram["c_iota"])],
                            mean, scale, dinv, pa, pb, panel_in)
                symmetric_mix_block(nc, c, dram["adj"], dram["adj_t"], mean, scale, y, dinv, pa, pb, panel_in, again_in)
            mix_block(nc, c, dram["adj_t"], y, pa, again_in)
        with ExitStack() as st:
            xt = split_tile(st, nc, "m0_xt", [P, DC, N])
            layernorm_block(nc, c, "1", xt)
            moe0_block(nc, c, xt, dram["L0_ffn_router_w"], dram["L0_ffn_router_b"], dram["w1_0"],
                       dram["b1_0"], dram["w2_0"], dram["L0_ffn_b2"])
        c.stage_ends()
        attention_stage(nc, c, dram)
        c.stage_ends()
        moe1_stage(nc, c, dram, out)


def layouts(np, inp):
    a = {k: np.ascontiguousarray(inp[k]) for k in ("x", "adj", "L0_ffn_router_w", "L0_ffn_router_b", "L0_ffn_b2")}
    a["adj_t"] = np.ascontiguousarray(inp["adj"].T)
    a["w1_0"] = np.ascontiguousarray(inp["L0_ffn_W1"]).reshape(E0 * D, F0)
    a["w2_0"] = np.ascontiguousarray(inp["L0_ffn_W2"]).reshape(E0 * F0, D)
    a["b1_0"] = np.ascontiguousarray(inp["L0_ffn_b1"].reshape(E0 * HC0, P).T)
    a["c_ident"] = np.eye(P, dtype=np.float32)
    a["c_iota"] = np.tile(np.arange(E1, dtype=np.float32), (P, 1))
    a["w_heads"] = np.ascontiguousarray(inp["L1_gnn_W"].transpose(1, 0, 2)).reshape(D, HEADS * HID)
    a["a_rows"] = np.stack([inp["L1_gnn_a1"].reshape(-1), inp["L1_gnn_a2"].reshape(-1)])
    for j in range(4):
        a[f"enc_w{j}"] = np.ascontiguousarray(inp[f"L1_gnn_W{j + 1}"].T)
        b = inp[f"L1_gnn_b{j + 1}"]
        a[f"enc_b{j}"] = np.ascontiguousarray(b.reshape(-1, P).T) if j < 3 else np.ascontiguousarray(b)
    a["wg_t"] = np.ascontiguousarray(inp["L1_ffn_wg"].T)
    for j in (1, 2, 3):
        a[f"w{j}_1"] = np.ascontiguousarray(inp[f"L1_ffn_w{j}"]).reshape(E1 * D, D)
        a[f"sw{j}"] = np.ascontiguousarray(inp[f"L1_ffn_sw{j}"])
    a["c_before"] = np.triu(np.ones((P, P), np.float32), 1)
    a["c_ones"] = np.ones((P, P), np.float32)
    a["c_first_slot"] = np.tile(np.arange(E1, dtype=np.float32) * CAP, (P, 1))
    a["c_tokens"] = (np.arange(NT) * P + np.arange(P)[:, None]).astype(np.float32)
    a["c_no_token"] = np.full((SLOTS, 1), N, np.float32)
    return a


def kernel(**inputs):
    import numpy as _np
    import concourse.bacc as _bacc
    from concourse import mybir as _mybir
    from concourse.bass_utils import run_bass_kernel_spmd as _run

    nc = _bacc.Bacc("TRN2", target_bir_lowering=False, num_devices=1)
    arrays = {f"in_{k}": v for k, v in layouts(_np, {k: _np.asarray(v) for k, v in inputs.items()}).items()}
    dram = {k[3:]: nc.dram_tensor(k, v.shape, _mybir.dt.from_np(v.dtype), kind="ExternalInput").ap() for k, v in arrays.items()}
    out = nc.dram_tensor("out_dram", (N, D), _mybir.dt.float32, kind="ExternalOutput").ap()
    build(nc, dram, out)
    return _run(nc, [arrays], core_ids=[0]).results[0]["out_dram"]
```
